# Optimizing a Trainium2 kernel written in Bass

```python
import numpy as np
import jax
import jax.numpy as jnp

def _softmax(x, axis=-1):
    return jax.nn.softmax(x, axis=axis)

def _gelu(x):
    return jax.nn.gelu(x, approximate=True)

def _silu(x):
    return jax.nn.silu(x)

def _sigmoid(x):
    return jax.nn.sigmoid(x)

def _layernorm(x, axis=-1, eps=1e-05):
    m = jnp.mean(x, axis=axis, keepdims=True)
    v = jnp.var(x, axis=axis, keepdims=True)
    return (x - m) / jnp.sqrt(v + eps)

def _scatter_add(tgt, idx, src, axis=0):
    return tgt.at[idx].add(src)

def _segment_sum(src, seg, n):
    return jax.ops.segment_sum(src, seg, n)
kernel_name = 'mk_recurrent_d2_jaxref_r4_5c9c62'

def setup_inputs(seed: int=0):
    np.random.seed(seed)
    _w = jnp.asarray

    def _L0_attn_setup():
        import jax, jax.numpy as jnp
        import numpy as np
        B, T, D_MODEL, D_STATE = (8, 512, 256, 64)
        key = jax.random.key(seed)
        ks = jax.random.split(key, 11)

        def lecun(k, shape):
            fan_in = shape[0]
            return jax.random.normal(k, shape, jnp.float32) / jnp.sqrt(jnp.float32(fan_in))
        return {'x': jax.random.normal(ks[0], (B, T, D_MODEL), jnp.float32), 'W_in': lecun(ks[1], (D_MODEL, D_STATE)), 'b_in': jnp.zeros((D_STATE,), jnp.float32), 'W_gate': lecun(ks[2], (D_MODEL, D_MODEL)), 'b_gate': jnp.zeros((D_MODEL,), jnp.float32), 'A': lecun(ks[3], (D_STATE, D_STATE)), 'Bm': lecun(ks[4], (D_STATE, D_STATE)), 'C': lecun(ks[5], (D_MODEL, D_STATE)), 'D': lecun(ks[6], (D_MODEL, D_STATE)), 'W_out': lecun(ks[7], (D_MODEL, D_MODEL)), 'b_out': jnp.zeros((D_MODEL,), jnp.float32)}
    _L0_attn_in = _L0_attn_setup()

    def _L0_ffn_setup():
        import jax, jax.numpy as jnp
        import numpy as np
        from jax import lax
        T, B, I, M, O = (64, 64, 256, 256, 256)

        def _xavier(key, shape):
            fan_out, fan_in = shape
            limit = float(np.sqrt(6.0 / (fan_in + fan_out)))
            return jax.random.uniform(key, shape, jnp.float32, -limit, limit)
        key = jax.random.key(seed)
        ks = jax.random.split(key, 9)
        x = jax.random.normal(ks[0], (T, B, I), jnp.float32)
        return {'x': x, 'wf': _xavier(ks[1], (M, I)), 'uf': _xavier(ks[2], (M, M)), 'bf': jnp.zeros((M,), jnp.float32), 'wi': _xavier(ks[3], (M, I)), 'ui': _xavier(ks[4], (M, M)), 'bi': jnp.zeros((M,), jnp.float32), 'wc': _xavier(ks[5], (M, I)), 'uc': _xavier(ks[6], (M, M)), 'bc': jnp.zeros((M,), jnp.float32), 'wo': _xavier(ks[7], (O, I)), 'uo': _xavier(ks[8], (O, M)), 'bo': jnp.zeros((O,), jnp.float32), 'in_c': jnp.zeros((M,), jnp.float32)}
    _L0_ffn_in = _L0_ffn_setup()

    def _L1_attn_setup():
        import jax, jax.numpy as jnp
        import numpy as np
        B, T, C = (4, 512, 256)
        NUM_HEADS = 16
        OUT_DIM = 256
        HEAD_DIM = OUT_DIM // NUM_HEADS
        key = jax.random.key(seed)
        kx, kk, kq, kv, kp = jax.random.split(key, 5)
        return {'x': jax.random.normal(kx, (B, T, C), dtype=jnp.float32), 'W_key': jax.random.normal(kk, (OUT_DIM, C), dtype=jnp.float32), 'W_query': jax.random.normal(kq, (OUT_DIM, C), dtype=jnp.float32), 'W_value': jax.random.normal(kv, (OUT_DIM, C), dtype=jnp.float32), 'W_proj': jax.random.normal(kp, (OUT_DIM, OUT_DIM), dtype=jnp.float32)}
    _L1_attn_in = _L1_attn_setup()

    def _L1_ffn_setup():
        import jax, jax.numpy as jnp
        import numpy as np
        IN_DIM, OUT_DIM, N_PROTO, RANK = (256, 256, 32, 16)
        key = jax.random.key(seed)
        ks = jax.random.split(key, 5)
        x = jax.random.normal(ks[0], (2, 1024, IN_DIM), dtype=jnp.float32)
        prototypes = jax.random.normal(ks[1], (N_PROTO, IN_DIM), dtype=jnp.float32) * 0.02
        B = jax.random.normal(ks[2], (N_PROTO, RANK, IN_DIM), dtype=jnp.float32) * 0.02
        A = jax.random.normal(ks[3], (N_PROTO, OUT_DIM, RANK), dtype=jnp.float32) * 0.02
        bias = jnp.zeros((N_PROTO, OUT_DIM), dtype=jnp.float32)
        temp = jnp.asarray(1.0, dtype=jnp.float32)
        return {'x': x, 'prototypes': prototypes, 'B': B, 'A': A, 'bias': bias, 'temp': temp}
    _L1_ffn_in = _L1_ffn_setup()
    _d = {'L0_attn_x': _L0_attn_in['x'], 'L0_attn_W_in': _L0_attn_in['W_in'], 'L0_attn_b_in': _L0_attn_in['b_in'], 'L0_attn_W_gate': _L0_attn_in['W_gate'], 'L0_attn_b_gate': _L0_attn_in['b_gate'], 'L0_attn_A': _L0_attn_in['A'], 'L0_attn_Bm': _L0_attn_in['Bm'], 'L0_attn_C': _L0_attn_in['C'], 'L0_attn_D': _L0_attn_in['D'], 'L0_attn_W_out': _L0_attn_in['W_out'], 'L0_attn_b_out': _L0_attn_in['b_out'], 'L0_ffn_wf': _L0_ffn_in['wf'], 'L0_ffn_uf': _L0_ffn_in['uf'], 'L0_ffn_bf': _L0_ffn_in['bf'], 'L0_ffn_wi': _L0_ffn_in['wi'], 'L0_ffn_ui': _L0_ffn_in['ui'], 'L0_ffn_bi': _L0_ffn_in['bi'], 'L0_ffn_wc': _L0_ffn_in['wc'], 'L0_ffn_uc': _L0_ffn_in['uc'], 'L0_ffn_bc': _L0_ffn_in['bc'], 'L0_ffn_wo': _L0_ffn_in['wo'], 'L0_ffn_uo': _L0_ffn_in['uo'], 'L0_ffn_bo': _L0_ffn_in['bo'], 'L0_ffn_in_c': _L0_ffn_in['in_c'], 'L1_attn_W_key': _L1_attn_in['W_key'], 'L1_attn_W_query': _L1_attn_in['W_query'], 'L1_attn_W_value': _L1_attn_in['W_value'], 'L1_attn_W_proj': _L1_attn_in['W_proj'], 'L1_ffn_prototypes': _L1_ffn_in['prototypes'], 'L1_ffn_B': _L1_ffn_in['B'], 'L1_ffn_A': _L1_ffn_in['A'], 'L1_ffn_bias': _L1_ffn_in['bias'], 'L1_ffn_temp': _L1_ffn_in['temp']}
    _x0 = _d['L0_attn_x']
    _d['L0_attn_x'] = jax.random.normal(jax.random.fold_in(jax.random.key(seed), 1), (8, 512, 256), dtype=_x0.dtype)
    del _x0
    return _d

def reference(L0_attn_x, L0_attn_W_in, L0_attn_b_in, L0_attn_W_gate, L0_attn_b_gate, L0_attn_A, L0_attn_Bm, L0_attn_C, L0_attn_D, L0_attn_W_out, L0_attn_b_out, L0_ffn_wf, L0_ffn_uf, L0_ffn_bf, L0_ffn_wi, L0_ffn_ui, L0_ffn_bi, L0_ffn_wc, L0_ffn_uc, L0_ffn_bc, L0_ffn_wo, L0_ffn_uo, L0_ffn_bo, L0_ffn_in_c, L1_attn_W_key, L1_attn_W_query, L1_attn_W_value, L1_attn_W_proj, L1_ffn_prototypes, L1_ffn_B, L1_ffn_A, L1_ffn_bias, L1_ffn_temp):

    def _L0_attn_ref(x, W_in, b_in, W_gate, b_gate, A, Bm, C, D, W_out, b_out):
        import jax, jax.numpy as jnp
        import numpy as np
        B, T, D_MODEL, D_STATE = (8, 512, 256, 64)
        b, t, d_model = x.shape
        d_state = A.shape[0]
        u = x @ W_in + b_in
        g = jax.nn.sigmoid(x @ W_gate + b_gate)
        u_seq = jnp.swapaxes(u, 0, 1)
        g_seq = jnp.swapaxes(g, 0, 1)
        x_seq = jnp.swapaxes(x, 0, 1)

        def step(h_prev, inputs):
            u_t, g_t, x_t = inputs
            h_t = jnp.tanh(h_prev @ A + u_t @ Bm)
            y_t = h_t @ C.T + u_t @ D.T
            y_t = g_t * y_t + (1.0 - g_t) * x_t
            return (h_t, y_t)
        h0 = jnp.zeros((b, d_state), x.dtype)
        _, ys = jax.lax.scan(step, h0, xs=(u_seq, g_seq, x_seq))
        ys = jnp.swapaxes(ys, 0, 1)
        return ys @ W_out + b_out + x

    def _L0_ffn_ref(x, wf, uf, bf, wi, ui, bi, wc, uc, bc, wo, uo, bo, in_c):
        import jax, jax.numpy as jnp
        import numpy as np
        from jax import lax
        T, B, I, M, O = (64, 64, 256, 256, 256)

        def _xavier(key, shape):
            fan_out, fan_in = shape
            limit = float(np.sqrt(6.0 / (fan_in + fan_out)))
            return jax.random.uniform(key, shape, jnp.float32, -limit, limit)
        batch = x.shape[1]
        c0 = jnp.broadcast_to(in_c, (batch, in_c.shape[0]))

        def step(c, xt):
            ft = jax.nn.sigmoid(xt @ wf.T + c @ uf.T + bf)
            it = jax.nn.sigmoid(xt @ wi.T + c @ ui.T + bi)
            gt = jnp.tanh(xt @ wc.T + c @ uc.T + bc)
            c = ft * c + it * gt
            return (c, None)
        c_final, _ = lax.scan(step, c0, x)
        h = jnp.tanh(jnp.einsum('tbi,oi->tbo', x, wo) + c_final @ uo.T + bo)
        return h

    def _L1_attn_ref(x, W_key, W_query, W_value, W_proj):
        import jax, jax.numpy as jnp
        import numpy as np
        B, T, C = (4, 512, 256)
        NUM_HEADS = 16
        OUT_DIM = 256
        HEAD_DIM = OUT_DIM // NUM_HEADS
        b, t, c = x.shape
        h, hd = (NUM_HEADS, HEAD_DIM)
        inv_sqrt_c = c ** (-0.5)

        def proj(W):
            return jnp.einsum('btc,oc->bto', x, W).reshape(b, t, h, hd).transpose(0, 2, 1, 3) * inv_sqrt_c
        k = proj(W_key)
        q = proj(W_query)
        v = proj(W_value)
        scores = jnp.einsum('bhqd,bhkd->bhqk', q, k) * hd ** (-0.5)
        causal = jnp.tril(jnp.ones((t, t), dtype=bool))
        scores = jnp.where(causal, scores, -jnp.inf)
        weight = jax.nn.softmax(scores, axis=-1)
        out = jnp.einsum('bhqk,bhkd->bhqd', weight, v)
        out = out.transpose(0, 2, 1, 3).reshape(b, t, h * hd)
        out = jnp.einsum('bto,po->btp', out, W_proj) * W_proj.shape[-1] ** (-0.5)
        return out

    def _L1_ffn_ref(x, prototypes, B, A, bias, temp):
        import jax, jax.numpy as jnp
        import numpy as np
        IN_DIM, OUT_DIM, N_PROTO, RANK = (256, 256, 32, 16)
        lead = x.shape[:-1]
        xf = x.reshape(-1, IN_DIM)
        x2 = jnp.sum(xf * xf, axis=1, keepdims=True)
        p2 = jnp.sum(prototypes * prototypes, axis=1)
        d2 = x2 + p2[None, :] - 2.0 * (xf @ prototypes.T)
        dists = jnp.sqrt(jnp.maximum(d2, 0.0))
        t = jnp.maximum(jnp.abs(temp), 0.1)
        w = jax.nn.softmax(-dists / t, axis=1)
        topw, topi = jax.lax.top_k(w, 2)
        topw = topw / jnp.sum(topw, axis=1, keepdims=True)
        out = jnp.zeros((xf.shape[0], OUT_DIM), dtype=xf.dtype)
        for tslot in range(2):
            idx = topi[:, tslot]
            wt = topw[:, tslot:tslot + 1]
            h = jnp.einsum('nri,ni->nr', B[idx], xf)
            y = jnp.einsum('nor,nr->no', A[idx], h) + bias[idx]
            out = out + wt * y
        return out.reshape(*lead, OUT_DIM)
    x = L0_attn_x
    xn = _layernorm(x, axis=-1)
    s = _L0_attn_ref(xn, L0_attn_W_in, L0_attn_b_in, L0_attn_W_gate, L0_attn_b_gate, L0_attn_A, L0_attn_Bm, L0_attn_C, L0_attn_D, L0_attn_W_out, L0_attn_b_out)
    g = _silu(_L0_ffn_ref(xn, L0_ffn_wf, L0_ffn_uf, L0_ffn_bf, L0_ffn_wi, L0_ffn_ui, L0_ffn_bi, L0_ffn_wc, L0_ffn_uc, L0_ffn_bc, L0_ffn_wo, L0_ffn_uo, L0_ffn_bo, L0_ffn_in_c))
    x = x + s * g
    xn = _layernorm(x, axis=-1)
    s = _L1_attn_ref(xn, L1_attn_W_key, L1_attn_W_query, L1_attn_W_value, L1_attn_W_proj)
    g = _silu(_L1_ffn_ref(xn, L1_ffn_prototypes, L1_ffn_B, L1_ffn_A, L1_ffn_bias, L1_ffn_temp))
    x = x + s * g
    return x

_drawn_inputs = setup_inputs


def setup_inputs(seed=0):
    import zlib

    import numpy as np

    out = dict(_drawn_inputs(seed))
    spreads = {'L0_attn_b_in': (0.0, 0.8),
     'L0_attn_b_gate': (0.0, 0.8),
     'L0_attn_b_out': (0.0, 0.282),
     'L0_ffn_bf': (0.0, 0.8),
     'L0_ffn_bi': (0.0, 0.8),
     'L0_ffn_bc': (0.0, 0.29),
     'L0_ffn_bo': (0.0, 0.1),
     'L0_ffn_in_c': (0.0, 0.8),
     'L1_ffn_bias': (0.0, 0.8)}
    factors = {'L1_attn_W_key': 8.0,
     'L1_attn_W_query': 8.0,
     'L1_attn_W_value': 7.296,
     'L1_attn_W_proj': 7.285,
     'L1_ffn_prototypes': 7.607,
     'L1_ffn_B': 8.0,
     'L1_ffn_A': 8.0}
    for name, (base, spread) in spreads.items():
        noise = np.random.default_rng([zlib.crc32(name.encode()), seed]).standard_normal(out[name].shape)
        drawn = base * np.exp(spread * noise) if base else spread * noise
        out[name] = jnp.asarray(drawn.astype(out[name].dtype))
    for name, factor in factors.items():
        out[name] = (out[name] * factor).astype(out[name].dtype)
    return out
```

```python
from contextlib import ExitStack

import concourse.bass as bass
from concourse import mybir

F32 = mybir.dt.float32
BF16 = mybir.dt.bfloat16
U32 = mybir.dt.uint32
ALU = mybir.AluOpType
ACT = mybir.ActivationFunctionType
AX = mybir.AxisListType

B, T, D = 8, 512, 256
ST = 64
P = 128
KT = D // P
NT = T // P
H, HD = 16, 16
NP, RANK = 32, 16
NR = NP * RANK
HALF = T // 2
STEPS = T // B // 2
EPS = 1e-5
SPLIT = 3
PAIRS = [(0, 0), (0, 1), (1, 0), (0, 2), (2, 0), (1, 1)]
KS = len(PAIRS) * HD
KM = KS + 2
SCORE_SCALE = float(D) ** -1.0 * float(HD) ** -0.5
OUT_SCALE = float(D) ** -0.5
P_AT = {0: 0, 1: 512, 3: 896, 2: 1024}
PW = NT * (NT + 1) // 2 * P
BIG = 1.0e30


class Count:

    def __init__(self, handle, per, step=1, credit=1):
        self.sem, self.per, self.step, self.credit = handle, per, step, credit

    def at(self, it, n):
        return it * (self.per * self.step) + (n * self.step + self.credit)


def two_layers(nc, a, out):
    ctx = ExitStack()
    with ctx:
        def sb(name, shape, dt=F32):
            return ctx.enter_context(nc.sbuf_tensor(name, shape, dt))

        def sem(name):
            return ctx.enter_context(nc.semaphore(name))

        def count(name, per, credit=1):
            return Count(sem(name), per, credit=credit)

        def dcount(name, per):
            return Count(sem(name), per, step=16, credit=16)

        xt_d = nc.dram_tensor("xt_d", (B, P, KT, T), F32, kind="Internal").ap()
        xn_d = nc.dram_tensor("xn_d", (B, P, NT, D), F32, kind="Internal").ap()
        gt_d = nc.dram_tensor("gt_d", (B, P, KT, T), F32, kind="Internal").ap()
        wx_d = nc.dram_tensor("wx_d", (B, P, NT, D), F32, kind="Internal").ap()
        qk_d = nc.dram_tensor("qk_d", (SPLIT, 2, D, T), BF16, kind="Internal").ap()

        HU = sb("HU", [P, T * B])
        w_cd = sb("w_cd", [P, D])
        w_out = sb("w_out", [P, KT, D])
        w_qk = sb("w_qk", [P, 2, KT, D])
        w_v = sb("w_v", [P, KT, D])
        w_pr = sb("w_pr", [P, KT, D])
        w_b = sb("w_b", [P, KT, NR])
        w_a = sb("w_a", [P, NR // P, D])
        w_pt = sb("w_pt", [P, KT, NP])
        w_bias = sb("w_bias", [NP, D])
        ident = sb("ident", [P, P])
        identb = sb("identb", [P, P], BF16)
        negmask = sb("negmask", [P, P], BF16)
        negmask_t = sb("negmask_t", [P, P], BF16)
        halves = sb("halves", [P, P])
        mhalf = sb("mhalf", [P, NT])
        eps = sb("eps", [P, NT])
        iota = sb("iota", [P, NP])
        ones = sb("ones", [P, P])
        p2 = sb("p2", [P, NP])
        ntemp = sb("ntemp", [P, 1])
        atemp = sb("atemp", [P, 1])
        bout = sb("bout", [P, D])
        bo = sb("bo", [P, D])
        UC = sb("UC", [P, NT, D])
        scratch = sb("scratch", [P, 1])
        Q6 = sb("Q6", [P, H, T], BF16)
        K6 = sb("K6", [P, H, T], BF16)
        XT = sb("XT", [P, KT, T])
        GT = sb("GT", [P, KT, T])
        WX = sb("WX", [P, NT, D])
        X1 = sb("X1", [P, NT, D])
        XNB = sb("XNB", [P, NT, D])
        YS = sb("YS", [P, KT, T])
        SG = sb("SG", [P, NT, D])
        S1 = sb("S1", [P, NT, D])
        XT1 = sb("XT1", [P, KT, T])
        QF = sb("QF", [P, 2 * KT, T])
        QB = sb("QB", [P, SPLIT, 2 * KT, T], BF16)
        OS = sb("OS", [P, T])
        SG2 = sb("SG2", [P, NT, D])
        bnst = sb("bnst", [P, NT, 6])
        mv = sb("mv", [P, NT, 2])
        rst = sb("rst", [P, NT])
        x2 = sb("x2", [P, NT])
        dst = sb("dst", [P, NT, NP])
        dmn = sb("dmn", [P, NT])
        ex = sb("ex", [P, NT, NP])
        top = sb("top", [P, NT, 8])
        topi = sb("topi", [P, NT, 8], U32)
        topf = sb("topf", [P, NT, 2])
        hit = sb("hit", [P, NT, NP])
        wm = sb("wm", [P, NT, NP])
        rden = sb("rden", [P, NT])
        wmt = sb("wmt", [NP, T])
        nm = sb("nm", [P, NT, H])
        nmh = sb("nmh", [H, T], BF16)
        nml = sb("nml", [H, T], BF16)
        rec = sb("rec", [P, NT, NT])
        ARENA = 2 * 4 * PW + NR // P * T + T + NT * H * 32
        arena = sb("arena", [P, ARENA])
        used = [0]

        def part(*shape):
            n = 1
            for s in shape:
                n *= s
            v = arena[:, used[0]:used[0] + n]
            used[0] += n
            assert used[0] <= ARENA
            if len(shape) == 1:
                return v
            names = "abcd"[:len(shape)]
            return v.rearrange(f"p ({' '.join(names)}) -> p {' '.join(names)}",
                               **{k: s for k, s in zip(names, shape)})

        w_in = part(KT, ST)
        w_ab = part(ST)
        w_gate = part(KT, D)
        w_x = part(3, KT, D)
        w_c = part(3, KT, D)
        w_wo = part(KT, D)
        w_uo = part(KT, D)
        b_in = part(1)
        b_z = part(4, KT)
        HB = part(2 * STEPS, B)
        XB = part(2, KT, HALF)
        CT = part(KT, T)
        c0 = part(KT)
        TG = part(3, KT, HALF)
        GS = part(KT, HALF)
        WS = part(2, D)
        CA = part(KT, HALF)
        xin, xnp, xtp = (X1, SG2), (SG, S1), (XT1, YS)
        ptsq = part(KT, NP)
        used[0] = 0
        PR = part(2, 4, PW)
        HMT = part(NR // P, T)
        HM = part(T)
        VA = part(NT, H, 32)
        AT = YS[:, :, :].rearrange("p a b -> p (a b)").rearrange("p (t o) -> p t o", t=NT)
        AO = QF[:, 0:KT, :]

        PS = ctx.enter_context(nc.psum_tensor("PS", [P, 8, 512], F32))

        ld_w = sem("ld_w")
        const = sem("const")
        init = sem("init")
        temps = sem("temps")
        act_init = sem("act_init")
        pe_init = sem("pe_init")
        a_x = [dcount(f"a_x{s}", 1) for s in range(2)]
        a_st = count("a_st", 2 * (NT + NT))
        a_rs = count("a_rs", 2 * 2)
        a_xn = count("a_xn", 2)
        a_tr = count("a_tr", 2 * KT)
        a_xt = count("a_xt", 2 * KT)
        a_u = count("a_u", 2)
        a_ue = count("a_ue", 2)
        a_sv = dcount("a_sv", 4)
        c_x = [dcount(f"c_x{n}", 1) for n in range(2)]
        c_u = [dcount(f"c_u{n}", 1) for n in range(2)]
        c_mm = count("c_mm", 2 * STEPS)
        c_h = count("c_h", 2 * STEPS)
        c_z = count("c_z", 2 * 5)
        c_t = count("c_t", 2 * 8, 7)
        c_w = count("c_w", 2)
        c_c = count("c_c", 2 * 4, 5)
        c_hs = dcount("c_hs", 3)
        c_gs = dcount("c_gs", 2)
        c_ws = dcount("c_ws", 2)
        f_z = sem("f_z")
        f_e = sem("f_e")
        f_pe = sem("f_pe")
        f_act = sem("f_act")
        f_set = sem("f_set")
        l_xt, l_gt, l_wx, l_x, l_xn = (dcount(n, 1) for n in ("l_xt", "l_gt", "l_wx", "l_x", "l_xn"))
        y_mm = count("y_mm", KT)
        y_v = count("y_v", 3 * KT)
        p_xn = count("p_xn", 1)
        p_hq = count("p_hq", 1)
        g_t = count("g_t", 2)
        p_sg = count("p_sg", 2)
        s_mm = count("s_mm", 2)
        s_v = count("s_v", 3 * 2)
        n_st = count("n_st", 2 * NT)
        n_rs = count("n_rs", 2)
        n_xn = count("n_xn", NT)
        n_x2 = count("n_x2", NT)
        n_tr = count("n_tr", KT)
        n_xt = count("n_xt", KT)
        q_mm = count("q_mm", 4)
        q_e = count("q_e", 4)
        q_s = count("q_s", 3)
        q_r = count("q_r", 2)
        q_st = dcount("q_st", 1)
        q_ld = dcount("q_ld", 2 * len(PAIRS))
        v_mm = count("v_mm", 2)
        v_e = count("v_e", 2)
        d_mm = count("d_mm", 1)
        d_v = count("d_v", 13)
        d_p = count("d_p", 1)
        d_e = count("d_e", 1)
        d_m = count("d_m", 2 * NT)
        m_mm = count("m_mm", NT * H // 2)
        m_r = count("m_r", NT * H // 2)
        m_t = count("m_t", 1)
        m_h = count("m_h", 2)
        m_ld = dcount("m_ld", 2)
        h_mm = count("h_mm", NT)
        h_v = count("h_v", NT)
        h_t = count("h_t", NT)
        h_e = count("h_e", NT)
        w_t = count("w_t", 1)
        w_e = count("w_e", 1)
        e_mm = count("e_mm", 2)
        e_t = count("e_t", 2)
        e_v = count("e_v", 2)
        t_mm = count("t_mm", H)
        t_e = count("t_e", H)
        o_mm = count("o_mm", 4)
        o_e = count("o_e", 4)
        o_t = count("o_t", 4)
        o_r = count("o_r", 4)
        o_v = count("o_v", 4)
        r_t = count("r_t", KT)
        r_e = count("r_e", KT)
        z_mm = count("z_mm", 2)
        z_v = count("z_v", 2 * 2)
        z_o = dcount("z_o", 1)

        x_v = a["L0_attn_x"].rearrange("b (j p) d -> b p j d", p=P)
        o_view = out.rearrange("b (j p) d -> b p j d", p=P)

        def rows(w):
            return w.rearrange("(k p) n -> p k n", p=P)

        loads = [
            (w_in, rows(a["W_in"])), (w_ab[0:ST, :], a["A"]), (w_ab[ST:P, :], a["Bm"]),
            (w_gate, rows(a["W_gate"])), (w_cd[0:ST, :], a["CT"]), (w_cd[ST:P, :], a["DT"]),
            (w_out[:, :, :], rows(a["W_out"])),
            (w_x[:, 0], rows(a["wfT"])), (w_x[:, 1], rows(a["wiT"])), (w_x[:, 2], rows(a["wcT"])),
            (w_c[:, 0], rows(a["ufT"])), (w_c[:, 1], rows(a["uiT"])), (w_c[:, 2], rows(a["ucT"])),
            (w_wo, rows(a["woT"])), (w_uo, rows(a["uoT"])),
            (b_in[ST:P, :], a["b_in"].rearrange("(p o) -> p o", o=1)),
            (b_z[:, 0], a["bf"]), (b_z[:, 1], a["bi"]), (b_z[:, 2], a["bc"]),
            (b_z[:, 3], a["b_gate"]), (c0, a["in_c"]),
            (w_qk[:, 0], rows(a["WqT"])), (w_qk[:, 1], rows(a["WkT"])), (w_v[:, :, :], rows(a["WvT"])),
            (w_pr[:, :, :], rows(a["WpT"])), (w_b[:, :, :], rows(a["BT"])), (w_a[:, :, :], rows(a["AT"])),
            (w_pt[:, :, :], rows(a["protoT"])), (w_bias[:, :], a["bias"]),
            (bout[:, :], a["b_out"].partition_broadcast(P)), (bo[:, :], a["bo"].partition_broadcast(P)),
            (ntemp[:, :], a["temp"].partition_broadcast(P)),
        ]
        LOADED = 16 * len(loads)

        block = ctx.enter_context(nc.Block())

        @block.sync
        def _(sp):
            for s in (*a_x, a_sv, *c_x, *c_u, c_hs, c_gs, c_ws, l_xt, l_gt, l_wx, l_x, l_xn, q_st, q_ld, m_ld, z_o):
                sp.sem_inc(s.sem, s.credit)
            for dst, src in loads:
                sp.dma_start(dst, src).then_inc(ld_w, 16)

            def prepass(g):
                for s in range(2):
                    sp.wait_ge(a_xn.sem, a_xn.at(g, 0))
                    sp.dma_start(xin[s][:, :, :], x_v[bass.ds(g * 2 + s, 1)].rearrange("o p j d -> p (o j) d")
                                 ).then_inc(a_x[s].sem, 16)
                for s in range(2):
                    sp.wait_ge(a_xn.sem, a_xn.at(g, s + 1))
                    sp.dma_start(xn_d[bass.ds(g * 2 + s, 1)].rearrange("o p j d -> p (o j) d"), xnp[s][:, :, :]
                                 ).then_inc(a_sv.sem, 16)
                    sp.wait_ge(a_xt.sem, a_xt.at(g, KT * (s + 1)))
                    sp.dma_start(xt_d[bass.ds(g * 2 + s, 1)].rearrange("o p k t -> p (o k) t"), xtp[s][:, :, :]
                                 ).then_inc(a_sv.sem, 16)

            with sp.Fori(0, B // 2) as g:
                prepass(g)
            sp.wait_ge(a_sv.sem, 16 * (2 * B + 1))
            sp.wait_ge(a_ue.sem, B + 1)

            def load_half(b, n):
                sp.dma_start(XB[:, n], xt_d[bass.ds(b, 1), :, :, n * HALF:(n + 1) * HALF]
                             .rearrange("o p k t -> p (o k) t")).then_inc(c_x[n].sem, 16)
                sp.dma_start(HB[ST:P, n * STEPS:(n + 1) * STEPS],
                             HU[ST:P, bass.ds(b * (2 * STEPS * B) + n * STEPS * B, STEPS * B)]
                             .rearrange("p (s b) -> p s b", b=B)).then_inc(c_u[n].sem, 16)

            def save_half(b, n):
                col = b * (2 * STEPS * B)
                sp.wait_ge(c_h.sem, c_h.at(b, (n + 1) * STEPS))
                if n == 0:
                    sp.dma_start(HU[0:ST, bass.ds(col, STEPS * B)], HB[0:ST, 1:STEPS + 1]
                                 .rearrange("p s b -> p (s b)")).then_inc(c_hs.sem, 16)
                else:
                    sp.dma_start(HU[0:ST, bass.ds(col + STEPS * B, (STEPS - 1) * B)],
                                 HB[0:ST, STEPS + 1:2 * STEPS].rearrange("p s b -> p (s b)")
                                 ).then_inc(c_hs.sem, 16)
                    sp.dma_start(HU[0:ST, bass.ds(col + (2 * STEPS - 1) * B, B)], HB[0:ST, 0]
                                 ).then_inc(c_hs.sem, 16)
                sp.wait_ge(c_t.sem, c_t.at(b, 8 * (n + 1)))
                sp.dma_start(gt_d[bass.ds(b, 1), :, :, n * HALF:(n + 1) * HALF]
                             .rearrange("o p k t -> p (o k) t"), GS).then_inc(c_gs.sem, 16)
                sp.wait_ge(c_w.sem, c_w.at(b, n + 1))
                sp.dma_start(wx_d[bass.ds(b, 1), :, 2 * n:2 * n + 2]
                             .rearrange("o p j d -> p (o j) d"), WS).then_inc(c_ws.sem, 16)

            load_half(0, 0)
            load_half(0, 1)

            with sp.Fori(0, B - 1) as b:
                save_half(b, 0)
                sp.wait_ge(c_z.sem, c_z.at(b, 5))
                load_half(b + 1, 0)
                save_half(b, 1)
                sp.wait_ge(c_z.sem, c_z.at(b, 10))
                load_half(b + 1, 1)
            save_half(B - 1, 0)
            save_half(B - 1, 1)
            sp.wait_ge(c_hs.sem, 16 * (3 * B + 1))
            sp.wait_ge(c_gs.sem, 16 * (2 * B + 1))
            sp.wait_ge(c_ws.sem, 16 * (2 * B + 1))

            def load_batch(b):
                one = bass.ds(b, 1)
                sp.dma_start(XT[:, :, :], xt_d[one].rearrange("o p k t -> p (o k) t")).then_inc(l_xt.sem, 16)
                sp.dma_start(GT[:, :, :], gt_d[one].rearrange("o p k t -> p (o k) t")).then_inc(l_gt.sem, 16)
                sp.dma_start(WX[:, :, :], wx_d[one].rearrange("o p j d -> p (o j) d")).then_inc(l_wx.sem, 16)
                sp.dma_start(XNB[:, :, :], xn_d[one].rearrange("o p j d -> p (o j) d")).then_inc(l_xn.sem, 16)

            def load_x(b):
                sp.dma_start(X1[:, :, :], x_v[bass.ds(b, 1)].rearrange("o p j d -> p (o j) d")
                             ).then_inc(l_x.sem, 16)

            def batch(b):
                sp.wait_ge(q_s.sem, q_s.at(b, 3))
                sp.wait_ge(q_ld.sem, q_ld.at(b, 0))
                sp.wait_ge(t_mm.sem, t_mm.at(b, 0))
                sp.dma_start(qk_d.rearrange("s c (m p) t -> p s (c m) t", p=P), QB[:, :, :, :]
                             ).then_inc(q_st.sem, 16)
                sp.wait_ge(q_st.sem, q_st.at(b, 1))
                for r, pair in enumerate(PAIRS):
                    for c, dst in enumerate((Q6, K6)):
                        sp.dma_start(dst[r * HD:(r + 1) * HD, :, :],
                                     qk_d[pair[c], c].rearrange("(h d) t -> d h t", d=HD)
                                     ).then_inc(q_ld.sem, 16)
                sp.wait_ge(m_h.sem, m_h.at(b, 2))
                sp.dma_start(Q6[KS:KS + 1, :, :], nmh[:, :]).then_inc(m_ld.sem, 16)
                sp.dma_start(Q6[KS + 1:KS + 2, :, :], nml[:, :]).then_inc(m_ld.sem, 16)

            def store(b):
                sp.wait_ge(z_v.sem, z_v.at(b, 4))
                sp.dma_start(o_view[bass.ds(b, 1)].rearrange("o p j d -> p (o j) d"), SG2[:, :, :]
                             ).then_inc(z_o.sem, 16)

            load_batch(0)
            load_x(0)
            with sp.Fori(0, B - 1) as b:
                batch(b)
                sp.wait_ge(s_v.sem, s_v.at(b, 6))
                sp.wait_ge(y_v.sem, y_v.at(b, 3 * KT))
                sp.wait_ge(p_sg.sem, p_sg.at(b, 2))
                load_batch(b + 1)
                store(b)
                load_x(b + 1)
            batch(B - 1)
            store(B - 1)
            sp.wait_ge(z_o.sem, 16 * (B + 1))

        @block.gpsimd
        def _(pool):
            g_ = nc.gpsimd
            for s in (a_rs, p_xn, p_hq, p_sg, n_rs, q_r, d_p):
                pool.sem_inc(s.sem, s.credit)
            g_.memset(ident[:, :], 0.0).then_inc(const, 1)
            g_.memset(negmask[:, :], 0.0).then_inc(const, 1)
            g_.memset(negmask_t[:, :], 0.0).then_inc(const, 1)
            g_.memset(eps[:, :], EPS).then_inc(const, 1)
            g_.memset(halves[:, :], 0.5).then_inc(const, 1)
            g_.memset(mhalf[:, :], -0.5).then_inc(const, 1)
            g_.memset(ones[:, :], 1.0).then_inc(const, 1)
            g_.iota(iota[:, :], pattern=[[1, NP]], base=0, channel_multiplier=0,
                    allow_small_or_imprecise_dtypes=True).then_inc(const, 1)
            pool.wait_ge(const, 8)
            g_.affine_select(out=ident[:, :], in_=ident[:, :], compare_op=ALU.not_equal, fill=1.0, base=0,
                             pattern=[[-1, P]], channel_multiplier=1).then_inc(const, 1)
            g_.affine_select(out=negmask[:, :], in_=negmask[:, :], compare_op=ALU.is_ge, fill=-BIG, base=0,
                             pattern=[[-1, P]], channel_multiplier=1).then_inc(const, 1)
            g_.affine_select(out=negmask_t[:, :], in_=negmask_t[:, :], compare_op=ALU.is_ge, fill=-BIG, base=0,
                             pattern=[[1, P]], channel_multiplier=-1).then_inc(const, 1)
            pool.wait_ge(const, 11)
            g_.tensor_copy(identb[:, :], ident[:, :]).then_inc(const, 1)

            with pool.Fori(0, B // 2) as g:
                for s in range(2):
                    pool.wait_ge(a_st.sem, a_st.at(g, 2 * NT * (s + 1)))
                    g_.tensor_tensor(rst[:, :], mv[:, :, 1], eps[:, :], ALU.add).then_inc(a_rs.sem, 1)
                    pool.wait_ge(a_rs.sem, a_rs.at(g, 2 * s + 1))
                    g_.tensor_tensor(rst[:, :], rst[:, :], mhalf[:, :], ALU.pow).then_inc(a_rs.sem, 1)

            pool.wait_ge(f_pe, 1)
            pool.wait_ge(f_act, 1)
            pool.wait_ge(c_hs.sem, 16 * (3 * B + 1))
            pool.wait_ge(c_gs.sem, 16 * (2 * B + 1))
            pool.wait_ge(c_ws.sem, 16 * (2 * B + 1))
            g_.memset(VA[:, :, :, :], 0.0).then_inc(f_set, 1)
            pool.wait_ge(f_set, 1)
            g_.memset(VA[:, :, :, HD:HD + 1], 1.0).then_inc(f_set, 1)

            def batch(b):
                pool.wait_ge(l_xn.sem, l_xn.at(b, 1))
                g_.tensor_tensor(XNB[:, :, :], XNB[:, :, :],
                                 bout[:, :].unsqueeze(1).to_broadcast([P, NT, D]), ALU.add
                                 ).then_inc(p_xn.sem, 1)
                pool.wait_ge(l_wx.sem, l_wx.at(b, 1))
                g_.tensor_tensor(WX[:, :, :], WX[:, :, :], UC[:, :, :], ALU.add).then_inc(p_hq.sem, 1)
                pool.wait_ge(g_t.sem, g_t.at(b, 2))
                g_.tensor_tensor(SG[:, :, :], SG[:, :, :], WX[:, :, :], ALU.mult).then_inc(p_sg.sem, 1)
                pool.wait_ge(p_sg.sem, p_sg.at(b, 1))
                g_.tensor_tensor(SG[:, :, :], SG[:, :, :], WX[:, :, :], ALU.add).then_inc(p_sg.sem, 1)
                pool.wait_ge(n_st.sem, n_st.at(b, 2 * NT))
                g_.tensor_tensor(rst[:, :], mv[:, :, 1], eps[:, :], ALU.add).then_inc(n_rs.sem, 1)
                pool.wait_ge(n_rs.sem, n_rs.at(b, 1))
                g_.tensor_tensor(rst[:, :], rst[:, :], mhalf[:, :], ALU.pow).then_inc(n_rs.sem, 1)
                for n in range(2):
                    pool.wait_ge(q_s.sem, q_s.at(b, n + 1))
                    g_.tensor_tensor(QF[:, :, :], QF[:, :, :], QB[:, n], ALU.subtract).then_inc(q_r.sem, 1)
                pool.wait_ge(d_v.sem, d_v.at(b, 3))
                g_.tensor_tensor(dst[:, :, :].rearrange("p a b -> p (a b)"),
                                 dst[:, :, :].rearrange("p a b -> p (a b)"), halves[:, :], ALU.pow
                                 ).then_inc(d_p.sem, 1)

            pool.wait_ge(f_e, 2)
            with pool.Fori(0, B) as b:
                batch(b)

        @block.tensor
        def _(pe):
            for s in (a_tr, a_u, c_mm, c_z, y_mm, s_mm, n_tr, q_mm, v_mm, d_mm, m_mm, m_t, h_mm, h_t, w_t,
                      e_mm, t_mm, o_mm, o_t, r_t, z_mm):
                pe.sem_inc(s.sem, s.credit)
            pe.wait_ge(ld_w, LOADED)
            pe.wait_ge(const, 12)

            pe.wait_ge(init, 1)
            for k in range(KT):
                mm = pe.matmul(PS[:, 7, 0:NP], ones[:, :], ptsq[:, k], start=(k == 0), stop=(k == KT - 1))
            mm.then_inc(pe_init, 1)

            with pe.Fori(0, B // 2) as g:
                for s in range(2):
                    pe.wait_ge(a_xn.sem, a_xn.at(g, s + 1))
                    for k in range(KT):
                        pe.wait_ge(a_xt.sem, a_xt.at(g, KT * s if s else 0))
                        for j in range(NT):
                            mm = pe.transpose(PS[:, k, j * P:(j + 1) * P], xnp[s][:, j, k * P:(k + 1) * P],
                                              ident[:, :])
                        mm.then_inc(a_tr.sem, 1)
                    pe.wait_ge(a_ue.sem, a_ue.at(g, s))
                    pe.wait_ge(a_xt.sem, a_xt.at(g, KT * (s + 1)))
                    for k in range(KT):
                        mm = pe.matmul(PS[ST:P, 2, :], w_in[:, k], xtp[s][:, k], start=(k == 0),
                                       stop=(k == KT - 1))
                    mm.then_inc(a_u.sem, 1)

            pe.wait_ge(init, 8)

            def half(b, n):
                work = []
                for z in range(3):
                    for m in range(KT):
                        o = PS[:, z, m * HALF:(m + 1) * HALF]
                        w = slice(m * P, (m + 1) * P)
                        for k in range(KT):
                            work.append((o, w_x[:, z, k, w], XB[:, n, k], k == 0, False, None, z, m))
                        for k in range(KT):
                            work.append((o, w_c[:, z, k, w], CT[:, k, n * HALF:(n + 1) * HALF], False,
                                         k == KT - 1, c_z if m == k == 1 else None, z, m))
                for m in range(KT):
                    for k in range(KT):
                        work.append((PS[:, 3, m * HALF:(m + 1) * HALF], w_gate[:, k, m * P:(m + 1) * P],
                                     XB[:, n, k], k == 0, k == 1, c_z if m == k == 1 else None, 3, m))
                for j in range(2):
                    for k in range(KT):
                        work.append((PS[:, 4, j * D:(j + 1) * D], XB[:, n, k, j * P:(j + 1) * P], w_wo[:, k],
                                     k == 0, k == 1, c_z if j == k == 1 else None, 4, j))
                assert len(work) == STEPS
                pe.wait_ge(c_u[n].sem, c_u[n].at(b, 1))
                pe.wait_ge(c_x[n].sem, c_x[n].at(b, 1))
                for s, (o, lhs, rhs, first, last, done, z, m) in enumerate(work):
                    step = n * STEPS + s
                    pe.wait_ge(c_h.sem, c_h.at(b, step))
                    pe.matmul(PS[0:ST, 7, 0:B], w_ab, HB[:, step], start=True, stop=True
                              ).then_inc(c_mm.sem, 1)
                    if m == 0 and first:
                        if z < 3:
                            pe.wait_ge(c_t.sem, c_t.at(b, 8 * n - 8 + 2 * z + 2))
                        elif z == 3:
                            pe.wait_ge(c_t.sem, c_t.at(b, 8 * n))
                        else:
                            pe.wait_ge(c_w.sem, c_w.at(b, n))
                    if z == 0 and m == 0 and not first and s == KT:
                        pe.wait_ge(c_c.sem, c_c.at(b, 4 * n - 4))
                    mm = pe.matmul(o, lhs, rhs, start=first, stop=last)
                    if done:
                        mm.then_inc(done.sem, 1)

            with pe.Fori(0, B) as b:
                half(b, 0)
                half(b, 1)

            pe.wait_ge(c_c.sem, 8 * B + c_c.credit)
            pe.wait_ge(c_t.sem, 16 * B + c_t.credit)
            for j in range(NT):
                for k in range(KT):
                    mm = pe.matmul(PS[:, j // 2, j % 2 * D:(j % 2 + 1) * D], CT[:, k, j * P:(j + 1) * P],
                                   w_uo[:, k], start=(k == 0), stop=(k == KT - 1))
            mm.then_inc(f_pe, 1)
            pe.wait_ge(f_e, 2)
            pe.wait_ge(c_hs.sem, 16 * (3 * B + 1))
            pe.wait_ge(f_set, 2)

            def tokens(bank, j):
                return PS[:, bank + j // 2, j % 2 * D:(j % 2 + 1) * D]

            def batch(b):
                pe.wait_ge(z_v.sem, z_v.at(b, 0))
                hu = HU[:, :].rearrange("p (t b) -> p b t", b=B)[:, bass.ds(b, 1)].rearrange("p o t -> p (o t)")
                for m in range(KT):
                    pe.matmul(PS[:, 6 + m, :], w_cd[:, m * P:(m + 1) * P], hu, start=True, stop=True
                              ).then_inc(y_mm.sem, 1)
                pe.wait_ge(t_e.sem, t_e.at(b, 0))
                pe.wait_ge(y_v.sem, y_v.at(b, 3 * KT))
                for j in range(NT):
                    for k in range(KT):
                        mm = pe.matmul(tokens(0, j), YS[:, k, j * P:(j + 1) * P], w_out[:, k],
                                       start=(k == 0), stop=(k == KT - 1))
                    if j % 2:
                        mm.then_inc(s_mm.sem, 1)
                pe.wait_ge(n_xn.sem, n_xn.at(b, NT))
                for k in range(KT):
                    for j in range(NT):
                        mm = pe.transpose(PS[:, 2 + k, j * P:(j + 1) * P], S1[:, j, k * P:(k + 1) * P],
                                          ident[:, :])
                    mm.then_inc(n_tr.sem, 1)
                pe.wait_ge(n_xt.sem, n_xt.at(b, KT))
                pe.wait_ge(s_v.sem, s_v.at(b, 6))
                for n in range(4):
                    for k in range(KT):
                        mm = pe.matmul(PS[:, (4 + n) % 6, :], w_qk[:, n // 2, k, n % 2 * P:(n % 2 + 1) * P],
                                       XT1[:, k], start=(k == 0), stop=(k == KT - 1))
                    mm.then_inc(q_mm.sem, 1)
                pe.wait_ge(y_v.sem, y_v.at(b, 3 * KT))
                for j in range(NT):
                    for k in range(KT):
                        mm = pe.matmul(PS[:, 7, j * NP:(j + 1) * NP], XT1[:, k, j * P:(j + 1) * P],
                                       w_pt[:, k], start=(k == 0), stop=(k == KT - 1))
                mm.then_inc(d_mm.sem, 1)
                for j in range(NT):
                    for k in range(KT):
                        mm = pe.matmul(tokens(2, j), XT1[:, k, j * P:(j + 1) * P], w_v[:, k],
                                       start=(k == 0), stop=(k == KT - 1))
                    if j % 2:
                        mm.then_inc(v_mm.sem, 1)

                def low_rank(j):
                    pe.wait_ge(h_v.sem, h_v.at(b, j))
                    for k in range(KT):
                        mm = pe.matmul(PS[:, 6, :], XT1[:, k, j * P:(j + 1) * P], w_b[:, k],
                                       start=(k == 0), stop=(k == KT - 1))
                    mm.then_inc(h_mm.sem, 1)

                def low_rank_turn(j):
                    pe.wait_ge(h_v.sem, h_v.at(b, j + 1))
                    pe.wait_ge(h_e.sem, h_e.at(b, j))
                    for n in range(NR // P):
                        mm = pe.transpose(PS[:, 7, n * P:(n + 1) * P], HM[:, n * P:(n + 1) * P], ident[:, :])
                    mm.then_inc(h_t.sem, 1)

                def weights_turn():
                    pe.wait_ge(h_v.sem, h_v.at(b, NT))
                    for j in range(NT):
                        mm = pe.transpose(PS[0:NP, 6, j * P:(j + 1) * P], wm[:, j], ident[:, :])
                    mm.then_inc(w_t.sem, 1)

                def experts(p):
                    if p == 0:
                        pe.wait_ge(h_e.sem, h_e.at(b, NT))
                    pe.wait_ge(w_e.sem, w_e.at(b, 1))
                    for j in (2 * p, 2 * p + 1):
                        o = PS[:, 7 - p, j % 2 * D:(j % 2 + 1) * D]
                        for n in range(NR // P):
                            pe.matmul(o, HMT[:, n, j * P:(j + 1) * P], w_a[:, n], start=(n == 0), stop=False)
                        mm = pe.matmul(o, wmt[:, j * P:(j + 1) * P], w_bias[:, :], start=False, stop=True)
                    mm.then_inc(e_mm.sem, 1)

                pe.wait_ge(q_ld.sem, q_ld.at(b, 2 * len(PAIRS)))
                pe.wait_ge(q_e.sem, q_e.at(b, 4))
                pe.wait_ge(v_e.sem, v_e.at(b, 2))
                pe.wait_ge(d_v.sem, d_v.at(b, 1))
                side = {1: lambda: low_rank(0), 5: lambda: low_rank_turn(0), 6: lambda: low_rank(1),
                        10: lambda: low_rank_turn(1), 11: lambda: low_rank(2), 15: lambda: low_rank_turn(2),
                        16: lambda: low_rank(3), 20: lambda: low_rank_turn(3), 21: weights_turn,
                        24: lambda: experts(0), 27: lambda: experts(1)}
                for u in range(NT * H // 2):
                    hp, i = u // NT, u % NT
                    if u >= 3:
                        pe.wait_ge(m_r.sem, m_r.at(b, u - 2))
                    for e in range(2):
                        h = 2 * hp + e
                        bank = 2 * (u % 3) + e
                        pe.matmul(PS[:, bank, 0:(i + 1) * P], Q6[0:KS, h, i * P:(i + 1) * P],
                                  K6[0:KS, h, 0:(i + 1) * P], start=True, stop=False)
                        mm = pe.matmul(PS[:, bank, i * P:(i + 1) * P], identb[:, :], negmask[:, :],
                                       start=False, stop=True)
                    mm.then_inc(m_mm.sem, 1)
                    if u in side:
                        side[u]()
                pe.wait_ge(m_r.sem, m_r.at(b, NT * H // 2))
                pe.wait_ge(e_v.sem, e_v.at(b, 2))
                for i in range(NT):
                    mm = pe.transpose(PS[0:H, 6, i * P:(i + 1) * P], nm[:, i], ident[:, :])
                mm.then_inc(m_t.sem, 1)
                pe.wait_ge(m_ld.sem, m_ld.at(b, 2))

                def turned_scores(h):
                    base = 3 * (h % 2)
                    if h >= 2:
                        pe.wait_ge(t_e.sem, t_e.at(b, h - 1))
                    for kt, bank, at in ((0, 0, 0), (1, 1, 0), (3, 1, 384), (2, 2, 0)):
                        w = T - kt * P
                        pe.matmul(PS[:, base + bank, at:at + w], K6[0:KM, h, kt * P:(kt + 1) * P],
                                  Q6[0:KM, h, kt * P:T], start=True, stop=False)
                        mm = pe.matmul(PS[:, base + bank, at:at + P], identb[:, :], negmask_t[:, :],
                                       start=False, stop=True)
                    mm.then_inc(t_mm.sem, 1)

                def values(g):
                    pe.wait_ge(t_e.sem, t_e.at(b, 4 * (g + 1)))
                    pe.wait_ge(m_h.sem, m_h.at(b, 2))
                    pe.wait_ge(o_e.sem, o_e.at(b, g))
                    for kt in range(NT):
                        for j in range(4):
                            w = T - kt * P
                            mm = pe.matmul(PS[32 * j:32 * j + 32, 6, kt * P:T], VA[:, kt, 4 * g + j],
                                           PR[:, g % 2, j, P_AT[kt]:P_AT[kt] + w],
                                           start=(kt == 0), stop=(kt == NT - 1))
                    mm.then_inc(o_mm.sem, 1)

                def values_turn(g):
                    pe.wait_ge(o_e.sem, o_e.at(b, g + 1))
                    pe.wait_ge(o_v.sem, o_v.at(b, g))
                    for j in range(NT):
                        mm = pe.transpose(PS[:, 7, j * P:(j + 1) * P], OS[:, j * P:(j + 1) * P], ident[:, :])
                    mm.then_inc(o_t.sem, 1)

                for h in range(H):
                    turned_scores(h)
                    if h % 4 == 1 and h > 4:
                        values(h // 4 - 1)
                    if h % 4 == 3 and h > 4:
                        values_turn(h // 4 - 1)
                values(3)
                values_turn(3)
                pe.wait_ge(o_v.sem, o_v.at(b, 4))
                pe.wait_ge(t_e.sem, t_e.at(b, H))
                for k in range(KT):
                    for j in range(NT):
                        mm = pe.transpose(PS[:, k, j * P:(j + 1) * P], AT[:, j, k * P:(k + 1) * P], ident[:, :])
                    mm.then_inc(r_t.sem, 1)
                pe.wait_ge(r_e.sem, r_e.at(b, KT))
                for j in range(NT):
                    for k in range(KT):
                        mm = pe.matmul(tokens(6, j), AO[:, k, j * P:(j + 1) * P], w_pr[:, k],
                                       start=(k == 0), stop=(k == KT - 1))
                    if j % 2:
                        mm.then_inc(z_mm.sem, 1)

            with pe.Fori(0, B) as b:
                batch(b)

        @block.scalar
        def _(act):
            s_ = nc.scalar
            for s in (a_xt, c_h, c_t, g_t, n_x2, n_xt, q_e, d_e, h_e, e_t, t_e, o_e, r_e):
                act.sem_inc(s.sem, s.credit)
            act.wait_ge(ld_w, LOADED)
            s_.mul(b_z[:, 0:2], b_z[:, 0:2], 0.5).then_inc(act_init, 1)
            s_.mul(b_z[:, 3], b_z[:, 3], 0.5).then_inc(act_init, 1)
            act.wait_ge(act_init, 2)

            with act.Fori(0, B // 2) as g:
                for s in range(2):
                    act.wait_ge(a_ue.sem, a_ue.at(g, 0))
                    act.wait_ge(a_sv.sem, a_sv.at(g, 0))
                    for k in range(KT):
                        act.wait_ge(a_tr.sem, a_tr.at(g, KT * s + k + 1))
                        s_.copy(xtp[s][:, k], PS[:, k, :]).then_inc(a_xt.sem, 1)
            act.wait_ge(init, 8)

            tasks = {10: (0, 0), 12: (0, 1), 18: (1, 0), 20: (1, 1), 26: (2, 0), 28: (2, 1),
                     30: (3, 0), 31: (3, 1)}

            def half(b, n):
                for s in range(STEPS):
                    step = n * STEPS + s
                    act.wait_ge(c_mm.sem, c_mm.at(b, step + 1))
                    nxt = (step + 1) % (2 * STEPS)
                    if step == 0:
                        act.wait_ge(c_hs.sem, c_hs.at(b, 0))
                    s_.activation(HB[0:ST, nxt], PS[0:ST, 7, 0:B], ACT.Tanh).then_inc(c_h.sem, 1)
                    if s in tasks:
                        z, m = tasks[s]
                        if m == 0:
                            act.wait_ge(c_z.sem, c_z.at(b, 5 * n + z + 1))
                            if z < 3:
                                act.wait_ge(c_c.sem, c_c.at(b, 4 * n))
                            else:
                                act.wait_ge(c_gs.sem, c_gs.at(b, n))
                        dst = TG[:, z, m] if z < 3 else GS[:, m]
                        s_.activation(dst, PS[:, z, m * HALF:(m + 1) * HALF], ACT.Tanh,
                                      bias=b_z[:, z, m:m + 1], scale=(1.0 if z == 2 else 0.5)
                                      ).then_inc(c_t.sem, 1)

            with act.Fori(0, B) as b:
                half(b, 0)
                half(b, 1)
            act.wait_ge(c_h.sem, 2 * STEPS * B + 1)
            act.wait_ge(c_t.sem, 16 * B + c_t.credit)
            act.sem_inc(f_act, 1)

            def batch(b):
                act.wait_ge(p_hq.sem, p_hq.at(b, 1))
                s_.activation(WX[:, :, :], WX[:, :, :], ACT.Tanh).then_inc(g_t.sem, 1)
                act.wait_ge(g_t.sem, g_t.at(b, 1))
                act.wait_ge(s_v.sem, s_v.at(b, 0))
                s_.activation(SG[:, :, :], WX[:, :, :], ACT.Tanh, scale=0.5).then_inc(g_t.sem, 1)
                act.wait_ge(n_xn.sem, n_xn.at(b, NT))
                act.wait_ge(z_o.sem, z_o.at(b, 0))
                for j in range(NT):
                    s_.activation(SG2[:, j], S1[:, j], ACT.Square, accum_out=x2[:, j:j + 1]
                                  ).then_inc(n_x2.sem, 1)
                for k in range(KT):
                    act.wait_ge(n_tr.sem, n_tr.at(b, k + 1))
                    s_.copy(XT1[:, k], PS[:, 2 + k, :]).then_inc(n_xt.sem, 1)
                act.wait_ge(q_s.sem, q_s.at(b, 0))
                for n in range(4):
                    act.wait_ge(q_mm.sem, q_mm.at(b, n + 1))
                    s_.copy(QF[:, n], PS[:, (4 + n) % 6, :]).then_inc(q_e.sem, 1)
                act.wait_ge(d_v.sem, d_v.at(b, 5))
                s_.activation(ex[:, :, :], dst[:, :, :], ACT.Exp, scale=ntemp[:, 0:1]).then_inc(d_e.sem, 1)
                for j in range(NT):
                    act.wait_ge(h_t.sem, h_t.at(b, j + 1))
                    s_.copy(HMT[:, :, j * P:(j + 1) * P],
                            PS[:, 7, :].rearrange("p (n q) -> p n q", q=P)).then_inc(h_e.sem, 1)
                act.wait_ge(n_x2.sem, n_x2.at(b, NT))
                for p in range(2):
                    act.wait_ge(e_mm.sem, e_mm.at(b, p + 1))
                    s_.activation(SG2[:, 2 * p:2 * p + 2], PS[:, 7 - p, :].rearrange("p (j d) -> p j d", d=D),
                                  ACT.Tanh, scale=0.5).then_inc(e_t.sem, 1)

                def exp(h):
                    act.wait_ge(t_mm.sem, t_mm.at(b, h + 1))
                    base = 3 * (h % 2)
                    if h % 4 == 0:
                        if h >= 8:
                            act.wait_ge(o_mm.sem, o_mm.at(b, h // 4 - 1))
                        else:
                            act.wait_ge(o_mm.sem, o_mm.at(b, 0))
                    s_.activation(PR[:, h // 4 % 2, h % 4],
                                  PS[:, base:base + 3, :].rearrange("p a b -> p (a b)")[:, 0:PW],
                                  ACT.Exp, scale=SCORE_SCALE).then_inc(t_e.sem, 1)

                def take_values(g):
                    act.wait_ge(o_mm.sem, o_mm.at(b, g + 1))
                    act.wait_ge(o_t.sem, o_t.at(b, g))
                    s_.copy(OS[:, :], PS[:, 6, :]).then_inc(o_e.sem, 1)

                for h in range(H):
                    exp(h)
                    if h % 4 == 2 and h > 4:
                        take_values(h // 4 - 1)
                take_values(3)
                for k in range(KT):
                    act.wait_ge(r_t.sem, r_t.at(b, k + 1))
                    s_.copy(AO[:, k], PS[:, k, :]).then_inc(r_e.sem, 1)

            with act.Fori(0, B) as b:
                batch(b)

        @block.vector
        def _(dve):
            v_ = nc.vector
            for s in (a_st, a_xn, a_ue, c_w, c_c, y_v, s_v, n_st, n_xn, q_s, v_e, d_v, d_m, m_r, m_h, h_v,
                      w_e, e_v, o_r, o_v, z_v):
                dve.sem_inc(s.sem, s.credit)

            def hold():
                v_.memset(scratch[:, :], 0.0)

            dve.wait_ge(ld_w, LOADED)
            v_.tensor_tensor(ptsq, w_pt[:, :, :], w_pt[:, :, :], ALU.mult).then_inc(init, 1)
            v_.scalar_tensor_tensor(out=atemp[:, :], in0=ntemp[:, :], scalar=-1.0, in1=ntemp[:, :],
                                    op0=ALU.mult, op1=ALU.max).then_inc(temps, 1)
            dve.wait_ge(temps, 1)
            v_.tensor_scalar(ntemp[:, :], atemp[:, :], 0.1, None, ALU.max).then_inc(init, 1)
            dve.wait_ge(init, 2)
            v_.reciprocal(ntemp[:, :], ntemp[:, :]).then_inc(init, 1)
            dve.wait_ge(init, 3)
            v_.tensor_scalar(ntemp[:, :], ntemp[:, :], -1.0, None, ALU.mult).then_inc(init, 1)
            dve.wait_ge(pe_init, 1)
            v_.tensor_copy(p2[:, :], PS[:, 7, 0:NP]).then_inc(init, 1)
            v_.memset(HB[0:ST, 0], 0.0).then_inc(init, 1)
            v_.memset(K6[KS:P, :, :], 1.0).then_inc(init, 1)
            v_.tensor_copy(CT, c0.unsqueeze(2).to_broadcast([P, KT, T])).then_inc(init, 1)

            def statistics(x, st, b, base):
                for j in range(NT):
                    v_.bn_stats(bnst[:, j], x[:, j]).then_inc(st.sem, 1)
                dve.wait_ge(st.sem, st.at(b, base + NT))
                hold()
                for j in range(NT):
                    v_.bn_aggr(mv[:, j], bnst[:, j]).then_inc(st.sem, 1)

            with dve.Fori(0, B // 2) as g:
                for s in range(2):
                    dve.wait_ge(a_x[s].sem, a_x[s].at(g, 1))
                    statistics(xin[s][:, :, :], a_st, g, 2 * NT * s)
                    dve.wait_ge(a_rs.sem, a_rs.at(g, 2 * (s + 1)))
                    dve.wait_ge(a_sv.sem, a_sv.at(g, 0))
                    for j in range(NT):
                        mm = v_.tensor_scalar(xnp[s][:, j], xin[s][:, j], mv[:, j, 0:1], rst[:, j:j + 1],
                                              ALU.subtract, ALU.mult)
                    mm.then_inc(a_xn.sem, 1)
                    dve.wait_ge(a_u.sem, a_u.at(g, s + 1))
                    v_.tensor_scalar(HU[ST:P, :].rearrange("p (t b) -> p b t", b=B)
                                     [:, bass.ds(g * 2 + s, 1)].rearrange("p o t -> p (o t)"),
                                     PS[ST:P, 2, :], b_in[ST:P, 0:1], None, ALU.add).then_inc(a_ue.sem, 1)

            def half(b, n):
                c = CT[:, :, n * HALF:(n + 1) * HALF]
                dve.wait_ge(c_t.sem, c_t.at(b, 8 * n + 6))
                v_.scalar_tensor_tensor(out=c, in0=TG[:, 0], scalar=1.0, in1=c, op0=ALU.add, op1=ALU.mult
                                        ).then_inc(c_c.sem, 1)
                v_.scalar_tensor_tensor(out=CA, in0=TG[:, 1], scalar=1.0, in1=TG[:, 2], op0=ALU.add,
                                        op1=ALU.mult).then_inc(c_c.sem, 1)
                dve.wait_ge(c_c.sem, c_c.at(b, 4 * n + 2))
                v_.tensor_tensor(c, c, CA, ALU.add).then_inc(c_c.sem, 1)
                dve.wait_ge(c_c.sem, c_c.at(b, 4 * n + 3))
                v_.tensor_scalar(c, c, 0.5, None, ALU.mult).then_inc(c_c.sem, 1)
                dve.wait_ge(c_z.sem, c_z.at(b, 5 * n + 5))
                dve.wait_ge(c_ws.sem, c_ws.at(b, n))
                v_.tensor_copy(WS, PS[:, 4, :].rearrange("p (j d) -> p j d", d=D)).then_inc(c_w.sem, 1)

            with dve.Fori(0, B) as b:
                half(b, 0)
                half(b, 1)

            dve.wait_ge(f_pe, 1)
            for n in range(2):
                v_.tensor_tensor(UC[:, 2 * n:2 * n + 2], PS[:, n, :].rearrange("p (j d) -> p j d", d=D),
                                 bo[:, :].unsqueeze(1).to_broadcast([P, 2, D]), ALU.add).then_inc(f_e, 1)

            def batch(b):
                dve.wait_ge(l_xt.sem, l_xt.at(b, 1))
                dve.wait_ge(l_gt.sem, l_gt.at(b, 1))
                for m in range(KT):
                    dve.wait_ge(y_mm.sem, y_mm.at(b, m + 1))
                    v_.tensor_tensor(YS[:, m], PS[:, 6 + m, :], XT[:, m], ALU.subtract).then_inc(y_v.sem, 1)
                dve.wait_ge(y_v.sem, y_v.at(b, KT))
                for m in range(KT):
                    v_.scalar_tensor_tensor(out=YS[:, m], in0=GT[:, m], scalar=1.0, in1=YS[:, m],
                                            op0=ALU.add, op1=ALU.mult).then_inc(y_v.sem, 1)
                dve.wait_ge(y_v.sem, y_v.at(b, 2 * KT))
                for m in range(KT):
                    v_.scalar_tensor_tensor(out=YS[:, m], in0=YS[:, m], scalar=0.5, in1=XT[:, m],
                                            op0=ALU.mult, op1=ALU.add).then_inc(y_v.sem, 1)
                dve.wait_ge(p_xn.sem, p_xn.at(b, 1))
                for p in range(2):
                    dve.wait_ge(s_mm.sem, s_mm.at(b, p + 1))
                    v_.tensor_tensor(S1[:, 2 * p:2 * p + 2], PS[:, p, :].rearrange("p (j d) -> p j d", d=D),
                                     XNB[:, 2 * p:2 * p + 2], ALU.add).then_inc(s_v.sem, 1)
                dve.wait_ge(p_sg.sem, p_sg.at(b, 2))
                dve.wait_ge(s_v.sem, s_v.at(b, 2))
                for p in range(2):
                    v_.tensor_tensor(S1[:, 2 * p:2 * p + 2], S1[:, 2 * p:2 * p + 2], SG[:, 2 * p:2 * p + 2],
                                     ALU.mult).then_inc(s_v.sem, 1)
                dve.wait_ge(l_x.sem, l_x.at(b, 1))
                dve.wait_ge(s_v.sem, s_v.at(b, 4))
                for p in range(2):
                    v_.scalar_tensor_tensor(out=X1[:, 2 * p:2 * p + 2], in0=S1[:, 2 * p:2 * p + 2], scalar=0.5,
                                            in1=X1[:, 2 * p:2 * p + 2], op0=ALU.mult, op1=ALU.add
                                            ).then_inc(s_v.sem, 1)
                dve.wait_ge(s_v.sem, s_v.at(b, 6))
                statistics(X1, n_st, b, 0)
                dve.wait_ge(n_rs.sem, n_rs.at(b, 2))
                for j in range(NT):
                    v_.tensor_scalar(S1[:, j], X1[:, j], mv[:, j, 0:1], rst[:, j:j + 1], ALU.subtract,
                                     ALU.mult).then_inc(n_xn.sem, 1)
                dve.wait_ge(q_e.sem, q_e.at(b, 4))
                dve.wait_ge(q_st.sem, q_st.at(b, 0))
                for n in range(SPLIT):
                    if n:
                        dve.wait_ge(q_r.sem, q_r.at(b, n))
                    v_.tensor_copy(QB[:, n], QF[:, :, :]).then_inc(q_s.sem, 1)
                    if n == 0:
                        dve.wait_ge(d_mm.sem, d_mm.at(b, 1))
                        v_.scalar_tensor_tensor(out=dst[:, :, :],
                                                in0=PS[:, 7, 0:NT * NP].rearrange("p (j n) -> p j n", n=NP),
                                                scalar=-2.0, in1=p2[:, :].unsqueeze(1).to_broadcast([P, NT, NP]),
                                                op0=ALU.mult, op1=ALU.add).then_inc(d_v.sem, 1)
                        dve.wait_ge(d_v.sem, d_v.at(b, 1))
                        dve.wait_ge(n_x2.sem, n_x2.at(b, NT))
                        v_.tensor_tensor(dst[:, :, :], dst[:, :, :],
                                         x2[:, :].unsqueeze(2).to_broadcast([P, NT, NP]), ALU.add
                                         ).then_inc(d_v.sem, 1)
                        dve.wait_ge(d_v.sem, d_v.at(b, 2))
                        v_.tensor_scalar(dst[:, :, :], dst[:, :, :], 0.0, None, ALU.max).then_inc(d_v.sem, 1)
                    if n == 1:
                        for p in range(2):
                            dve.wait_ge(v_mm.sem, v_mm.at(b, p + 1))
                            v_.tensor_scalar(VA[:, 2 * p:2 * p + 2, :, 0:HD],
                                             PS[:, 2 + p, :].rearrange("p (j h d) -> p j h d", j=2, d=HD),
                                             OUT_SCALE, None, ALU.mult).then_inc(v_e.sem, 1)
                dve.wait_ge(d_p.sem, d_p.at(b, 1))
                v_.tensor_reduce(dmn[:, :], dst[:, :, :], AX.X, ALU.min).then_inc(d_v.sem, 1)
                dve.wait_ge(d_v.sem, d_v.at(b, 4))
                v_.tensor_tensor(dst[:, :, :], dst[:, :, :], dmn[:, :].unsqueeze(2).to_broadcast([P, NT, NP]),
                                 ALU.subtract).then_inc(d_v.sem, 1)

                def maxima(u):
                    hp, i = u // NT, u % NT
                    dve.wait_ge(m_mm.sem, m_mm.at(b, u + 1))
                    v_.tensor_reduce(nm[:, i, 2 * hp:2 * hp + 2],
                                     PS[:, 2 * (u % 3):2 * (u % 3) + 2, 0:(i + 1) * P], AX.X, ALU.max,
                                     negate=True).then_inc(m_r.sem, 1)

                def choose():
                    dve.wait_ge(d_e.sem, d_e.at(b, 1))
                    hold()
                    for j in range(NT):
                        v_.max(top[:, j], ex[:, j]).then_inc(d_m.sem, 1)
                    dve.wait_ge(d_m.sem, d_m.at(b, NT))
                    hold()
                    for j in range(NT):
                        v_.max_index(topi[:, j], top[:, j], ex[:, j]).then_inc(d_m.sem, 1)
                    dve.wait_ge(d_m.sem, d_m.at(b, 2 * NT))
                    v_.tensor_copy(topf[:, :, :], topi[:, :, 0:2]).then_inc(d_v.sem, 1)
                    v_.tensor_tensor(rden[:, :], top[:, :, 0], top[:, :, 1], ALU.add).then_inc(d_v.sem, 1)
                    dve.wait_ge(d_v.sem, d_v.at(b, 7))
                    v_.reciprocal(rden[:, :], rden[:, :]).then_inc(d_v.sem, 1)
                    for n, dst_ in enumerate((hit, wm)):
                        v_.tensor_tensor(dst_[:, :, :], iota[:, :].unsqueeze(1).to_broadcast([P, NT, NP]),
                                         topf[:, :, n:n + 1].to_broadcast([P, NT, NP]), ALU.is_equal
                                         ).then_inc(d_v.sem, 1)
                    dve.wait_ge(d_v.sem, d_v.at(b, 10))
                    v_.tensor_tensor(hit[:, :, :], hit[:, :, :], wm[:, :, :], ALU.add).then_inc(d_v.sem, 1)
                    v_.tensor_tensor(ex[:, :, :], ex[:, :, :], rden[:, :].unsqueeze(2).to_broadcast([P, NT, NP]),
                                     ALU.mult).then_inc(d_v.sem, 1)
                    dve.wait_ge(d_v.sem, d_v.at(b, 12))
                    v_.tensor_tensor(wm[:, :, :], ex[:, :, :], hit[:, :, :], ALU.mult).then_inc(d_v.sem, 1)

                def weigh(j):
                    dve.wait_ge(h_mm.sem, h_mm.at(b, j + 1))
                    dve.wait_ge(d_v.sem, d_v.at(b, 13))
                    dve.wait_ge(h_t.sem, h_t.at(b, j))
                    v_.tensor_tensor(HM.rearrange("p (n r) -> p n r", r=RANK),
                                     PS[:, 6, :].rearrange("p (n r) -> p n r", r=RANK),
                                     wm[:, j].unsqueeze(2).to_broadcast([P, NP, RANK]), ALU.mult
                                     ).then_inc(h_v.sem, 1)

                def take_weights():
                    dve.wait_ge(w_t.sem, w_t.at(b, 1))
                    v_.tensor_copy(wmt[:, :], PS[0:NP, 6, :]).then_inc(w_e.sem, 1)

                def gate(p):
                    dve.wait_ge(e_t.sem, e_t.at(b, p + 1))
                    v_.scalar_tensor_tensor(out=SG2[:, 2 * p:2 * p + 2], in0=SG2[:, 2 * p:2 * p + 2],
                                            scalar=1.0, in1=PS[:, 7 - p, :].rearrange("p (j d) -> p j d", d=D),
                                            op0=ALU.add, op1=ALU.mult).then_inc(e_v.sem, 1)

                side = {0: choose, 2: lambda: weigh(0), 7: lambda: weigh(1), 12: lambda: weigh(2),
                        17: lambda: weigh(3), 22: take_weights, 26: lambda: gate(0), 29: lambda: gate(1)}
                for u in range(NT * H // 2):
                    maxima(u)
                    if u in side:
                        side[u]()
                dve.wait_ge(m_t.sem, m_t.at(b, 1))
                v_.tensor_copy(nmh[:, :], PS[0:H, 6, :]).then_inc(m_h.sem, 1)
                dve.wait_ge(m_h.sem, m_h.at(b, 1))
                v_.tensor_tensor(nml[:, :], PS[0:H, 6, :], nmh[:, :], ALU.subtract).then_inc(m_h.sem, 1)
                for g in range(4):
                    dve.wait_ge(o_t.sem, o_t.at(b, g + 1))
                    o = PS[:, 7, :].rearrange("p (j n d) -> p j n d", n=4, d=32)
                    v_.reciprocal(rec[:, :, :], o[:, :, :, HD]).then_inc(o_r.sem, 1)
                    dve.wait_ge(o_r.sem, o_r.at(b, g + 1))
                    v_.tensor_tensor(AT[:, :, g * 64:(g + 1) * 64].rearrange("p j (n d) -> p j n d", d=HD),
                                     o[:, :, :, 0:HD], rec[:, :, :].unsqueeze(3).to_broadcast([P, NT, 4, HD]),
                                     ALU.mult).then_inc(o_v.sem, 1)
                for p in range(2):
                    dve.wait_ge(z_mm.sem, z_mm.at(b, p + 1))
                    v_.tensor_tensor(SG2[:, 2 * p:2 * p + 2], PS[:, 6 + p, :].rearrange("p (j d) -> p j d", d=D),
                                     SG2[:, 2 * p:2 * p + 2], ALU.mult).then_inc(z_v.sem, 1)
                dve.wait_ge(z_v.sem, z_v.at(b, 2))
                for p in range(2):
                    v_.scalar_tensor_tensor(out=SG2[:, 2 * p:2 * p + 2], in0=SG2[:, 2 * p:2 * p + 2],
                                            scalar=0.5 * OUT_SCALE, in1=X1[:, 2 * p:2 * p + 2],
                                            op0=ALU.mult, op1=ALU.add).then_inc(z_v.sem, 1)

            with dve.Fori(0, B) as b:
                batch(b)


_SHAPE = ((B, T, D), "float32")


def _layout(inputs):
    import numpy as np

    def c(x):
        return np.ascontiguousarray(x)

    i = {k: np.asarray(v) for k, v in inputs.items()}
    f, s = "L0_ffn_", "L0_attn_"
    w = {"L0_attn_x": c(i["L0_attn_x"]), "W_in": c(i[s + "W_in"]), "W_gate": c(i[s + "W_gate"]),
         "A": c(i[s + "A"]), "Bm": c(i[s + "Bm"]), "CT": c(i[s + "C"].T), "DT": c(i[s + "D"].T),
         "W_out": c(i[s + "W_out"]), "b_in": c(i[s + "b_in"]), "b_gate": c(i[s + "b_gate"]),
         "b_out": c(i[s + "b_out"])}
    for n in ("wf", "uf", "wi", "ui", "wc", "uc", "wo", "uo"):
        w[n + "T"] = c(i[f + n].T)
    w["bo"] = c(i[f + "bo"])
    w["b_gate"] = c(w["b_gate"].reshape(KT, P).T)
    for n in ("bf", "bi", "bc", "in_c"):
        w[n] = c(i[f + n].reshape(KT, P).T)
    for n, m in (("WqT", "W_query"), ("WkT", "W_key"), ("WvT", "W_value"), ("WpT", "W_proj")):
        w[n] = c(i["L1_attn_" + m].T)
    w["BT"] = c(i["L1_ffn_B"].reshape(NR, D).T)
    w["AT"] = c(i["L1_ffn_A"].transpose(0, 2, 1).reshape(NR, D))
    w["protoT"] = c(i["L1_ffn_prototypes"].T)
    w["bias"] = c(i["L1_ffn_bias"])
    w["temp"] = c(i["L1_ffn_temp"].reshape(1))
    return w


def kernel(**inputs):
    import concourse.bacc as bacc
    from concourse.bass_utils import run_bass_kernel_spmd

    nc = bacc.Bacc("TRN2", target_bir_lowering=False, num_devices=1)
    arrays = {}
    aps = {}
    for name, x in _layout(inputs).items():
        arrays[f"in_{name}"] = x
        aps[name] = nc.dram_tensor(f"in_{name}", x.shape, mybir.dt.from_np(x.dtype), kind="ExternalInput").ap()
    out = nc.dram_tensor("out_0", _SHAPE[0], F32, kind="ExternalOutput").ap()
    two_layers(nc, aps, out)
    r = run_bass_kernel_spmd(nc, [arrays], core_ids=[0])
    return r.results[0]["out_0"]
```

```python
from contextlib import ExitStack

import concourse.bass as bass
from concourse import mybir

F32 = mybir.dt.float32
BF16 = mybir.dt.bfloat16
U32 = mybir.dt.uint32
ALU = mybir.AluOpType
ACT = mybir.ActivationFunctionType
AX = mybir.AxisListType

B, T, D = 8, 512, 256
ST = 64
P = 128
KT = D // P
NT = T // P
H, HD = 16, 16
NP, RANK = 32, 16
NR = NP * RANK
HALF = T // 2
STEPS = T // B // 2
EPS = 1e-5
SPLIT = 3
PAIRS = [(0, 0), (0, 1), (1, 0), (0, 2), (2, 0), (1, 1)]
KS = len(PAIRS) * HD
KM = KS + 2
SCORE_SCALE = float(D) ** -1.0 * float(HD) ** -0.5
OUT_SCALE = float(D) ** -0.5
P_AT = {0: 0, 1: 512, 3: 896, 2: 1024}
PU = P_AT[2]
TU = 3 * H // 2
PW = NT * (NT + 1) // 2 * P
BIG = 1.0e30


class Count:

    def __init__(self, handle, per, step=1, credit=1):
        self.sem, self.per, self.step, self.credit = handle, per, step, credit

    def at(self, it, n):
        return it * (self.per * self.step) + (n * self.step + self.credit)


def two_layers(nc, a, out):
    ctx = ExitStack()
    with ctx:
        def sb(name, shape, dt=F32):
            return ctx.enter_context(nc.sbuf_tensor(name, shape, dt))

        def sem(name):
            return ctx.enter_context(nc.semaphore(name))

        def count(name, per, credit=1):
            return Count(sem(name), per, credit=credit)

        def dcount(name, per):
            return Count(sem(name), per, step=16, credit=16)

        xt_d = nc.dram_tensor("xt_d", (B, P, KT, T), F32, kind="Internal").ap()
        xn_d = nc.dram_tensor("xn_d", (B, P, NT, D), F32, kind="Internal").ap()
        gt_d = nc.dram_tensor("gt_d", (B, P, KT, T), F32, kind="Internal").ap()
        wx_d = nc.dram_tensor("wx_d", (B, P, NT, D), F32, kind="Internal").ap()
        x1_d = nc.dram_tensor("x1_d", (B, P, NT, D), F32, kind="Internal").ap()
        qk_d = nc.dram_tensor("qk_d", (SPLIT, 2, D, T), BF16, kind="Internal").ap()

        HU = sb("HU", [P, T * B])
        w_cd = sb("w_cd", [P, D])
        w_out = sb("w_out", [P, KT, D])
        w_qk = sb("w_qk", [P, 2, KT, D])
        w_v = sb("w_v", [P, KT, D])
        w_pr = sb("w_pr", [P, KT, D])
        w_b = sb("w_b", [P, KT, NR])
        w_a = sb("w_a", [P, NR // P, D])
        w_pt = sb("w_pt", [P, KT, NP])
        w_bias = sb("w_bias", [NP, D])
        ident = sb("ident", [P, P])
        identb = sb("identb", [P, P], BF16)
        negmask = sb("negmask", [P, P], BF16)
        negmask_t = sb("negmask_t", [P, P], BF16)
        halves = sb("halves", [P, 2 * NT])
        mhalf = sb("mhalf", [P, NT])
        vscale = sb("vscale", [P, H])
        eps = sb("eps", [P, NT])
        iota = sb("iota", [P, NP])
        ones = sb("ones", [P, P])
        p2 = sb("p2", [P, NP])
        ntemp = sb("ntemp", [P, 1])
        atemp = sb("atemp", [P, 1])
        bout = sb("bout", [P, D])
        bo = sb("bo", [P, D])
        UC = sb("UC", [P, NT, D])
        scratch = sb("scratch", [P, 1])
        Q6 = sb("Q6", [P, H, T], BF16)
        K6 = sb("K6", [P, H, T], BF16)
        XT = sb("XT", [P, KT, T])
        GT = sb("GT", [P, KT, T])
        WX = sb("WX", [P, NT, D])
        X1 = sb("X1", [P, NT, D])
        XNB = sb("XNB", [P, NT, D])
        YS = sb("YS", [P, KT, T])
        SG = sb("SG", [P, NT, D])
        S1 = sb("S1", [P, NT, D])
        XT1 = sb("XT1", [P, KT, T])
        QF = sb("QF", [P, 2 * KT, T])
        QB = sb("QB", [P, SPLIT, 2 * KT, T], BF16)
        OS = sb("OS", [P, T])
        SG2 = sb("SG2", [P, NT, D])
        bnst = sb("bnst", [P, NT, 6])
        mv = sb("mv", [P, NT, 2])
        rst = sb("rst", [P, NT])
        x2 = sb("x2", [P, NT])
        dst = sb("dst", [P, NT, NP])
        top = sb("top", [P, NT, 8])
        topi = sb("topi", [P, NT, 8], U32)
        topf = sb("topf", [P, NT, 2])
        near = sb("near", [P, NT, 2])
        odds = sb("odds", [P, NT])
        hit = sb("hit", [P, NT, NP])
        wm = sb("wm", [P, NT, NP])
        rden = sb("rden", [P, NT])
        wmt = sb("wmt", [NP, T])
        nm = sb("nm", [P, NT, H])
        nmh = sb("nmh", [H, T], BF16)
        nml = sb("nml", [H, T], BF16)
        rec = sb("rec", [P, NT, NT])
        ARENA = 2 * 4 * PW + NR // P * T + T + NT * H * 32
        arena = sb("arena", [P, ARENA])
        used = [0]

        def part(*shape):
            n = 1
            for s in shape:
                n *= s
            v = arena[:, used[0]:used[0] + n]
            used[0] += n
            assert used[0] <= ARENA
            if len(shape) == 1:
                return v
            names = "abcd"[:len(shape)]
            return v.rearrange(f"p ({' '.join(names)}) -> p {' '.join(names)}",
                               **{k: s for k, s in zip(names, shape)})

        w_in = part(KT, ST)
        w_ab = part(ST)
        w_gate = part(KT, D)
        w_x = part(3, KT, D)
        w_c = part(3, KT, D)
        w_wo = part(KT, D)
        w_uo = part(KT, D)
        b_in = part(1)
        b_z = part(4, KT)
        HB = part(2 * STEPS, B)
        XB = part(2, KT, HALF)
        CT = part(KT, T)
        c0 = part(KT)
        TG = part(3, KT, HALF)
        GS = part(KT, HALF)
        WS = part(2, D)
        CA = part(KT, HALF)
        xin, xnp, xtp = (X1, SG2), (SG, S1), (XT1, YS)
        ptsq = part(KT, NP)
        used[0] = 0
        PR = part(2, 4, PW)
        HMT = part(NR // P, T)
        HM = part(T)
        VA = part(NT, H, 32)
        AT = GT[:, :, :].rearrange("p a b -> p (a b)").rearrange("p (t o) -> p t o", t=NT)
        V1 = YS[:, :, :].rearrange("p a b -> p (a b)").rearrange("p (t o) -> p t o", t=NT)
        AO = QF[:, 0:KT, :]

        PS = ctx.enter_context(nc.psum_tensor("PS", [P, 8, 512], F32))

        ld_w = sem("ld_w")
        const = sem("const")
        init = sem("init")
        temps = sem("temps")
        act_init = sem("act_init")
        pe_init = sem("pe_init")
        carried = sem("carried")
        a_x = [dcount(f"a_x{s}", 1) for s in range(2)]
        a_st = count("a_st", 2 * (NT + NT))
        a_rs = count("a_rs", 2 * 2)
        a_xn = count("a_xn", 2)
        a_tr = count("a_tr", 2 * KT)
        a_xt = count("a_xt", 2 * KT)
        a_u = count("a_u", 2)
        a_ue = count("a_ue", 2)
        a_sv = dcount("a_sv", 4)
        c_x = [dcount(f"c_x{n}", 1) for n in range(2)]
        c_u = [dcount(f"c_u{n}", 1) for n in range(2)]
        c_mm = count("c_mm", 2 * STEPS)
        c_h = count("c_h", 2 * STEPS)
        c_z = count("c_z", 2 * 5)
        c_t = count("c_t", 2 * 8, 7)
        c_w = count("c_w", 2)
        c_c = count("c_c", 2 * 4, 5)
        c_hs = dcount("c_hs", 3)
        c_gs = dcount("c_gs", 2)
        c_ws = dcount("c_ws", 2)
        f_z = sem("f_z")
        f_e = sem("f_e")
        f_pe = sem("f_pe")
        f_act = sem("f_act")
        f_set = sem("f_set")
        l_xt, l_gt, l_wx, l_x, l_xn = (dcount(n, 1) for n in ("l_xt", "l_gt", "l_wx", "l_x", "l_xn"))
        y_mm = count("y_mm", KT)
        y_v = count("y_v", 3 * KT)
        p_xn = count("p_xn", 1)
        p_hq = count("p_hq", 1)
        g_t = count("g_t", 2)
        p_sg = count("p_sg", 2)
        s_mm = count("s_mm", 2)
        s_v = count("s_v", 3 * 2)
        n_st = count("n_st", 2 * NT)
        n_rs = count("n_rs", 2)
        n_xn = count("n_xn", NT)
        n_x2 = count("n_x2", NT)
        n_tr = count("n_tr", KT)
        n_xt = count("n_xt", KT)
        q_mm = count("q_mm", 4)
        q_e = count("q_e", 4)
        q_s = count("q_s", 3)
        q_r = count("q_r", 2)
        q_st = dcount("q_st", 1)
        x_sv = dcount("x_sv", 1)
        x_ld = dcount("x_ld", 1)
        q_ld = dcount("q_ld", 2 * len(PAIRS))
        v_mm = count("v_mm", 2)
        v_e = count("v_e", 2)
        v_c = count("v_c", 1)
        d_mm = count("d_mm", 1)
        d_v = count("d_v", 14)
        d_p = count("d_p", 1)
        d_e = count("d_e", 1)
        d_m = count("d_m", 2 * NT)
        m_mm = count("m_mm", NT * H // 2)
        m_r = count("m_r", NT * H // 2)
        m_t = count("m_t", 1)
        m_h = count("m_h", 2)
        m_ld = dcount("m_ld", 2)
        h_mm = count("h_mm", NT)
        h_v = count("h_v", NT)
        h_t = count("h_t", NT)
        h_e = count("h_e", NT)
        w_t = count("w_t", 1)
        w_e = count("w_e", 1)
        e_mm = count("e_mm", 2)
        e_t = count("e_t", 2)
        e_v = count("e_v", 2)
        t_mm = count("t_mm", TU)
        t_e = count("t_e", TU)
        o_mm = count("o_mm", 4)
        o_e = count("o_e", 4)
        o_t = count("o_t", 4)
        o_r = count("o_r", 4)
        o_v = count("o_v", 4)
        r_t = count("r_t", KT, KT + 1)
        r_e = count("r_e", KT)
        z_mm = count("z_mm", 2, 3)
        z_v = count("z_v", 2 * 2)
        z_o = dcount("z_o", 1)

        x_v = a["L0_attn_x"].rearrange("b (j p) d -> b p j d", p=P)
        o_view = out.rearrange("b (j p) d -> b p j d", p=P)

        def rows(w):
            return w.rearrange("(k p) n -> p k n", p=P)

        loads = [
            (w_in, rows(a["W_in"])), (w_ab[0:ST, :], a["A"]), (w_ab[ST:P, :], a["Bm"]),
            (w_gate, rows(a["W_gate"])), (w_cd[0:ST, :], a["CT"]), (w_cd[ST:P, :], a["DT"]),
            (w_out[:, :, :], rows(a["W_out"])),
            (w_x[:, 0], rows(a["wfT"])), (w_x[:, 1], rows(a["wiT"])), (w_x[:, 2], rows(a["wcT"])),
            (w_c[:, 0], rows(a["ufT"])), (w_c[:, 1], rows(a["uiT"])), (w_c[:, 2], rows(a["ucT"])),
            (w_wo, rows(a["woT"])), (w_uo, rows(a["uoT"])),
            (b_in[ST:P, :], a["b_in"].rearrange("(p o) -> p o", o=1)),
            (b_z[:, 0], a["bf"]), (b_z[:, 1], a["bi"]), (b_z[:, 2], a["bc"]),
            (b_z[:, 3], a["b_gate"]), (c0, a["in_c"]),
            (w_qk[:, 0], rows(a["WqT"])), (w_qk[:, 1], rows(a["WkT"])), (w_v[:, :, :], rows(a["WvT"])),
            (w_pr[:, :, :], rows(a["WpT"])), (w_b[:, :, :], rows(a["BT"])), (w_a[:, :, :], rows(a["AT"])),
            (w_pt[:, :, :], rows(a["protoT"])), (w_bias[:, :], a["bias"]),
            (bout[:, :], a["b_out"].partition_broadcast(P)), (bo[:, :], a["bo"].partition_broadcast(P)),
            (ntemp[:, :], a["temp"].partition_broadcast(P)),
        ]
        LOADED = 16 * len(loads)

        block = ctx.enter_context(nc.Block())

        @block.sync
        def _(sp):
            for s in (*a_x, a_sv, *c_x, *c_u, c_hs, c_gs, c_ws, l_xt, l_gt, l_wx, l_x, l_xn, q_st, x_sv, x_ld, q_ld, m_ld, z_o):
                sp.sem_inc(s.sem, s.credit)
            for dst, src in loads:
                sp.dma_start(dst, src).then_inc(ld_w, 16)

            def prepass(g):
                for s in range(2):
                    sp.wait_ge(a_xn.sem, a_xn.at(g, 0))
                    sp.dma_start(xin[s][:, :, :], x_v[bass.ds(g * 2 + s, 1)].rearrange("o p j d -> p (o j) d")
                                 ).then_inc(a_x[s].sem, 16)
                for s in range(2):
                    sp.wait_ge(a_xn.sem, a_xn.at(g, s + 1))
                    sp.dma_start(xn_d[bass.ds(g * 2 + s, 1)].rearrange("o p j d -> p (o j) d"), xnp[s][:, :, :]
                                 ).then_inc(a_sv.sem, 16)
                    sp.wait_ge(a_xt.sem, a_xt.at(g, KT * (s + 1)))
                    sp.dma_start(xt_d[bass.ds(g * 2 + s, 1)].rearrange("o p k t -> p (o k) t"), xtp[s][:, :, :]
                                 ).then_inc(a_sv.sem, 16)

            with sp.Fori(0, B // 2) as g:
                prepass(g)
            sp.wait_ge(a_sv.sem, 16 * (2 * B + 1))
            sp.wait_ge(a_ue.sem, B + 1)

            def load_half(b, n):
                sp.dma_start(XB[:, n], xt_d[bass.ds(b, 1), :, :, n * HALF:(n + 1) * HALF]
                             .rearrange("o p k t -> p (o k) t")).then_inc(c_x[n].sem, 16)
                sp.dma_start(HB[ST:P, n * STEPS:(n + 1) * STEPS],
                             HU[ST:P, bass.ds(b * (2 * STEPS * B) + n * STEPS * B, STEPS * B)]
                             .rearrange("p (s b) -> p s b", b=B)).then_inc(c_u[n].sem, 16)

            def save_half(b, n):
                col = b * (2 * STEPS * B)
                sp.wait_ge(c_h.sem, c_h.at(b, (n + 1) * STEPS))
                if n == 0:
                    sp.dma_start(HU[0:ST, bass.ds(col, STEPS * B)], HB[0:ST, 1:STEPS + 1]
                                 .rearrange("p s b -> p (s b)")).then_inc(c_hs.sem, 16)
                else:
                    sp.dma_start(HU[0:ST, bass.ds(col + STEPS * B, (STEPS - 1) * B)],
                                 HB[0:ST, STEPS + 1:2 * STEPS].rearrange("p s b -> p (s b)")
                                 ).then_inc(c_hs.sem, 16)
                    sp.dma_start(HU[0:ST, bass.ds(col + (2 * STEPS - 1) * B, B)], HB[0:ST, 0]
                                 ).then_inc(c_hs.sem, 16)
                sp.wait_ge(c_t.sem, c_t.at(b, 8 * (n + 1)))
                sp.dma_start(gt_d[bass.ds(b, 1), :, :, n * HALF:(n + 1) * HALF]
                             .rearrange("o p k t -> p (o k) t"), GS).then_inc(c_gs.sem, 16)
                sp.wait_ge(c_w.sem, c_w.at(b, n + 1))
                sp.dma_start(wx_d[bass.ds(b, 1), :, 2 * n:2 * n + 2]
                             .rearrange("o p j d -> p (o j) d"), WS).then_inc(c_ws.sem, 16)

            load_half(0, 0)
            load_half(0, 1)

            with sp.Fori(0, B - 1) as b:
                save_half(b, 0)
                sp.wait_ge(c_z.sem, c_z.at(b, 5))
                load_half(b + 1, 0)
                save_half(b, 1)
                sp.wait_ge(c_z.sem, c_z.at(b, 10))
                load_half(b + 1, 1)
            save_half(B - 1, 0)
            save_half(B - 1, 1)
            sp.wait_ge(c_hs.sem, 16 * (3 * B + 1))
            sp.wait_ge(c_gs.sem, 16 * (2 * B + 1))
            sp.wait_ge(c_ws.sem, 16 * (2 * B + 1))

            def hold():
                sp.sem_inc(carried, 1)

            def load_batch(b):
                one = bass.ds(b, 1)
                sp.wait_ge(s_v.sem, s_v.at(b, 0))
                sp.wait_ge(p_sg.sem, p_sg.at(b, 0))
                sp.wait_ge(r_t.sem, r_t.at(b, -KT))
                sp.wait_ge(x_sv.sem, x_sv.at(b, 0))
                sp.wait_ge(n_xn.sem, n_xn.at(b, 0))
                sp.dma_start(XT[:, :, :], xt_d[one].rearrange("o p k t -> p (o k) t")).then_inc(l_xt.sem, 16)
                sp.dma_start(GT[:, :, :], gt_d[one].rearrange("o p k t -> p (o k) t")).then_inc(l_gt.sem, 16)
                sp.dma_start(WX[:, :, :], wx_d[one].rearrange("o p j d -> p (o j) d")).then_inc(l_wx.sem, 16)
                sp.dma_start(XNB[:, :, :], xn_d[one].rearrange("o p j d -> p (o j) d")).then_inc(l_xn.sem, 16)
                sp.dma_start(X1[:, :, :], x_v[one].rearrange("o p j d -> p (o j) d")).then_inc(l_x.sem, 16)

            def save_x1(b):
                sp.wait_ge(s_v.sem, s_v.at(b, 6))
                sp.dma_start(x1_d[bass.ds(b, 1)].rearrange("o p j d -> p (o j) d"), X1[:, :, :]
                             ).then_inc(x_sv.sem, 16)

            def operands(b):
                sp.wait_ge(q_s.sem, q_s.at(b, 3))
                sp.dma_start(qk_d.rearrange("s c (m p) t -> p s (c m) t", p=P), QB[:, :, :, :]
                             ).then_inc(q_st.sem, 16)
                sp.wait_ge(q_st.sem, q_st.at(b, 1))
                hold()
                sp.wait_ge(t_mm.sem, t_mm.at(b, 0))
                for r, pair in enumerate(PAIRS):
                    for c, dst in enumerate((Q6, K6)):
                        sp.dma_start(dst[r * HD:(r + 1) * HD, :, :],
                                     qk_d[pair[c], c].rearrange("(h d) t -> d h t", d=HD)
                                     ).then_inc(q_ld.sem, 16)

            def batch(b, more):
                if more:
                    load_batch(b + 1)
                sp.wait_ge(m_h.sem, m_h.at(b, 2))
                sp.dma_start(Q6[KS:KS + 1, :, :], nmh[:, :]).then_inc(m_ld.sem, 16)
                sp.dma_start(Q6[KS + 1:KS + 2, :, :], nml[:, :]).then_inc(m_ld.sem, 16)
                if more:
                    save_x1(b + 1)
                    sp.wait_ge(n_tr.sem, n_tr.at(b + 1, KT))
                    hold()
                    sp.wait_ge(n_x2.sem, n_x2.at(b + 1, NT))
                    hold()
                sp.wait_ge(x_sv.sem, x_sv.at(b, 1))
                sp.dma_start(S1[:, :, :], x1_d[bass.ds(b, 1)].rearrange("o p j d -> p (o j) d")
                             ).then_inc(x_ld.sem, 16)
                if more:
                    operands(b + 1)
                sp.wait_ge(z_v.sem, z_v.at(b, 4))
                sp.dma_start(o_view[bass.ds(b, 1)].rearrange("o p j d -> p (o j) d"), SG2[:, :, :]
                             ).then_inc(z_o.sem, 16)

            load_batch(0)
            save_x1(0)
            operands(0)
            with sp.Fori(0, B - 1) as b:
                batch(b, True)
            batch(B - 1, False)
            sp.wait_ge(z_o.sem, 16 * (B + 1))

        @block.gpsimd
        def _(pool):
            g_ = nc.gpsimd
            for s in (a_rs, p_xn, p_hq, p_sg, n_rs, q_r, d_p, v_c):
                pool.sem_inc(s.sem, s.credit)
            g_.memset(ident[:, :], 0.0).then_inc(const, 1)
            g_.memset(negmask[:, :], 0.0).then_inc(const, 1)
            g_.memset(negmask_t[:, :], 0.0).then_inc(const, 1)
            g_.memset(eps[:, :], EPS).then_inc(const, 1)
            g_.memset(halves[:, :], 0.5).then_inc(const, 1)
            g_.memset(mhalf[:, :], -0.5).then_inc(const, 1)
            g_.memset(ones[:, :], 1.0).then_inc(const, 1)
            g_.iota(iota[:, :], pattern=[[1, NP]], base=0, channel_multiplier=0,
                    allow_small_or_imprecise_dtypes=True).then_inc(const, 1)
            pool.wait_ge(const, 8)
            g_.affine_select(out=ident[:, :], in_=ident[:, :], compare_op=ALU.not_equal, fill=1.0, base=0,
                             pattern=[[-1, P]], channel_multiplier=1).then_inc(const, 1)
            g_.affine_select(out=negmask[:, :], in_=negmask[:, :], compare_op=ALU.is_ge, fill=-BIG, base=0,
                             pattern=[[-1, P]], channel_multiplier=1).then_inc(const, 1)
            g_.affine_select(out=negmask_t[:, :], in_=negmask_t[:, :], compare_op=ALU.is_ge, fill=-BIG, base=0,
                             pattern=[[1, P]], channel_multiplier=-1).then_inc(const, 1)
            g_.memset(vscale[:, :], OUT_SCALE).then_inc(const, 1)
            pool.wait_ge(const, 11)
            g_.tensor_copy(identb[:, :], ident[:, :]).then_inc(const, 1)

            with pool.Fori(0, B // 2) as g:
                for s in range(2):
                    pool.wait_ge(a_st.sem, a_st.at(g, 2 * NT * (s + 1)))
                    g_.tensor_tensor(rst[:, :], mv[:, :, 1], eps[:, :], ALU.add).then_inc(a_rs.sem, 1)
                    pool.wait_ge(a_rs.sem, a_rs.at(g, 2 * s + 1))
                    g_.tensor_tensor(rst[:, :], rst[:, :], mhalf[:, :], ALU.pow).then_inc(a_rs.sem, 1)

            pool.wait_ge(f_pe, 1)
            pool.wait_ge(f_act, 1)
            pool.wait_ge(c_hs.sem, 16 * (3 * B + 1))
            pool.wait_ge(c_gs.sem, 16 * (2 * B + 1))
            pool.wait_ge(c_ws.sem, 16 * (2 * B + 1))
            g_.memset(VA[:, :, :, :], 0.0).then_inc(f_set, 1)
            pool.wait_ge(f_set, 1)
            g_.memset(VA[:, :, :, HD:HD + 1], 1.0).then_inc(f_set, 1)

            def batch(b):
                pool.wait_ge(l_xn.sem, l_xn.at(b, 1))
                g_.tensor_tensor(XNB[:, :, :], XNB[:, :, :],
                                 bout[:, :].unsqueeze(1).to_broadcast([P, NT, D]), ALU.add
                                 ).then_inc(p_xn.sem, 1)
                pool.wait_ge(l_wx.sem, l_wx.at(b, 1))
                g_.tensor_tensor(WX[:, :, :], WX[:, :, :], UC[:, :, :], ALU.add).then_inc(p_hq.sem, 1)
                pool.wait_ge(g_t.sem, g_t.at(b, 2))
                g_.tensor_tensor(SG[:, :, :], SG[:, :, :], WX[:, :, :], ALU.mult).then_inc(p_sg.sem, 1)
                pool.wait_ge(p_sg.sem, p_sg.at(b, 1))
                g_.tensor_tensor(SG[:, :, :], SG[:, :, :], WX[:, :, :], ALU.add).then_inc(p_sg.sem, 1)
                pool.wait_ge(n_st.sem, n_st.at(b, 2 * NT))
                g_.tensor_tensor(rst[:, :], mv[:, :, 1], eps[:, :], ALU.add).then_inc(n_rs.sem, 1)
                pool.wait_ge(n_rs.sem, n_rs.at(b, 1))
                g_.tensor_tensor(rst[:, :], rst[:, :], mhalf[:, :], ALU.pow).then_inc(n_rs.sem, 1)
                pool.wait_ge(q_s.sem, q_s.at(b, 1))
                g_.tensor_tensor(QF[:, :, :], QF[:, :, :], QB[:, 0], ALU.subtract).then_inc(q_r.sem, 1)
                pool.wait_ge(d_v.sem, d_v.at(b, 5))
                g_.tensor_tensor(near[:, :, :].rearrange("p a b -> p (a b)"),
                                 near[:, :, :].rearrange("p a b -> p (a b)"), halves[:, :], ALU.pow
                                 ).then_inc(d_p.sem, 1)
                pool.wait_ge(q_s.sem, q_s.at(b, 2))
                g_.tensor_tensor(QF[:, :, :], QF[:, :, :], QB[:, 1], ALU.subtract).then_inc(q_r.sem, 1)
                pool.wait_ge(v_e.sem, v_e.at(b, 2))
                pool.wait_ge(o_mm.sem, o_mm.at(b, 0))
                for j in range(NT):
                    mm = g_.tensor_tensor(VA[:, j, :, 0:HD], V1[:, j].rearrange("p (h d) -> p h d", d=HD),
                                          vscale[:, :].unsqueeze(2).to_broadcast([P, H, HD]), ALU.mult)
                mm.then_inc(v_c.sem, 1)

            pool.wait_ge(f_e, 2)
            with pool.Fori(0, B) as b:
                batch(b)

        @block.tensor
        def _(pe):
            for s in (a_tr, a_u, c_mm, c_z, y_mm, s_mm, n_tr, q_mm, v_mm, d_mm, m_mm, m_t, h_mm, h_t, w_t,
                      e_mm, t_mm, o_mm, o_t, r_t, z_mm):
                pe.sem_inc(s.sem, s.credit)
            pe.wait_ge(ld_w, LOADED)
            pe.wait_ge(const, 13)

            pe.wait_ge(init, 1)
            for k in range(KT):
                mm = pe.matmul(PS[:, 7, 0:NP], ones[:, :], ptsq[:, k], start=(k == 0), stop=(k == KT - 1))
            mm.then_inc(pe_init, 1)

            with pe.Fori(0, B // 2) as g:
                for s in range(2):
                    pe.wait_ge(a_xn.sem, a_xn.at(g, s + 1))
                    for k in range(KT):
                        pe.wait_ge(a_xt.sem, a_xt.at(g, KT * s if s else 0))
                        for j in range(NT):
                            mm = pe.transpose(PS[:, k, j * P:(j + 1) * P], xnp[s][:, j, k * P:(k + 1) * P],
                                              ident[:, :])
                        mm.then_inc(a_tr.sem, 1)
                    pe.wait_ge(a_ue.sem, a_ue.at(g, s))
                    pe.wait_ge(a_xt.sem, a_xt.at(g, KT * (s + 1)))
                    for k in range(KT):
                        mm = pe.matmul(PS[ST:P, 2, :], w_in[:, k], xtp[s][:, k], start=(k == 0),
                                       stop=(k == KT - 1))
                    mm.then_inc(a_u.sem, 1)

            pe.wait_ge(init, 8)

            def half(b, n):
                work = []
                for z in range(3):
                    for m in range(KT):
                        o = PS[:, z, m * HALF:(m + 1) * HALF]
                        w = slice(m * P, (m + 1) * P)
                        for k in range(KT):
                            work.append((o, w_x[:, z, k, w], XB[:, n, k], k == 0, False, None, z, m))
                        for k in range(KT):
                            work.append((o, w_c[:, z, k, w], CT[:, k, n * HALF:(n + 1) * HALF], False,
                                         k == KT - 1, c_z if m == k == 1 else None, z, m))
                for m in range(KT):
                    for k in range(KT):
                        work.append((PS[:, 3, m * HALF:(m + 1) * HALF], w_gate[:, k, m * P:(m + 1) * P],
                                     XB[:, n, k], k == 0, k == 1, c_z if m == k == 1 else None, 3, m))
                for j in range(2):
                    for k in range(KT):
                        work.append((PS[:, 4, j * D:(j + 1) * D], XB[:, n, k, j * P:(j + 1) * P], w_wo[:, k],
                                     k == 0, k == 1, c_z if j == k == 1 else None, 4, j))
                assert len(work) == STEPS
                pe.wait_ge(c_u[n].sem, c_u[n].at(b, 1))
                pe.wait_ge(c_x[n].sem, c_x[n].at(b, 1))
                for s, (o, lhs, rhs, first, last, done, z, m) in enumerate(work):
                    step = n * STEPS + s
                    pe.wait_ge(c_h.sem, c_h.at(b, step))
                    pe.matmul(PS[0:ST, 7, 0:B], w_ab, HB[:, step], start=True, stop=True
                              ).then_inc(c_mm.sem, 1)
                    if m == 0 and first:
                        if z < 3:
                            pe.wait_ge(c_t.sem, c_t.at(b, 8 * n - 8 + 2 * z + 2))
                        elif z == 3:
                            pe.wait_ge(c_t.sem, c_t.at(b, 8 * n))
                        else:
                            pe.wait_ge(c_w.sem, c_w.at(b, n))
                    if z == 0 and m == 0 and not first and s == KT:
                        pe.wait_ge(c_c.sem, c_c.at(b, 4 * n - 4))
                    mm = pe.matmul(o, lhs, rhs, start=first, stop=last)
                    if done:
                        mm.then_inc(done.sem, 1)

            with pe.Fori(0, B) as b:
                half(b, 0)
                half(b, 1)

            pe.wait_ge(c_c.sem, 8 * B + c_c.credit)
            pe.wait_ge(c_t.sem, 16 * B + c_t.credit)
            for j in range(NT):
                for k in range(KT):
                    mm = pe.matmul(PS[:, j // 2, j % 2 * D:(j % 2 + 1) * D], CT[:, k, j * P:(j + 1) * P],
                                   w_uo[:, k], start=(k == 0), stop=(k == KT - 1))
            mm.then_inc(f_pe, 1)
            pe.wait_ge(f_e, 2)
            pe.wait_ge(c_hs.sem, 16 * (3 * B + 1))
            pe.wait_ge(f_set, 2)

            def tokens(bank, j):
                return PS[:, bank + j // 2, j % 2 * D:(j % 2 + 1) * D]

            def mix(b):
                pe.wait_ge(e_v.sem, e_v.at(b, 0))
                hu = HU[:, :].rearrange("p (t b) -> p b t", b=B)[:, bass.ds(b, 1)].rearrange("p o t -> p (o t)")
                for m in range(KT):
                    pe.matmul(PS[:, 6 + m, :], w_cd[:, m * P:(m + 1) * P], hu, start=True, stop=True
                              ).then_inc(y_mm.sem, 1)

            def leave(b, p):
                pe.wait_ge(y_v.sem, y_v.at(b, 3 * KT))
                for j in (2 * p, 2 * p + 1):
                    for k in range(KT):
                        mm = pe.matmul(tokens(6, j), YS[:, k, j * P:(j + 1) * P], w_out[:, k],
                                       start=(k == 0), stop=(k == KT - 1))
                mm.then_inc(s_mm.sem, 1)

            def normal_turn(b):
                pe.wait_ge(n_xn.sem, n_xn.at(b, NT))
                for k in range(KT):
                    for j in range(NT):
                        mm = pe.transpose(PS[:, 6 + k, j * P:(j + 1) * P], S1[:, j, k * P:(k + 1) * P],
                                          ident[:, :])
                    mm.then_inc(n_tr.sem, 1)

            def query_key(b, n):
                if n == 0:
                    pe.wait_ge(n_xt.sem, n_xt.at(b, KT))
                elif n > 1:
                    pe.wait_ge(q_e.sem, q_e.at(b, n - 1))
                for k in range(KT):
                    mm = pe.matmul(PS[:, 6 + n % 2, :], w_qk[:, n // 2, k, n % 2 * P:(n % 2 + 1) * P],
                                   XT1[:, k], start=(k == 0), stop=(k == KT - 1))
                mm.then_inc(q_mm.sem, 1)

            def value(b, p):
                pe.wait_ge(q_e.sem, q_e.at(b, 3 + p))
                for j in (2 * p, 2 * p + 1):
                    for k in range(KT):
                        mm = pe.matmul(tokens(6, j), XT1[:, k, j * P:(j + 1) * P], w_v[:, k],
                                       start=(k == 0), stop=(k == KT - 1))
                mm.then_inc(v_mm.sem, 1)

            def distance(b):
                pe.wait_ge(v_e.sem, v_e.at(b, 1))
                for j in range(NT):
                    for k in range(KT):
                        mm = pe.matmul(PS[:, 6, j * NP:(j + 1) * NP], XT1[:, k, j * P:(j + 1) * P],
                                       w_pt[:, k], start=(k == 0), stop=(k == KT - 1))
                mm.then_inc(d_mm.sem, 1)

            def low_rank(b, j):
                if j == 0:
                    pe.wait_ge(d_v.sem, d_v.at(b, 1))
                else:
                    pe.wait_ge(h_v.sem, h_v.at(b, j))
                for k in range(KT):
                    mm = pe.matmul(PS[:, 6, :], XT1[:, k, j * P:(j + 1) * P], w_b[:, k],
                                   start=(k == 0), stop=(k == KT - 1))
                mm.then_inc(h_mm.sem, 1)

            def low_rank_turn(b, j):
                if j == 0:
                    pe.wait_ge(v_e.sem, v_e.at(b, 2))
                else:
                    pe.wait_ge(h_e.sem, h_e.at(b, j))
                pe.wait_ge(h_v.sem, h_v.at(b, j + 1))
                for n in range(NR // P):
                    mm = pe.transpose(PS[:, 7, n * P:(n + 1) * P], HM[:, n * P:(n + 1) * P], ident[:, :])
                mm.then_inc(h_t.sem, 1)

            def weights_turn(b):
                pe.wait_ge(h_v.sem, h_v.at(b, NT))
                for j in range(NT):
                    mm = pe.transpose(PS[0:NP, 6, j * P:(j + 1) * P], wm[:, j], ident[:, :])
                mm.then_inc(w_t.sem, 1)

            def experts(b, p):
                if p == 0:
                    pe.wait_ge(h_e.sem, h_e.at(b, NT))
                pe.wait_ge(w_e.sem, w_e.at(b, 1))
                for j in (2 * p, 2 * p + 1):
                    o = PS[:, 7 - p, j % 2 * D:(j % 2 + 1) * D]
                    for n in range(NR // P):
                        pe.matmul(o, HMT[:, n, j * P:(j + 1) * P], w_a[:, n], start=(n == 0), stop=False)
                    mm = pe.matmul(o, wmt[:, j * P:(j + 1) * P], w_bias[:, :], start=False, stop=True)
                mm.then_inc(e_mm.sem, 1)

            def scores(b, u):
                hp, i = u // NT, u % NT
                if u >= 3:
                    pe.wait_ge(m_r.sem, m_r.at(b, u - 2))
                for e in range(2):
                    h = 2 * hp + e
                    bank = 2 * (u % 3) + e
                    pe.matmul(PS[:, bank, 0:(i + 1) * P], Q6[0:KS, h, i * P:(i + 1) * P],
                              K6[0:KS, h, 0:(i + 1) * P], start=True, stop=False)
                    mm = pe.matmul(PS[:, bank, i * P:(i + 1) * P], identb[:, :], negmask[:, :],
                                   start=False, stop=True)
                mm.then_inc(m_mm.sem, 1)

            def maxima_turn(b):
                pe.wait_ge(m_r.sem, m_r.at(b, NT * H // 2))
                for i in range(NT):
                    mm = pe.transpose(PS[0:H, 5, i * P:(i + 1) * P], nm[:, i], ident[:, :])
                mm.then_inc(m_t.sem, 1)

            def turned_tile(b, h, kt, bank, at):
                w = T - kt * P
                pe.matmul(PS[:, bank, at:at + w], K6[0:KM, h, kt * P:(kt + 1) * P],
                          Q6[0:KM, h, kt * P:T], start=True, stop=False)
                return pe.matmul(PS[:, bank, at:at + P], identb[:, :], negmask_t[:, :],
                                 start=False, stop=True)

            def turned_scores(b, h):
                unit = 3 * (h // 2) + 2 * (h % 2)
                base = 3 * (h % 2)
                if h >= 2:
                    pe.wait_ge(t_e.sem, t_e.at(b, unit - 2))
                for kt in (0, 1, 3):
                    mm = turned_tile(b, h, kt, base + P_AT[kt] // 512, P_AT[kt] % 512)
                mm.then_inc(t_mm.sem, 1)
                if h % 2 == 0:
                    if h >= 2:
                        pe.wait_ge(t_e.sem, t_e.at(b, unit - 1))
                    turned_tile(b, h, 2, 2, 0)
                    turned_tile(b, h + 1, 2, 2, 2 * P).then_inc(t_mm.sem, 1)

            def values(b, g):
                pe.wait_ge(t_e.sem, t_e.at(b, 6 * (g + 1)))
                if g == 0:
                    pe.wait_ge(m_h.sem, m_h.at(b, 2))
                    pe.wait_ge(v_c.sem, v_c.at(b, 1))
                else:
                    pe.wait_ge(o_v.sem, o_v.at(b, g))
                for kt in range(NT):
                    for j in range(4):
                        w = T - kt * P
                        at = P_AT[kt]
                        mm = pe.matmul(PS[32 * j:32 * j + 32, 5, kt * P:T], VA[:, kt, 4 * g + j],
                                       PR[:, g % 2, j, at:at + w],
                                       start=(kt == 0), stop=(kt == NT - 1))
                mm.then_inc(o_mm.sem, 1)

            def values_turn(b, g):
                pe.wait_ge(o_e.sem, o_e.at(b, g + 1))
                for j in range(NT):
                    mm = pe.transpose(PS[:, 5, j * P:(j + 1) * P], OS[:, j * P:(j + 1) * P], ident[:, :])
                mm.then_inc(o_t.sem, 1)

            def heads_turn(b):
                pe.wait_ge(o_v.sem, o_v.at(b, 4))
                pe.wait_ge(t_e.sem, t_e.at(b, TU))
                for k in range(KT):
                    for j in range(NT):
                        mm = pe.transpose(PS[:, k, j * P:(j + 1) * P], AT[:, j, k * P:(k + 1) * P], ident[:, :])
                    mm.then_inc(r_t.sem, 1)

            def project(b):
                pe.wait_ge(r_e.sem, r_e.at(b, KT))
                for j in range(NT):
                    for k in range(KT):
                        mm = pe.matmul(tokens(2, j), AO[:, k, j * P:(j + 1) * P], w_pr[:, k],
                                       start=(k == 0), stop=(k == KT - 1))
                    if j % 2:
                        mm.then_inc(z_mm.sem, 1)

            def run(steps, n):
                for step in steps.get(n, ()):
                    step()

            def batch(b, more):
                pe.wait_ge(q_ld.sem, q_ld.at(b, 2 * len(PAIRS)))
                pe.wait_ge(z_v.sem, z_v.at(b, 0))
                side = {3: [lambda: low_rank_turn(b, 2)], 4: [lambda: low_rank(b, 3)],
                        8: [lambda: low_rank_turn(b, 3), lambda: weights_turn(b)],
                        12: [lambda: experts(b, 0)], 15: [lambda: experts(b, 1)]}
                if more:
                    side[19] = [lambda: mix(b + 1)]
                    side[26] = [lambda: leave(b + 1, 0)]
                    side[27] = [lambda: leave(b + 1, 1)]
                for u in range(NT * H // 2):
                    scores(b, u)
                    run(side, u)
                maxima_turn(b)
                pe.wait_ge(m_ld.sem, m_ld.at(b, 2))
                side = {4: [lambda: values(b, 0)], 6: [lambda: values_turn(b, 0)],
                        8: [lambda: values(b, 1)], 10: [lambda: values_turn(b, 1)],
                        12: [lambda: values(b, 2)], 14: [lambda: values_turn(b, 2)]}
                if more:
                    side[5] = [lambda: normal_turn(b + 1)]
                    side[7] = [lambda: query_key(b + 1, 0), lambda: query_key(b + 1, 1)]
                    side[9] = [lambda: query_key(b + 1, 2), lambda: query_key(b + 1, 3)]
                    side[10] += [lambda: value(b + 1, 0)]
                    side[11] = [lambda: value(b + 1, 1), lambda: distance(b + 1)]
                for h in range(H):
                    turned_scores(b, h)
                    run(side, h)
                if more:
                    low_rank(b + 1, 0)
                values(b, 3)
                if more:
                    low_rank_turn(b + 1, 0)
                    low_rank(b + 1, 1)
                values_turn(b, 3)
                heads_turn(b)
                if more:
                    low_rank_turn(b + 1, 1)
                project(b)
                if more:
                    low_rank(b + 1, 2)

            mix(0)
            leave(0, 0)
            leave(0, 1)
            normal_turn(0)
            for n in range(4):
                query_key(0, n)
            value(0, 0)
            value(0, 1)
            distance(0)
            low_rank(0, 0)
            low_rank_turn(0, 0)
            low_rank(0, 1)
            low_rank_turn(0, 1)
            low_rank(0, 2)
            with pe.Fori(0, B - 1) as b:
                batch(b, True)
            batch(B - 1, False)

        @block.scalar
        def _(act):
            s_ = nc.scalar
            for s in (a_xt, c_h, c_t, g_t, n_x2, n_xt, q_e, d_e, h_e, e_t, t_e, o_e, r_e):
                act.sem_inc(s.sem, s.credit)
            act.wait_ge(ld_w, LOADED)
            s_.mul(b_z[:, 0:2], b_z[:, 0:2], 0.5).then_inc(act_init, 1)
            s_.mul(b_z[:, 3], b_z[:, 3], 0.5).then_inc(act_init, 1)
            act.wait_ge(act_init, 2)

            with act.Fori(0, B // 2) as g:
                for s in range(2):
                    act.wait_ge(a_ue.sem, a_ue.at(g, 0))
                    act.wait_ge(a_sv.sem, a_sv.at(g, 0))
                    for k in range(KT):
                        act.wait_ge(a_tr.sem, a_tr.at(g, KT * s + k + 1))
                        s_.copy(xtp[s][:, k], PS[:, k, :]).then_inc(a_xt.sem, 1)
            act.wait_ge(init, 8)

            tasks = {10: (0, 0), 12: (0, 1), 18: (1, 0), 20: (1, 1), 26: (2, 0), 28: (2, 1),
                     30: (3, 0), 31: (3, 1)}

            def half(b, n):
                for s in range(STEPS):
                    step = n * STEPS + s
                    act.wait_ge(c_mm.sem, c_mm.at(b, step + 1))
                    nxt = (step + 1) % (2 * STEPS)
                    if step == 0:
                        act.wait_ge(c_hs.sem, c_hs.at(b, 0))
                    s_.activation(HB[0:ST, nxt], PS[0:ST, 7, 0:B], ACT.Tanh).then_inc(c_h.sem, 1)
                    if s in tasks:
                        z, m = tasks[s]
                        if m == 0:
                            act.wait_ge(c_z.sem, c_z.at(b, 5 * n + z + 1))
                            if z < 3:
                                act.wait_ge(c_c.sem, c_c.at(b, 4 * n))
                            else:
                                act.wait_ge(c_gs.sem, c_gs.at(b, n))
                        dst = TG[:, z, m] if z < 3 else GS[:, m]
                        s_.activation(dst, PS[:, z, m * HALF:(m + 1) * HALF], ACT.Tanh,
                                      bias=b_z[:, z, m:m + 1], scale=(1.0 if z == 2 else 0.5)
                                      ).then_inc(c_t.sem, 1)

            with act.Fori(0, B) as b:
                half(b, 0)
                half(b, 1)
            act.wait_ge(c_h.sem, 2 * STEPS * B + 1)
            act.wait_ge(c_t.sem, 16 * B + c_t.credit)
            act.sem_inc(f_act, 1)

            def hidden(b):
                act.wait_ge(p_hq.sem, p_hq.at(b, 1))
                s_.activation(WX[:, :, :], WX[:, :, :], ACT.Tanh).then_inc(g_t.sem, 1)
                act.wait_ge(g_t.sem, g_t.at(b, 1))
                act.wait_ge(s_v.sem, s_v.at(b, 0))
                act.wait_ge(n_x2.sem, n_x2.at(b, 0))
                s_.activation(SG[:, :, :], WX[:, :, :], ACT.Tanh, scale=0.5).then_inc(g_t.sem, 1)

            def take_normal(b):
                for k in range(KT):
                    act.wait_ge(n_tr.sem, n_tr.at(b, k + 1))
                    s_.copy(XT1[:, k], PS[:, 6 + k, :]).then_inc(n_xt.sem, 1)

            def square(b):
                act.wait_ge(n_xn.sem, n_xn.at(b, NT))
                for j in range(NT):
                    s_.activation(SG[:, j], S1[:, j], ACT.Square, accum_out=x2[:, j:j + 1]
                                  ).then_inc(n_x2.sem, 1)

            def take_query_key(b, n):
                if n == 0:
                    act.wait_ge(z_mm.sem, z_mm.at(b, -2))
                act.wait_ge(q_mm.sem, q_mm.at(b, n + 1))
                s_.copy(QF[:, n], PS[:, 6 + n % 2, :]).then_inc(q_e.sem, 1)

            def second_odds(b):
                act.wait_ge(d_v.sem, d_v.at(b, 8))
                s_.activation(odds[:, :], odds[:, :], ACT.Exp, scale=ntemp[:, 0:1]).then_inc(d_e.sem, 1)

            def take_low_rank(b, j):
                act.wait_ge(h_t.sem, h_t.at(b, j + 1))
                s_.copy(HMT[:, :, j * P:(j + 1) * P],
                        PS[:, 7, :].rearrange("p (n q) -> p n q", q=P)).then_inc(h_e.sem, 1)

            def expert_gate(b, p):
                if p == 0:
                    act.wait_ge(z_o.sem, z_o.at(b, 0))
                act.wait_ge(e_mm.sem, e_mm.at(b, p + 1))
                s_.activation(SG2[:, 2 * p:2 * p + 2], PS[:, 7 - p, :].rearrange("p (j d) -> p j d", d=D),
                              ACT.Tanh, scale=0.5).then_inc(e_t.sem, 1)

            def exp(b, h):
                if h % 4 == 0:
                    act.wait_ge(o_mm.sem, o_mm.at(b, h // 4 - 1 if h >= 8 else 0))
                unit = 3 * (h // 2) + h % 2
                act.wait_ge(t_mm.sem, t_mm.at(b, unit + 1))
                if h % 2:
                    s_.activation(PR[:, h // 4 % 2, h % 4 - 1:h % 4 + 1, PU:PW],
                                  PS[:, 2, :].rearrange("p (a b) -> p a b", a=2),
                                  ACT.Exp, scale=SCORE_SCALE).then_inc(t_e.sem, 1)
                    act.wait_ge(t_mm.sem, t_mm.at(b, unit + 2))
                base = 3 * (h % 2)
                s_.activation(PR[:, h // 4 % 2, h % 4, 0:PU],
                              PS[:, base:base + 2, :].rearrange("p a b -> p (a b)"),
                              ACT.Exp, scale=SCORE_SCALE).then_inc(t_e.sem, 1)

            def take_values(b, g):
                act.wait_ge(o_mm.sem, o_mm.at(b, g + 1))
                act.wait_ge(o_t.sem, o_t.at(b, g))
                s_.copy(OS[:, :], PS[:, 5, :]).then_inc(o_e.sem, 1)

            def take_heads(b):
                for k in range(KT):
                    act.wait_ge(r_t.sem, r_t.at(b, k + 1))
                    s_.copy(AO[:, k], PS[:, k, :]).then_inc(r_e.sem, 1)

            def run(steps, n):
                for step in steps.get(n, ()):
                    step()

            def batch(b, more):
                take_low_rank(b, 2)
                take_low_rank(b, 3)
                expert_gate(b, 0)
                expert_gate(b, 1)
                if more:
                    hidden(b + 1)
                side = {4: [lambda: take_values(b, 0)], 8: [lambda: take_values(b, 1)],
                        12: [lambda: take_values(b, 2)]}
                if more:
                    side[5] = [lambda: take_normal(b + 1)]
                    side[7] = [lambda: take_query_key(b + 1, 0), lambda: take_query_key(b + 1, 1)]
                    side[8] += [lambda: square(b + 1)]
                    side[9] = [lambda: take_query_key(b + 1, 2), lambda: take_query_key(b + 1, 3)]
                    side[15] = [lambda: second_odds(b + 1)]
                for h in range(H):
                    exp(b, h)
                    run(side, h)
                take_values(b, 3)
                if more:
                    take_low_rank(b + 1, 0)
                take_heads(b)
                if more:
                    take_low_rank(b + 1, 1)

            hidden(0)
            take_normal(0)
            square(0)
            for n in range(4):
                take_query_key(0, n)
            second_odds(0)
            take_low_rank(0, 0)
            take_low_rank(0, 1)
            with act.Fori(0, B - 1) as b:
                batch(b, True)
            batch(B - 1, False)

        @block.vector
        def _(dve):
            v_ = nc.vector
            for s in (a_st, a_xn, a_ue, c_w, c_c, y_v, s_v, n_st, n_xn, q_s, v_e, d_v, d_m, m_r, m_h, h_v,
                      w_e, e_v, o_r, o_v, z_v):
                dve.sem_inc(s.sem, s.credit)

            def hold():
                v_.memset(scratch[:, :], 0.0)

            dve.wait_ge(ld_w, LOADED)
            v_.tensor_tensor(ptsq, w_pt[:, :, :], w_pt[:, :, :], ALU.mult).then_inc(init, 1)
            v_.scalar_tensor_tensor(out=atemp[:, :], in0=ntemp[:, :], scalar=-1.0, in1=ntemp[:, :],
                                    op0=ALU.mult, op1=ALU.max).then_inc(temps, 1)
            dve.wait_ge(temps, 1)
            v_.tensor_scalar(ntemp[:, :], atemp[:, :], 0.1, None, ALU.max).then_inc(init, 1)
            dve.wait_ge(init, 2)
            v_.reciprocal(ntemp[:, :], ntemp[:, :]).then_inc(init, 1)
            dve.wait_ge(init, 3)
            v_.tensor_scalar(ntemp[:, :], ntemp[:, :], -1.0, None, ALU.mult).then_inc(init, 1)
            dve.wait_ge(pe_init, 1)
            v_.tensor_copy(p2[:, :], PS[:, 7, 0:NP]).then_inc(init, 1)
            v_.memset(HB[0:ST, 0], 0.0).then_inc(init, 1)
            v_.memset(K6[KS:P, :, :], 1.0).then_inc(init, 1)
            v_.tensor_copy(CT, c0.unsqueeze(2).to_broadcast([P, KT, T])).then_inc(init, 1)

            def statistics(x, st, b, base):
                for j in range(NT):
                    v_.bn_stats(bnst[:, j], x[:, j]).then_inc(st.sem, 1)
                dve.wait_ge(st.sem, st.at(b, base + NT))
                hold()
                for j in range(NT):
                    v_.bn_aggr(mv[:, j], bnst[:, j]).then_inc(st.sem, 1)

            with dve.Fori(0, B // 2) as g:
                for s in range(2):
                    dve.wait_ge(a_x[s].sem, a_x[s].at(g, 1))
                    statistics(xin[s][:, :, :], a_st, g, 2 * NT * s)
                    dve.wait_ge(a_rs.sem, a_rs.at(g, 2 * (s + 1)))
                    dve.wait_ge(a_sv.sem, a_sv.at(g, 0))
                    for j in range(NT):
                        mm = v_.tensor_scalar(xnp[s][:, j], xin[s][:, j], mv[:, j, 0:1], rst[:, j:j + 1],
                                              ALU.subtract, ALU.mult)
                    mm.then_inc(a_xn.sem, 1)
                    dve.wait_ge(a_u.sem, a_u.at(g, s + 1))
                    v_.tensor_scalar(HU[ST:P, :].rearrange("p (t b) -> p b t", b=B)
                                     [:, bass.ds(g * 2 + s, 1)].rearrange("p o t -> p (o t)"),
                                     PS[ST:P, 2, :], b_in[ST:P, 0:1], None, ALU.add).then_inc(a_ue.sem, 1)

            def half(b, n):
                c = CT[:, :, n * HALF:(n + 1) * HALF]
                dve.wait_ge(c_t.sem, c_t.at(b, 8 * n + 6))
                v_.scalar_tensor_tensor(out=c, in0=TG[:, 0], scalar=1.0, in1=c, op0=ALU.add, op1=ALU.mult
                                        ).then_inc(c_c.sem, 1)
                v_.scalar_tensor_tensor(out=CA, in0=TG[:, 1], scalar=1.0, in1=TG[:, 2], op0=ALU.add,
                                        op1=ALU.mult).then_inc(c_c.sem, 1)
                dve.wait_ge(c_c.sem, c_c.at(b, 4 * n + 2))
                v_.tensor_tensor(c, c, CA, ALU.add).then_inc(c_c.sem, 1)
                dve.wait_ge(c_c.sem, c_c.at(b, 4 * n + 3))
                v_.tensor_scalar(c, c, 0.5, None, ALU.mult).then_inc(c_c.sem, 1)
                dve.wait_ge(c_z.sem, c_z.at(b, 5 * n + 5))
                dve.wait_ge(c_ws.sem, c_ws.at(b, n))
                v_.tensor_copy(WS, PS[:, 4, :].rearrange("p (j d) -> p j d", d=D)).then_inc(c_w.sem, 1)

            with dve.Fori(0, B) as b:
                half(b, 0)
                half(b, 1)

            dve.wait_ge(f_pe, 1)
            for n in range(2):
                v_.tensor_tensor(UC[:, 2 * n:2 * n + 2], PS[:, n, :].rearrange("p (j d) -> p j d", d=D),
                                 bo[:, :].unsqueeze(1).to_broadcast([P, 2, D]), ALU.add).then_inc(f_e, 1)

            def mix(b):
                dve.wait_ge(l_xt.sem, l_xt.at(b, 1))
                dve.wait_ge(l_gt.sem, l_gt.at(b, 1))
                dve.wait_ge(v_c.sem, v_c.at(b, 0))
                for m in range(KT):
                    dve.wait_ge(y_mm.sem, y_mm.at(b, m + 1))
                    v_.tensor_tensor(YS[:, m], PS[:, 6 + m, :], XT[:, m], ALU.subtract).then_inc(y_v.sem, 1)
                dve.wait_ge(y_v.sem, y_v.at(b, KT))
                for m in range(KT):
                    v_.scalar_tensor_tensor(out=YS[:, m], in0=GT[:, m], scalar=1.0, in1=YS[:, m],
                                            op0=ALU.add, op1=ALU.mult).then_inc(y_v.sem, 1)
                dve.wait_ge(y_v.sem, y_v.at(b, 2 * KT))
                for m in range(KT):
                    v_.scalar_tensor_tensor(out=YS[:, m], in0=YS[:, m], scalar=0.5, in1=XT[:, m],
                                            op0=ALU.mult, op1=ALU.add).then_inc(y_v.sem, 1)

            def leave(b):
                dve.wait_ge(p_xn.sem, p_xn.at(b, 1))
                for p in range(2):
                    dve.wait_ge(s_mm.sem, s_mm.at(b, p + 1))
                    v_.tensor_tensor(S1[:, 2 * p:2 * p + 2], PS[:, 6 + p, :].rearrange("p (j d) -> p j d", d=D),
                                     XNB[:, 2 * p:2 * p + 2], ALU.add).then_inc(s_v.sem, 1)
                dve.wait_ge(p_sg.sem, p_sg.at(b, 2))
                dve.wait_ge(s_v.sem, s_v.at(b, 2))
                for p in range(2):
                    v_.tensor_tensor(S1[:, 2 * p:2 * p + 2], S1[:, 2 * p:2 * p + 2], SG[:, 2 * p:2 * p + 2],
                                     ALU.mult).then_inc(s_v.sem, 1)
                dve.wait_ge(l_x.sem, l_x.at(b, 1))
                dve.wait_ge(s_v.sem, s_v.at(b, 4))
                for p in range(2):
                    v_.scalar_tensor_tensor(out=X1[:, 2 * p:2 * p + 2], in0=S1[:, 2 * p:2 * p + 2], scalar=0.5,
                                            in1=X1[:, 2 * p:2 * p + 2], op0=ALU.mult, op1=ALU.add
                                            ).then_inc(s_v.sem, 1)
                dve.wait_ge(s_v.sem, s_v.at(b, 6))
                statistics(X1, n_st, b, 0)

            def normalise(b):
                dve.wait_ge(n_rs.sem, n_rs.at(b, 2))
                for j in range(NT):
                    v_.tensor_scalar(S1[:, j], X1[:, j], mv[:, j, 0:1], rst[:, j:j + 1], ALU.subtract,
                                     ALU.mult).then_inc(n_xn.sem, 1)

            def split(b, n):
                if n == 0:
                    dve.wait_ge(q_e.sem, q_e.at(b, 4))
                    dve.wait_ge(q_st.sem, q_st.at(b, 0))
                else:
                    dve.wait_ge(q_r.sem, q_r.at(b, n))
                v_.tensor_copy(QB[:, n], QF[:, :, :]).then_inc(q_s.sem, 1)

            def value(b, p):
                dve.wait_ge(v_mm.sem, v_mm.at(b, p + 1))
                v_.tensor_copy(V1[:, 2 * p:2 * p + 2], PS[:, 6 + p, :].rearrange("p (j d) -> p j d", d=D)
                               ).then_inc(v_e.sem, 1)

            def distance(b):
                dve.wait_ge(d_mm.sem, d_mm.at(b, 1))
                v_.scalar_tensor_tensor(out=dst[:, :, :],
                                        in0=PS[:, 6, 0:NT * NP].rearrange("p (j n) -> p j n", n=NP),
                                        scalar=2.0, in1=p2[:, :].unsqueeze(1).to_broadcast([P, NT, NP]),
                                        op0=ALU.mult, op1=ALU.subtract).then_inc(d_v.sem, 1)
                dve.wait_ge(d_v.sem, d_v.at(b, 1))
                dve.wait_ge(n_x2.sem, n_x2.at(b, NT))
                v_.tensor_tensor(dst[:, :, :], dst[:, :, :],
                                 x2[:, :].unsqueeze(2).to_broadcast([P, NT, NP]), ALU.subtract
                                 ).then_inc(d_v.sem, 1)
                dve.wait_ge(d_v.sem, d_v.at(b, 2))
                v_.tensor_scalar(dst[:, :, :], dst[:, :, :], 0.0, None, ALU.min).then_inc(d_v.sem, 1)
                dve.wait_ge(d_v.sem, d_v.at(b, 3))
                hold()
                for j in range(NT):
                    v_.max(top[:, j], dst[:, j]).then_inc(d_m.sem, 1)
                dve.wait_ge(d_m.sem, d_m.at(b, NT))
                hold()
                for j in range(NT):
                    v_.max_index(topi[:, j], top[:, j], dst[:, j]).then_inc(d_m.sem, 1)
                dve.wait_ge(d_m.sem, d_m.at(b, 2 * NT))
                v_.tensor_copy(topf[:, :, :], topi[:, :, 0:2]).then_inc(d_v.sem, 1)
                v_.tensor_scalar(near[:, :, :], top[:, :, 0:2], -1.0, None, ALU.mult).then_inc(d_v.sem, 1)
                dve.wait_ge(d_v.sem, d_v.at(b, 5))
                for n, chosen in enumerate((hit, wm)):
                    v_.tensor_tensor(chosen[:, :, :], iota[:, :].unsqueeze(1).to_broadcast([P, NT, NP]),
                                     topf[:, :, n:n + 1].to_broadcast([P, NT, NP]), ALU.is_equal
                                     ).then_inc(d_v.sem, 1)

            def odds_apart(b):
                dve.wait_ge(d_p.sem, d_p.at(b, 1))
                v_.tensor_tensor(odds[:, :], near[:, :, 1], near[:, :, 0], ALU.subtract).then_inc(d_v.sem, 1)

            def choose(b):
                dve.wait_ge(d_e.sem, d_e.at(b, 1))
                v_.tensor_scalar(rden[:, :], odds[:, :], 1.0, None, ALU.add).then_inc(d_v.sem, 1)
                dve.wait_ge(d_v.sem, d_v.at(b, 9))
                v_.reciprocal(rden[:, :], rden[:, :]).then_inc(d_v.sem, 1)
                dve.wait_ge(d_v.sem, d_v.at(b, 10))
                v_.tensor_tensor(odds[:, :], odds[:, :], rden[:, :], ALU.mult).then_inc(d_v.sem, 1)
                dve.wait_ge(d_v.sem, d_v.at(b, 11))
                for weight, chosen in ((rden, hit), (odds, wm)):
                    v_.tensor_tensor(chosen[:, :, :], chosen[:, :, :],
                                     weight[:, :].unsqueeze(2).to_broadcast([P, NT, NP]), ALU.mult
                                     ).then_inc(d_v.sem, 1)
                dve.wait_ge(d_v.sem, d_v.at(b, 13))
                v_.tensor_tensor(wm[:, :, :], wm[:, :, :], hit[:, :, :], ALU.add).then_inc(d_v.sem, 1)

            def weigh(b, j):
                dve.wait_ge(h_mm.sem, h_mm.at(b, j + 1))
                dve.wait_ge(d_v.sem, d_v.at(b, 14))
                dve.wait_ge(h_t.sem, h_t.at(b, j))
                v_.tensor_tensor(HM.rearrange("p (n r) -> p n r", r=RANK),
                                 PS[:, 6, :].rearrange("p (n r) -> p n r", r=RANK),
                                 wm[:, j].unsqueeze(2).to_broadcast([P, NP, RANK]), ALU.mult
                                 ).then_inc(h_v.sem, 1)

            def take_weights(b):
                dve.wait_ge(w_t.sem, w_t.at(b, 1))
                v_.tensor_copy(wmt[:, :], PS[0:NP, 6, :]).then_inc(w_e.sem, 1)

            def gate(b, p):
                dve.wait_ge(e_t.sem, e_t.at(b, p + 1))
                v_.scalar_tensor_tensor(out=SG2[:, 2 * p:2 * p + 2], in0=SG2[:, 2 * p:2 * p + 2],
                                        scalar=1.0, in1=PS[:, 7 - p, :].rearrange("p (j d) -> p j d", d=D),
                                        op0=ALU.add, op1=ALU.mult).then_inc(e_v.sem, 1)

            def maxima(b, u):
                hp, i = u // NT, u % NT
                dve.wait_ge(m_mm.sem, m_mm.at(b, u + 1))
                v_.tensor_reduce(nm[:, i, 2 * hp:2 * hp + 2],
                                 PS[:, 2 * (u % 3):2 * (u % 3) + 2, 0:(i + 1) * P], AX.X, ALU.max,
                                 negate=True).then_inc(m_r.sem, 1)

            def maxima_rows(b):
                dve.wait_ge(m_t.sem, m_t.at(b, 1))
                v_.tensor_copy(nmh[:, :], PS[0:H, 5, :]).then_inc(m_h.sem, 1)
                dve.wait_ge(m_h.sem, m_h.at(b, 1))
                v_.tensor_tensor(nml[:, :], PS[0:H, 5, :], nmh[:, :], ALU.subtract).then_inc(m_h.sem, 1)

            def divide(b, g):
                dve.wait_ge(o_t.sem, o_t.at(b, g + 1))
                o = PS[:, 5, :].rearrange("p (j n d) -> p j n d", n=4, d=32)
                v_.reciprocal(rec[:, :, :], o[:, :, :, HD]).then_inc(o_r.sem, 1)
                dve.wait_ge(o_r.sem, o_r.at(b, g + 1))
                v_.tensor_tensor(AT[:, :, g * 64:(g + 1) * 64].rearrange("p j (n d) -> p j n d", d=HD),
                                 o[:, :, :, 0:HD], rec[:, :, :].unsqueeze(3).to_broadcast([P, NT, 4, HD]),
                                 ALU.mult).then_inc(o_v.sem, 1)

            def finish(b):
                for p in range(2):
                    dve.wait_ge(z_mm.sem, z_mm.at(b, p + 1))
                    v_.tensor_tensor(SG2[:, 2 * p:2 * p + 2], PS[:, 2 + p, :].rearrange("p (j d) -> p j d", d=D),
                                     SG2[:, 2 * p:2 * p + 2], ALU.mult).then_inc(z_v.sem, 1)
                dve.wait_ge(x_ld.sem, x_ld.at(b, 1))
                dve.wait_ge(z_v.sem, z_v.at(b, 2))
                for p in range(2):
                    v_.scalar_tensor_tensor(out=SG2[:, 2 * p:2 * p + 2], in0=SG2[:, 2 * p:2 * p + 2],
                                            scalar=0.5 * OUT_SCALE, in1=S1[:, 2 * p:2 * p + 2],
                                            op0=ALU.mult, op1=ALU.add).then_inc(z_v.sem, 1)

            def batch(b, more):
                side = {5: lambda: weigh(b, 3), 10: lambda: take_weights(b), 14: lambda: gate(b, 0),
                        17: lambda: gate(b, 1)}
                if more:
                    side[21] = lambda: mix(b + 1)
                    side[30] = lambda: leave(b + 1)
                for u in range(NT * H // 2):
                    maxima(b, u)
                    if u in side:
                        side[u]()
                maxima_rows(b)
                if more:
                    normalise(b + 1)
                divide(b, 0)
                if more:
                    split(b + 1, 0)
                divide(b, 1)
                if more:
                    value(b + 1, 0)
                    value(b + 1, 1)
                    distance(b + 1)
                    split(b + 1, 1)
                    odds_apart(b + 1)
                divide(b, 2)
                if more:
                    split(b + 1, 2)
                    choose(b + 1)
                    weigh(b + 1, 0)
                    weigh(b + 1, 1)
                divide(b, 3)
                finish(b)
                if more:
                    weigh(b + 1, 2)

            mix(0)
            leave(0)
            normalise(0)
            split(0, 0)
            value(0, 0)
            value(0, 1)
            distance(0)
            split(0, 1)
            odds_apart(0)
            split(0, 2)
            choose(0)
            for j in range(3):
                weigh(0, j)
            with dve.Fori(0, B - 1) as b:
                batch(b, True)
            batch(B - 1, False)


_SHAPE = ((B, T, D), "float32")


def _layout(inputs):
    import numpy as np

    def c(x):
        return np.ascontiguousarray(x)

    i = {k: np.asarray(v) for k, v in inputs.items()}
    f, s = "L0_ffn_", "L0_attn_"
    w = {"L0_attn_x": c(i["L0_attn_x"]), "W_in": c(i[s + "W_in"]), "W_gate": c(i[s + "W_gate"]),
         "A": c(i[s + "A"]), "Bm": c(i[s + "Bm"]), "CT": c(i[s + "C"].T), "DT": c(i[s + "D"].T),
         "W_out": c(i[s + "W_out"]), "b_in": c(i[s + "b_in"]), "b_gate": c(i[s + "b_gate"]),
         "b_out": c(i[s + "b_out"])}
    for n in ("wf", "uf", "wi", "ui", "wc", "uc", "wo", "uo"):
        w[n + "T"] = c(i[f + n].T)
    w["bo"] = c(i[f + "bo"])
    w["b_gate"] = c(w["b_gate"].reshape(KT, P).T)
    for n in ("bf", "bi", "bc", "in_c"):
        w[n] = c(i[f + n].reshape(KT, P).T)
    for n, m in (("WqT", "W_query"), ("WkT", "W_key"), ("WvT", "W_value"), ("WpT", "W_proj")):
        w[n] = c(i["L1_attn_" + m].T)
    w["BT"] = c(i["L1_ffn_B"].reshape(NR, D).T)
    w["AT"] = c(i["L1_ffn_A"].transpose(0, 2, 1).reshape(NR, D))
    w["protoT"] = c(i["L1_ffn_prototypes"].T)
    w["bias"] = c(i["L1_ffn_bias"])
    w["temp"] = c(i["L1_ffn_temp"].reshape(1))
    return w


def kernel(**inputs):
    import concourse.bacc as bacc
    from concourse.bass_utils import run_bass_kernel_spmd

    nc = bacc.Bacc("TRN2", target_bir_lowering=False, num_devices=1)
    arrays = {}
    aps = {}
    for name, x in _layout(inputs).items():
        arrays[f"in_{name}"] = x
        aps[name] = nc.dram_tensor(f"in_{name}", x.shape, mybir.dt.from_np(x.dtype), kind="ExternalInput").ap()
    out = nc.dram_tensor("out_0", _SHAPE[0], F32, kind="ExternalOutput").ap()
    two_layers(nc, aps, out)
    r = run_bass_kernel_spmd(nc, [arrays], core_ids=[0])
    return r.results[0]["out_0"]
```

```python
from contextlib import ExitStack

import concourse.bass as bass
from concourse import mybir

F32 = mybir.dt.float32
BF16 = mybir.dt.bfloat16
U32 = mybir.dt.uint32
ALU = mybir.AluOpType
ACT = mybir.ActivationFunctionType
AX = mybir.AxisListType

B, T, D = 8, 512, 256
ST = 64
P = 128
KT = D // P
NT = T // P
H, HD = 16, 16
NP, RANK = 32, 16
NR = NP * RANK
HALF = T // 2
STEPS = T // B // 2
EPS = 1e-5
SPLIT = 3
PAIRS = [(0, 0), (0, 1), (1, 0), (0, 2), (2, 0), (1, 1)]
KS = len(PAIRS) * HD
KM = KS + 2
SCORE_SCALE = float(D) ** -1.0 * float(HD) ** -0.5
OUT_SCALE = float(D) ** -0.5
P_AT = {0: 0, 1: 512, 3: 896, 2: 1024}
PU = P_AT[2]
TU = 3 * H // 2
PW = NT * (NT + 1) // 2 * P
BIG = 1.0e30


class Count:

    def __init__(self, handle, per, step=1, credit=1):
        self.sem, self.per, self.step, self.credit = handle, per, step, credit

    def at(self, it, n):
        return it * (self.per * self.step) + (n * self.step + self.credit)


def two_layers(nc, a, out):
    ctx = ExitStack()
    with ctx:
        def sb(name, shape, dt=F32):
            return ctx.enter_context(nc.sbuf_tensor(name, shape, dt))

        def sem(name):
            return ctx.enter_context(nc.semaphore(name))

        def count(name, per, credit=1):
            return Count(sem(name), per, credit=credit)

        def dcount(name, per):
            return Count(sem(name), per, step=16, credit=16)

        xt_d = nc.dram_tensor("xt_d", (B, P, KT, T), F32, kind="Internal").ap()
        st_d = nc.dram_tensor("st_d", (B, P, 2, NT), F32, kind="Internal").ap()
        gt_d = nc.dram_tensor("gt_d", (B, P, KT, T), F32, kind="Internal").ap()
        wx_d = nc.dram_tensor("wx_d", (B, P, NT, D), F32, kind="Internal").ap()
        x1_d = nc.dram_tensor("x1_d", (B, P, NT, D), F32, kind="Internal").ap()
        qk_d = nc.dram_tensor("qk_d", (SPLIT, 2, D, T), BF16, kind="Internal").ap()

        HU = sb("HU", [P, T * B])
        w_cd = sb("w_cd", [P, D])
        w_out = sb("w_out", [P, KT, D])
        w_qk = sb("w_qk", [P, 2, KT, D])
        w_v = sb("w_v", [P, KT, D])
        w_pr = sb("w_pr", [P, KT, D])
        w_b = sb("w_b", [P, KT, NR])
        w_a = sb("w_a", [P, NR // P, D])
        w_pt = sb("w_pt", [P, KT, NP])
        w_bias = sb("w_bias", [NP, D])
        ident = sb("ident", [P, P])
        identb = sb("identb", [P, P], BF16)
        negmask = sb("negmask", [P, P], BF16)
        negmask_t = sb("negmask_t", [P, P], BF16)
        halves = sb("halves", [P, 2 * NT])
        mhalf = sb("mhalf", [P, NT])
        vscale = sb("vscale", [P, H])
        eps = sb("eps", [P, NT])
        iota = sb("iota", [P, NP])
        ones = sb("ones", [P, P])
        p2 = sb("p2", [P, NP])
        ntemp = sb("ntemp", [P, 1])
        atemp = sb("atemp", [P, 1])
        bout = sb("bout", [P, D])
        bo = sb("bo", [P, D])
        UC = sb("UC", [P, NT, D])
        scratch = sb("scratch", [P, 1])
        Q6 = sb("Q6", [P, H, T], BF16)
        K6 = sb("K6", [P, H, T], BF16)
        XT = sb("XT", [P, KT, T])
        GT = sb("GT", [P, KT, T])
        WX = sb("WX", [P, NT, D])
        X1 = sb("X1", [P, NT, D])
        XNB = sb("XNB", [P, NT, D])
        YS = sb("YS", [P, KT, T])
        SG = sb("SG", [P, NT, D])
        S1 = sb("S1", [P, NT, D])
        XT1 = sb("XT1", [P, KT, T])
        QF = sb("QF", [P, 2 * KT, T])
        QB = sb("QB", [P, SPLIT, 2 * KT, T], BF16)
        OS = sb("OS", [P, T])
        SG2 = sb("SG2", [P, NT, D])
        sst = sb("sst", [P, 2, 2, NT])
        stb = sb("stb", [P, 2, NT])
        amv = sb("amv", [P, 2, NT, 2])
        abn = sb("abn", [P, 2, NT, 6])
        minus = sb("minus", [P, NT])
        bnst = sb("bnst", [P, NT, 6])
        mv = sb("mv", [P, NT, 2])
        rst = sb("rst", [P, NT])
        mrs = sb("mrs", [P, NT])
        half1 = sb("half1", [P, 1])
        x2 = sb("x2", [P, NT])
        dst = sb("dst", [P, NT, NP])
        top = sb("top", [P, NT, 8])
        topi = sb("topi", [P, NT, 8], U32)
        topf = sb("topf", [P, NT, 2])
        near = sb("near", [P, NT, 2])
        odds = sb("odds", [P, NT])
        hit = sb("hit", [P, NT, NP])
        wm = sb("wm", [P, NT, NP])
        rden = sb("rden", [P, NT])
        wmt = sb("wmt", [NP, T])
        nm = sb("nm", [P, NT, H])
        nmh = sb("nmh", [H // 2, 2, T], BF16)
        nml = sb("nml", [H // 2, 2, T], BF16)
        rec = sb("rec", [P, NT, NT])
        ARENA = 2 * 4 * PW + NR // P * T + T + NT * H * 32
        arena = sb("arena", [P, ARENA])
        used = [0]

        def part(*shape):
            n = 1
            for s in shape:
                n *= s
            v = arena[:, used[0]:used[0] + n]
            used[0] += n
            assert used[0] <= ARENA
            if len(shape) == 1:
                return v
            names = "abcd"[:len(shape)]
            return v.rearrange(f"p ({' '.join(names)}) -> p {' '.join(names)}",
                               **{k: s for k, s in zip(names, shape)})

        w_in = part(KT, ST)
        w_ab = part(ST)
        w_gate = part(KT, D)
        w_x = part(3, KT, D)
        w_c = part(3, KT, D)
        w_wo = part(KT, D)
        w_uo = part(KT, D)
        b_in = part(1)
        b_z = part(4, KT)
        HB = part(2 * STEPS, B)
        XB = part(2, KT, HALF)
        CT = part(KT, T)
        c0 = part(KT)
        TG = part(3, KT, HALF)
        GS = part(KT, HALF)
        WS = part(2, D)
        CA = part(KT, HALF)
        xin, xnp, xtp = (X1, SG2), (SG, S1), (XT1, YS)
        ptsq = SG2[:, 0, 0:KT * NP].rearrange("p (a b) -> p a b", b=NP)
        used[0] = 0
        PR = part(2, 4, PW)
        HMT = part(NR // P, T)
        HM = part(T)
        VA = part(NT, H, 32)
        AT = GT[:, :, :].rearrange("p a b -> p (a b)").rearrange("p (t o) -> p t o", t=NT)
        V1 = YS[:, :, :].rearrange("p a b -> p (a b)").rearrange("p (t o) -> p t o", t=NT)
        AO = QF[:, 0:KT, :]

        PS = ctx.enter_context(nc.psum_tensor("PS", [P, 8, 512], F32))

        ld_in = sem("ld_in")
        ld_w = sem("ld_w")
        ld_b = sem("ld_b")
        const = sem("const")
        init = sem("init")
        temps = sem("temps")
        act_init = sem("act_init")
        carried = sem("carried")
        a_x = [dcount(f"a_x{s}", 1) for s in range(2)]
        a_st = count("a_st", 2 * (NT + NT))
        a_rs = count("a_rs", 2 * 2)
        a_mr = count("a_mr", 2 * 2)
        a_xn = count("a_xn", 2)
        a_tr = count("a_tr", 2 * KT)
        a_xt = count("a_xt", 2 * KT)
        a_u = count("a_u", 2)
        a_ue = count("a_ue", 2)
        a_sx = [dcount(f"a_sx{s}", 1) for s in range(2)]
        a_ss = [dcount(f"a_ss{s}", 1) for s in range(2)]
        c_x = [dcount(f"c_x{n}", 1) for n in range(2)]
        c_u = [dcount(f"c_u{n}", 1) for n in range(2)]
        c_mm = count("c_mm", 2 * STEPS)
        c_h = count("c_h", 2 * STEPS)
        c_z = count("c_z", 2 * 5)
        c_t = count("c_t", 2 * 8, 7)
        c_w = count("c_w", 2)
        c_c = count("c_c", 2 * 4, 5)
        c_hs = [dcount(f"c_hs{n}", n + 1) for n in range(2)]
        c_gs = dcount("c_gs", 2)
        c_ws = dcount("c_ws", 2)
        f_p2 = sem("f_p2")
        f_e = sem("f_e")
        f_pe = sem("f_pe")
        f_act = sem("f_act")
        f_set = sem("f_set")
        l_xt, l_gt, l_wx, l_x, l_st = (dcount(n, 1) for n in ("l_xt", "l_gt", "l_wx", "l_x", "l_st"))
        x_n = count("x_n", NT)
        y_mm = count("y_mm", KT)
        y_v = count("y_v", KT)
        y_p = count("y_p", 3)
        g_h = count("g_h", 1)
        p_xn = count("p_xn", 1)
        p_hq = count("p_hq", 1)
        g_t = count("g_t", 3)
        p_sg = count("p_sg", 1)
        s_mm = count("s_mm", 2)
        s_v = count("s_v", 2)
        s_p = count("s_p", 3)
        n_st = count("n_st", 2 * NT)
        n_rs = count("n_rs", 2)
        n_mr = count("n_mr", 2)
        n_xn = count("n_xn", NT)
        n_x2 = count("n_x2", NT)
        n_tr = count("n_tr", KT)
        n_xt = count("n_xt", KT)
        q_mm = count("q_mm", 4)
        q_e = count("q_e", 4)
        q_s = count("q_s", 2 * SPLIT)
        q_d = count("q_d", 2)
        q_r = count("q_r", 2)
        q_st = dcount("q_st", SPLIT)
        x_sv = dcount("x_sv", 1)
        x_ld = dcount("x_ld", 1)
        q_ld = dcount("q_ld", 2 * len(PAIRS))
        v_mm = count("v_mm", 2)
        v_e = count("v_e", 2)
        v_c = count("v_c", 1)
        d_mm = count("d_mm", 1)
        d_v = count("d_v", 14)
        d_p = count("d_p", 1)
        d_e = count("d_e", 1)
        d_m = count("d_m", 2 * NT)
        m_mm = count("m_mm", NT * H // 2)
        m_r = count("m_r", NT * H // 2)
        m_t = count("m_t", 2)
        m_a = count("m_a", 2)
        m_h = count("m_h", 2, 2)
        m_ld = [dcount(f"m_ld{n}", 2) for n in range(2)]
        h_mm = count("h_mm", NT)
        h_v = count("h_v", NT)
        h_t = count("h_t", NT)
        h_e = count("h_e", NT)
        w_t = count("w_t", 1)
        w_e = count("w_e", 1)
        e_mm = count("e_mm", 2)
        e_t = count("e_t", 2)
        e_v = count("e_v", 2)
        t_mm = count("t_mm", TU)
        t_e = count("t_e", TU)
        o_mm = count("o_mm", 4)
        o_e = count("o_e", 4)
        o_t = count("o_t", 4)
        o_r = count("o_r", 4)
        o_v = count("o_v", 4)
        r_t = count("r_t", KT, KT + 1)
        r_e = count("r_e", KT)
        z_mm = count("z_mm", 2, 3)
        z_v = count("z_v", 2 * 2, 3)
        z_o = dcount("z_o", 1)

        x_v = a["L0_attn_x"].rearrange("b (j p) d -> b p j d", p=P)
        o_view = out.rearrange("b (j p) d -> b p j d", p=P)

        def rows(w):
            return w.rearrange("(k p) n -> p k n", p=P)

        loads_in = [
            (w_in, rows(a["W_in"])), (b_in[ST:P, :], a["b_in"].rearrange("(p o) -> p o", o=1)),
        ]
        loads = [
            (w_ab[0:ST, :], a["A"]), (w_ab[ST:P, :], a["Bm"]),
            (b_z[:, 0], a["bf"]), (b_z[:, 1], a["bi"]), (b_z[:, 2], a["bc"]),
            (b_z[:, 3], a["b_gate"]), (c0, a["in_c"]),
            (w_x[:, 0], rows(a["wfT"])), (w_x[:, 1], rows(a["wiT"])), (w_x[:, 2], rows(a["wcT"])),
            (w_c[:, 0], rows(a["ufT"])), (w_c[:, 1], rows(a["uiT"])), (w_c[:, 2], rows(a["ucT"])),
            (w_gate, rows(a["W_gate"])), (w_wo, rows(a["woT"])),
            (w_pt[:, :, :], rows(a["protoT"])), (ntemp[:, :], a["temp"].partition_broadcast(P)),
        ]
        loads_b = [
            (w_uo, rows(a["uoT"])), (w_cd[0:ST, :], a["CT"]), (w_cd[ST:P, :], a["DT"]),
            (w_out[:, :, :], rows(a["W_out"])),
            (w_qk[:, 0], rows(a["WqT"])), (w_qk[:, 1], rows(a["WkT"])), (w_v[:, :, :], rows(a["WvT"])),
            (w_pr[:, :, :], rows(a["WpT"])), (w_b[:, :, :], rows(a["BT"])), (w_a[:, :, :], rows(a["AT"])),
            (w_bias[:, :], a["bias"]),
            (bout[:, :], a["b_out"].partition_broadcast(P)), (bo[:, :], a["bo"].partition_broadcast(P)),
        ]

        block = ctx.enter_context(nc.Block())

        @block.sync
        def _(sp):
            for s in (*a_x, *a_sx, *a_ss, *c_x, *c_u, *c_hs, c_gs, c_ws, l_xt, l_gt, l_wx, l_x, l_st, q_st, x_sv,
                      x_ld, q_ld, *m_ld, z_o):
                sp.sem_inc(s.sem, s.credit)

            def load_input(g, s):
                sp.dma_start(xin[s][:, :, :], x_v[bass.ds(g * 2 + s, 1)].rearrange("o p j d -> p (o j) d")
                             ).then_inc(a_x[s].sem, 16)

            def prepass(g, more):
                for s in range(2):
                    sp.wait_ge(a_xn.sem, a_xn.at(g, s + 1))
                    if more:
                        load_input(g + 1, s)
                for s in range(2):
                    sp.wait_ge(a_xt.sem, a_xt.at(g, KT * (s + 1)))
                    sp.dma_start(xt_d[bass.ds(g * 2 + s, 1)].rearrange("o p k t -> p (o k) t"), xtp[s][:, :, :]
                                 ).then_inc(a_sx[s].sem, 16)
                    sp.wait_ge(a_mr.sem, a_mr.at(g, 2 * (s + 1)))
                    sp.dma_start(st_d[bass.ds(g * 2 + s, 1)].rearrange("o p c j -> p (o c) j"), sst[:, s]
                                 ).then_inc(a_ss[s].sem, 16)

            for s in range(2):
                load_input(0, s)
            for dst, src in loads_in:
                sp.dma_start(dst, src).then_inc(ld_in, 16)
            for dst, src in loads:
                sp.dma_start(dst, src).then_inc(ld_w, 16)
            with sp.Fori(0, B // 2 - 1) as g:
                prepass(g, True)
            prepass(B // 2 - 1, False)
            for s in (*a_sx, *a_ss):
                sp.wait_ge(s.sem, 16 * (B // 2 + 1))
            sp.wait_ge(a_ue.sem, B + 1)

            def load_half(b, n):
                sp.dma_start(XB[:, n], xt_d[bass.ds(b, 1), :, :, n * HALF:(n + 1) * HALF]
                             .rearrange("o p k t -> p (o k) t")).then_inc(c_x[n].sem, 16)
                sp.dma_start(HB[ST:P, n * STEPS:(n + 1) * STEPS],
                             HU[ST:P, bass.ds(b * (2 * STEPS * B) + n * STEPS * B, STEPS * B)]
                             .rearrange("p (s b) -> p s b", b=B)).then_inc(c_u[n].sem, 16)

            def save_half(b, n):
                col = b * (2 * STEPS * B)
                sp.wait_ge(c_h.sem, c_h.at(b, (n + 1) * STEPS))
                if n == 0:
                    sp.dma_start(HU[0:ST, bass.ds(col, STEPS * B)], HB[0:ST, 1:STEPS + 1]
                                 .rearrange("p s b -> p (s b)")).then_inc(c_hs[n].sem, 16)
                else:
                    sp.dma_start(HU[0:ST, bass.ds(col + STEPS * B, (STEPS - 1) * B)],
                                 HB[0:ST, STEPS + 1:2 * STEPS].rearrange("p s b -> p (s b)")
                                 ).then_inc(c_hs[n].sem, 16)
                    sp.dma_start(HU[0:ST, bass.ds(col + (2 * STEPS - 1) * B, B)], HB[0:ST, 0]
                                 ).then_inc(c_hs[n].sem, 16)
                sp.wait_ge(c_t.sem, c_t.at(b, 8 * (n + 1)))
                sp.dma_start(gt_d[bass.ds(b, 1), :, :, n * HALF:(n + 1) * HALF]
                             .rearrange("o p k t -> p (o k) t"), GS).then_inc(c_gs.sem, 16)
                sp.wait_ge(c_w.sem, c_w.at(b, n + 1))
                sp.dma_start(wx_d[bass.ds(b, 1), :, 2 * n:2 * n + 2]
                             .rearrange("o p j d -> p (o j) d"), WS).then_inc(c_ws.sem, 16)

            load_half(0, 0)
            load_half(0, 1)
            for dst, src in loads_b:
                sp.dma_start(dst, src).then_inc(ld_b, 16)

            with sp.Fori(0, B - 1) as b:
                save_half(b, 0)
                sp.wait_ge(c_z.sem, c_z.at(b, 5))
                load_half(b + 1, 0)
                save_half(b, 1)
                sp.wait_ge(c_z.sem, c_z.at(b, 10))
                load_half(b + 1, 1)

            def hold():
                sp.sem_inc(carried, 1)

            def load_batch(b):
                one = bass.ds(b, 1)
                sp.wait_ge(y_p.sem, y_p.at(b, 0))
                hold()
                sp.wait_ge(p_sg.sem, p_sg.at(b, 0))
                hold()
                sp.wait_ge(r_t.sem, r_t.at(b, -KT))
                hold()
                sp.wait_ge(x_sv.sem, x_sv.at(b, 0))
                hold()
                sp.wait_ge(n_xn.sem, n_xn.at(b, 0))
                sp.dma_start(XT[:, :, :], xt_d[one].rearrange("o p k t -> p (o k) t")).then_inc(l_xt.sem, 16)
                sp.dma_start(GT[:, :, :], gt_d[one].rearrange("o p k t -> p (o k) t")).then_inc(l_gt.sem, 16)
                sp.dma_start(WX[:, :, :], wx_d[one].rearrange("o p j d -> p (o j) d")).then_inc(l_wx.sem, 16)
                sp.dma_start(X1[:, :, :], x_v[one].rearrange("o p j d -> p (o j) d")).then_inc(l_x.sem, 16)
                sp.dma_start(stb[:, :, :], st_d[one].rearrange("o p c j -> p (o c) j")).then_inc(l_st.sem, 16)

            def save_x1(b):
                sp.wait_ge(s_p.sem, s_p.at(b, 3))
                sp.dma_start(x1_d[bass.ds(b, 1)].rearrange("o p j d -> p (o j) d"), X1[:, :, :]
                             ).then_inc(x_sv.sem, 16)

            def operands(b):
                for n, ready in enumerate((2, 5, 6)):
                    sp.wait_ge(q_s.sem, q_s.at(b, ready))
                    sp.dma_start(qk_d[n].rearrange("c (m p) t -> p (c m) t", p=P), QB[:, n]
                                 ).then_inc(q_st.sem, 16)
                sp.wait_ge(q_st.sem, q_st.at(b, SPLIT))
                hold()
                sp.wait_ge(t_mm.sem, t_mm.at(b, 0))
                for r, pair in enumerate(PAIRS):
                    for c, dst in enumerate((Q6, K6)):
                        sp.dma_start(dst[r * HD:(r + 1) * HD, :, :],
                                     qk_d[pair[c], c].rearrange("(h d) t -> d h t", d=HD)
                                     ).then_inc(q_ld.sem, 16)

            def batch(b, more):
                if more:
                    load_batch(b + 1)
                for a in range(2):
                    sp.wait_ge(m_h.sem, m_h.at(b, a + 1))
                    heads = slice(a * H // 2, (a + 1) * H // 2)
                    sp.dma_start(Q6[KS:KS + 1, heads, :], nmh[:, a]).then_inc(m_ld[a].sem, 16)
                    sp.dma_start(Q6[KS + 1:KS + 2, heads, :], nml[:, a]).then_inc(m_ld[a].sem, 16)
                if more:
                    save_x1(b + 1)
                    sp.wait_ge(n_tr.sem, n_tr.at(b + 1, KT))
                    hold()
                    sp.wait_ge(n_x2.sem, n_x2.at(b + 1, NT))
                    hold()
                sp.wait_ge(x_sv.sem, x_sv.at(b, 1))
                sp.dma_start(S1[:, :, :], x1_d[bass.ds(b, 1)].rearrange("o p j d -> p (o j) d")
                             ).then_inc(x_ld.sem, 16)
                if more:
                    operands(b + 1)

            sp.wait_ge(c_gs.sem, c_gs.at(1, 0))
            sp.wait_ge(c_ws.sem, c_ws.at(1, 0))
            load_batch(0)
            save_half(B - 1, 0)
            save_half(B - 1, 1)
            for n in range(2):
                sp.wait_ge(c_hs[n].sem, c_hs[n].at(B, 0))
            sp.wait_ge(c_gs.sem, 16 * (2 * B + 1))
            sp.wait_ge(c_ws.sem, 16 * (2 * B + 1))
            save_x1(0)
            operands(0)
            with sp.Fori(0, B - 1) as b:
                batch(b, True)
            batch(B - 1, False)
            sp.wait_ge(z_o.sem, 16 * (B + 1))

        @block.gpsimd
        def _(pool):
            g_ = nc.gpsimd
            for s in (a_rs, a_mr, n_mr, y_p, s_p, p_xn, p_hq, p_sg, n_rs, q_r, d_p, v_c):
                pool.sem_inc(s.sem, s.credit)
            g_.memset(ident[:, :], 0.0).then_inc(const, 1)
            g_.memset(negmask[:, :], 0.0).then_inc(const, 1)
            g_.memset(negmask_t[:, :], 0.0).then_inc(const, 1)
            g_.memset(eps[:, :], EPS).then_inc(const, 1)
            g_.memset(halves[:, :], 0.5).then_inc(const, 1)
            g_.memset(mhalf[:, :], -0.5).then_inc(const, 1)
            g_.memset(minus[:, :], -1.0).then_inc(const, 1)
            g_.memset(half1[:, :], 0.5).then_inc(const, 1)
            g_.memset(ones[:, :], 1.0).then_inc(const, 1)
            g_.iota(iota[:, :], pattern=[[1, NP]], base=0, channel_multiplier=0,
                    allow_small_or_imprecise_dtypes=True).then_inc(const, 1)
            pool.wait_ge(const, 10)
            g_.affine_select(out=ident[:, :], in_=ident[:, :], compare_op=ALU.not_equal, fill=1.0, base=0,
                             pattern=[[-1, P]], channel_multiplier=1).then_inc(const, 1)
            g_.affine_select(out=negmask[:, :], in_=negmask[:, :], compare_op=ALU.is_ge, fill=-BIG, base=0,
                             pattern=[[-1, P]], channel_multiplier=1).then_inc(const, 1)
            g_.affine_select(out=negmask_t[:, :], in_=negmask_t[:, :], compare_op=ALU.is_ge, fill=-BIG, base=0,
                             pattern=[[1, P]], channel_multiplier=-1).then_inc(const, 1)
            g_.memset(vscale[:, :], OUT_SCALE).then_inc(const, 1)
            pool.wait_ge(const, 13)
            g_.tensor_copy(identb[:, :], ident[:, :]).then_inc(const, 1)

            with pool.Fori(0, B // 2) as g:
                for s in range(2):
                    pool.wait_ge(a_st.sem, a_st.at(g, 2 * NT * (s + 1)))
                    pool.wait_ge(a_ss[s].sem, a_ss[s].at(g, 0))
                    g_.tensor_tensor(sst[:, s, 0], amv[:, s, :, 1], eps[:, :], ALU.add).then_inc(a_rs.sem, 1)
                    pool.wait_ge(a_rs.sem, a_rs.at(g, 2 * s + 1))
                    g_.tensor_tensor(sst[:, s, 0], sst[:, s, 0], mhalf[:, :], ALU.pow).then_inc(a_rs.sem, 1)
                    g_.tensor_tensor(sst[:, s, 1], amv[:, s, :, 0], minus[:, :], ALU.mult).then_inc(a_mr.sem, 1)
                    pool.wait_ge(a_rs.sem, a_rs.at(g, 2 * s + 2))
                    pool.wait_ge(a_mr.sem, a_mr.at(g, 2 * s + 1))
                    g_.tensor_tensor(sst[:, s, 1], sst[:, s, 1], sst[:, s, 0], ALU.mult).then_inc(a_mr.sem, 1)

            pool.wait_ge(f_pe, 1)
            pool.wait_ge(f_act, 1)
            for n in range(2):
                pool.wait_ge(c_hs[n].sem, c_hs[n].at(B, 0))
            pool.wait_ge(c_gs.sem, 16 * (2 * B + 1))
            pool.wait_ge(c_ws.sem, 16 * (2 * B + 1))
            g_.memset(VA[:, :, :, :], 0.0).then_inc(f_set, 1)
            pool.wait_ge(f_set, 1)
            g_.memset(VA[:, :, :, HD:HD + 1], 1.0).then_inc(f_set, 1)

            def batch(b):
                pool.wait_ge(l_wx.sem, l_wx.at(b, 1))
                g_.tensor_tensor(WX[:, :, :], WX[:, :, :], UC[:, :, :], ALU.add).then_inc(p_hq.sem, 1)
                pool.wait_ge(y_v.sem, y_v.at(b, KT))
                pool.wait_ge(l_xt.sem, l_xt.at(b, 1))
                g_.tensor_tensor(YS[:, :, :], YS[:, :, :], XT[:, :, :], ALU.subtract).then_inc(y_p.sem, 1)
                pool.wait_ge(y_p.sem, y_p.at(b, 1))
                pool.wait_ge(g_h.sem, g_h.at(b, 1))
                g_.tensor_tensor(YS[:, :, :], YS[:, :, :], GT[:, :, :], ALU.mult).then_inc(y_p.sem, 1)
                pool.wait_ge(y_p.sem, y_p.at(b, 2))
                g_.tensor_tensor(YS[:, :, :], YS[:, :, :], XT[:, :, :], ALU.add).then_inc(y_p.sem, 1)
                pool.wait_ge(x_n.sem, x_n.at(b, NT))
                g_.tensor_tensor(XNB[:, :, :], XNB[:, :, :],
                                 bout[:, :].unsqueeze(1).to_broadcast([P, NT, D]), ALU.add
                                 ).then_inc(p_xn.sem, 1)
                pool.wait_ge(g_t.sem, g_t.at(b, 3))
                g_.tensor_tensor(SG[:, :, :], SG[:, :, :], WX[:, :, :], ALU.mult).then_inc(p_sg.sem, 1)
                pool.wait_ge(p_sg.sem, p_sg.at(b, 1))
                pool.wait_ge(s_v.sem, s_v.at(b, 2))
                g_.tensor_tensor(S1[:, :, :], S1[:, :, :], XNB[:, :, :], ALU.add).then_inc(s_p.sem, 1)
                pool.wait_ge(s_p.sem, s_p.at(b, 1))
                g_.tensor_tensor(S1[:, :, :], S1[:, :, :], SG[:, :, :], ALU.mult).then_inc(s_p.sem, 1)
                pool.wait_ge(s_p.sem, s_p.at(b, 2))
                pool.wait_ge(l_x.sem, l_x.at(b, 1))
                g_.tensor_tensor(X1[:, :, :], X1[:, :, :], S1[:, :, :], ALU.add).then_inc(s_p.sem, 1)
                pool.wait_ge(n_st.sem, n_st.at(b, 2 * NT))
                g_.tensor_tensor(rst[:, :], mv[:, :, 1], eps[:, :], ALU.add).then_inc(n_rs.sem, 1)
                g_.tensor_tensor(mrs[:, :], mv[:, :, 0], minus[:, :], ALU.mult).then_inc(n_mr.sem, 1)
                pool.wait_ge(n_rs.sem, n_rs.at(b, 1))
                g_.tensor_tensor(rst[:, :], rst[:, :], mhalf[:, :], ALU.pow).then_inc(n_rs.sem, 1)
                pool.wait_ge(n_mr.sem, n_mr.at(b, 1))
                pool.wait_ge(n_rs.sem, n_rs.at(b, 2))
                g_.tensor_tensor(mrs[:, :], mrs[:, :], rst[:, :], ALU.mult).then_inc(n_mr.sem, 1)
                pool.wait_ge(q_s.sem, q_s.at(b, 2))
                g_.tensor_tensor(QF[:, KT:], QF[:, KT:], QB[:, 0, KT:], ALU.subtract).then_inc(q_r.sem, 1)
                pool.wait_ge(q_s.sem, q_s.at(b, 5))
                g_.tensor_tensor(QF[:, KT:], QF[:, KT:], QB[:, 1, KT:], ALU.subtract).then_inc(q_r.sem, 1)
                pool.wait_ge(d_v.sem, d_v.at(b, 5))
                g_.tensor_tensor(near[:, :, :].rearrange("p a b -> p (a b)"),
                                 near[:, :, :].rearrange("p a b -> p (a b)"), halves[:, :], ALU.pow
                                 ).then_inc(d_p.sem, 1)
                pool.wait_ge(v_e.sem, v_e.at(b, 2))
                pool.wait_ge(o_mm.sem, o_mm.at(b, 0))
                for j in range(NT):
                    mm = g_.tensor_tensor(VA[:, j, :, 0:HD], V1[:, j].rearrange("p (h d) -> p h d", d=HD),
                                          vscale[:, :].unsqueeze(2).to_broadcast([P, H, HD]), ALU.mult)
                mm.then_inc(v_c.sem, 1)

            pool.wait_ge(f_e, 2)
            pool.wait_ge(ld_b, 16 * len(loads_b))
            with pool.Fori(0, B) as b:
                batch(b)

        @block.tensor
        def _(pe):
            for s in (a_tr, a_u, c_mm, c_z, y_mm, s_mm, n_tr, q_mm, v_mm, d_mm, m_mm, m_t, h_mm, h_t, w_t,
                      e_mm, t_mm, o_mm, o_t, r_t, z_mm):
                pe.sem_inc(s.sem, s.credit)
            pe.wait_ge(ld_in, 16 * len(loads_in))
            pe.wait_ge(const, 15)

            with pe.Fori(0, B // 2) as g:
                for s in range(2):
                    pe.wait_ge(a_xn.sem, a_xn.at(g, s + 1))
                    pe.wait_ge(a_xt.sem, a_xt.at(g, 0))
                    for k in range(KT):
                        for j in range(NT):
                            mm = pe.transpose(PS[:, 2 * s + k, j * P:(j + 1) * P],
                                              xnp[s][:, j, k * P:(k + 1) * P], ident[:, :])
                        mm.then_inc(a_tr.sem, 1)
                for s in range(2):
                    pe.wait_ge(a_ue.sem, a_ue.at(g, 0))
                    pe.wait_ge(a_xt.sem, a_xt.at(g, KT * (s + 1)))
                    for k in range(KT):
                        mm = pe.matmul(PS[ST:P, 4 + s, :], w_in[:, k], xtp[s][:, k], start=(k == 0),
                                       stop=(k == KT - 1))
                    mm.then_inc(a_u.sem, 1)

            pe.wait_ge(init, 2)
            pe.wait_ge(ld_w, 16 * len(loads))

            def half(b, n):
                work = []
                for z in range(3):
                    for m in range(KT):
                        o = PS[:, z, m * HALF:(m + 1) * HALF]
                        w = slice(m * P, (m + 1) * P)
                        for k in range(KT):
                            work.append((o, w_x[:, z, k, w], XB[:, n, k], k == 0, False, None, z, m))
                        for k in range(KT):
                            work.append((o, w_c[:, z, k, w], CT[:, k, n * HALF:(n + 1) * HALF], False,
                                         k == KT - 1, c_z if m == k == 1 else None, z, m))
                for m in range(KT):
                    for k in range(KT):
                        work.append((PS[:, 3, m * HALF:(m + 1) * HALF], w_gate[:, k, m * P:(m + 1) * P],
                                     XB[:, n, k], k == 0, k == 1, c_z if m == k == 1 else None, 3, m))
                for j in range(2):
                    for k in range(KT):
                        work.append((PS[:, 4, j * D:(j + 1) * D], XB[:, n, k, j * P:(j + 1) * P], w_wo[:, k],
                                     k == 0, k == 1, c_z if j == k == 1 else None, 4, j))
                assert len(work) == STEPS
                pe.wait_ge(c_u[n].sem, c_u[n].at(b, 1))
                pe.wait_ge(c_x[n].sem, c_x[n].at(b, 1))
                for s, (o, lhs, rhs, first, last, done, z, m) in enumerate(work):
                    step = n * STEPS + s
                    pe.wait_ge(c_h.sem, c_h.at(b, step))
                    pe.matmul(PS[0:ST, 7, 0:B], w_ab, HB[:, step], start=True, stop=True
                              ).then_inc(c_mm.sem, 1)
                    if m == 0 and first:
                        if z < 3:
                            pe.wait_ge(c_t.sem, c_t.at(b, 8 * n - 8 + 2 * z + 2))
                        elif z == 3:
                            pe.wait_ge(c_t.sem, c_t.at(b, 8 * n))
                        else:
                            pe.wait_ge(c_w.sem, c_w.at(b, n))
                    if z == 0 and m == 0 and not first and s == KT:
                        pe.wait_ge(c_c.sem, c_c.at(b, 4 * n - 4))
                    mm = pe.matmul(o, lhs, rhs, start=first, stop=last)
                    if done:
                        mm.then_inc(done.sem, 1)

            with pe.Fori(0, B) as b:
                half(b, 0)
                half(b, 1)

            pe.wait_ge(init, 3)
            for k in range(KT):
                pe.matmul(PS[:, 5, 0:NP], ones[:, :], ptsq[:, k], start=(k == 0), stop=(k == KT - 1))
            pe.wait_ge(ld_b, 16 * len(loads_b))
            pe.wait_ge(c_c.sem, 8 * B + c_c.credit)
            pe.wait_ge(c_t.sem, 16 * B + c_t.credit)
            for j in range(NT):
                for k in range(KT):
                    mm = pe.matmul(PS[:, j // 2, j % 2 * D:(j % 2 + 1) * D], CT[:, k, j * P:(j + 1) * P],
                                   w_uo[:, k], start=(k == 0), stop=(k == KT - 1))
            mm.then_inc(f_pe, 1)
            for n in range(2):
                pe.wait_ge(c_hs[n].sem, c_hs[n].at(B, 0))

            def tokens(bank, j):
                return PS[:, bank + j // 2, j % 2 * D:(j % 2 + 1) * D]

            def mix(b, m):
                if m == 0:
                    pe.wait_ge(w_e.sem, w_e.at(b, 0))
                    pe.wait_ge(h_e.sem, h_e.at(b, 0))
                hu = HU[:, :].rearrange("p (t b) -> p b t", b=B)[:, bass.ds(b, 1)].rearrange("p o t -> p (o t)")
                pe.matmul(PS[:, 6 + m, :], w_cd[:, m * P:(m + 1) * P], hu, start=True, stop=True
                          ).then_inc(y_mm.sem, 1)

            def leave(b, j):
                if j == 0:
                    pe.wait_ge(e_v.sem, e_v.at(b, 0))
                    pe.wait_ge(y_p.sem, y_p.at(b, 3))
                elif j == 2:
                    pe.wait_ge(m_h.sem, m_h.at(b, -1))
                for k in range(KT):
                    mm = pe.matmul(tokens(6, j), YS[:, k, j * P:(j + 1) * P], w_out[:, k],
                                   start=(k == 0), stop=(k == KT - 1))
                if j % 2:
                    mm.then_inc(s_mm.sem, 1)

            def normal_turn(b):
                pe.wait_ge(n_xn.sem, n_xn.at(b, NT))
                for k in range(KT):
                    for j in range(NT):
                        mm = pe.transpose(PS[:, 6 + k, j * P:(j + 1) * P], S1[:, j, k * P:(k + 1) * P],
                                          ident[:, :])
                    mm.then_inc(n_tr.sem, 1)

            def query_key(b, n):
                if n == 0:
                    pe.wait_ge(n_xt.sem, n_xt.at(b, KT))
                elif n > 1:
                    pe.wait_ge(q_e.sem, q_e.at(b, n - 1))
                for k in range(KT):
                    mm = pe.matmul(PS[:, 6 + n % 2, :], w_qk[:, n // 2, k, n % 2 * P:(n % 2 + 1) * P],
                                   XT1[:, k], start=(k == 0), stop=(k == KT - 1))
                mm.then_inc(q_mm.sem, 1)

            def value(b, p):
                pe.wait_ge(q_e.sem, q_e.at(b, 3 + p))
                for j in (2 * p, 2 * p + 1):
                    for k in range(KT):
                        mm = pe.matmul(tokens(6, j), XT1[:, k, j * P:(j + 1) * P], w_v[:, k],
                                       start=(k == 0), stop=(k == KT - 1))
                mm.then_inc(v_mm.sem, 1)

            def distance(b):
                pe.wait_ge(v_e.sem, v_e.at(b, 1))
                for j in range(NT):
                    for k in range(KT):
                        mm = pe.matmul(PS[:, 6, j * NP:(j + 1) * NP], XT1[:, k, j * P:(j + 1) * P],
                                       w_pt[:, k], start=(k == 0), stop=(k == KT - 1))
                mm.then_inc(d_mm.sem, 1)

            def low_rank(b, j):
                if j == 0:
                    pe.wait_ge(d_v.sem, d_v.at(b, 1))
                else:
                    pe.wait_ge(h_v.sem, h_v.at(b, j))
                for k in range(KT):
                    mm = pe.matmul(PS[:, 6, :], XT1[:, k, j * P:(j + 1) * P], w_b[:, k],
                                   start=(k == 0), stop=(k == KT - 1))
                mm.then_inc(h_mm.sem, 1)

            def low_rank_turn(b, j):
                if j == 0:
                    pe.wait_ge(v_e.sem, v_e.at(b, 2))
                else:
                    pe.wait_ge(h_e.sem, h_e.at(b, j))
                pe.wait_ge(h_v.sem, h_v.at(b, j + 1))
                for n in range(NR // P):
                    mm = pe.transpose(PS[:, 7, n * P:(n + 1) * P], HM[:, n * P:(n + 1) * P], ident[:, :])
                mm.then_inc(h_t.sem, 1)

            def weights_turn(b):
                pe.wait_ge(h_v.sem, h_v.at(b, NT))
                for j in range(NT):
                    mm = pe.transpose(PS[0:NP, 6, j * P:(j + 1) * P], wm[:, j], ident[:, :])
                mm.then_inc(w_t.sem, 1)

            def experts(b, n, more):
                if n == 0:
                    pe.wait_ge(h_e.sem, h_e.at(b, NT))
                    pe.wait_ge(w_e.sem, w_e.at(b, 1))
                    if more:
                        pe.wait_ge(y_v.sem, y_v.at(b + 1, KT))
                j = n // 2
                o = PS[:, 7 - j // 2, j % 2 * D:(j % 2 + 1) * D]
                for r in (2 * (n % 2), 2 * (n % 2) + 1):
                    pe.matmul(o, HMT[:, r, j * P:(j + 1) * P], w_a[:, r], start=(r == 0), stop=False)
                if n % 2:
                    mm = pe.matmul(o, wmt[:, j * P:(j + 1) * P], w_bias[:, :], start=False, stop=True)
                    if j % 2:
                        mm.then_inc(e_mm.sem, 1)

            def scores(b, u):
                hp, i = u // NT, u % NT
                if u >= 3:
                    pe.wait_ge(m_r.sem, m_r.at(b, u - 2))
                elif u == 0:
                    pe.wait_ge(r_e.sem, r_e.at(b, 0))
                elif u == 1:
                    pe.wait_ge(z_v.sem, z_v.at(b, -2))
                for e in range(2):
                    h = 2 * hp + e
                    bank = 2 * (u % 3) + e
                    pe.matmul(PS[:, bank, 0:(i + 1) * P], Q6[0:KS, h, i * P:(i + 1) * P],
                              K6[0:KS, h, 0:(i + 1) * P], start=True, stop=False)
                    mm = pe.matmul(PS[:, bank, i * P:(i + 1) * P], identb[:, :], negmask[:, :],
                                   start=False, stop=True)
                mm.then_inc(m_mm.sem, 1)

            def maxima_turn(b, a):
                if a == 0:
                    pe.wait_ge(e_v.sem, e_v.at(b, 2))
                pe.wait_ge(m_r.sem, m_r.at(b, (a + 1) * NT * H // 4))
                for i in range(NT):
                    mm = pe.transpose(PS[0:H // 2, 7 - 2 * a, i * P:(i + 1) * P],
                                      nm[:, i, a * H // 2:(a + 1) * H // 2], ident[:, :])
                mm.then_inc(m_t.sem, 1)

            def turned_tile(b, h, kt, bank, at):
                w = T - kt * P
                pe.matmul(PS[:, bank, at:at + w], K6[0:KM, h, kt * P:(kt + 1) * P],
                          Q6[0:KM, h, kt * P:T], start=True, stop=False)
                return pe.matmul(PS[:, bank, at:at + P], identb[:, :], negmask_t[:, :],
                                 start=False, stop=True)

            def turned_own(b, h):
                if h % (H // 2) == 0:
                    pe.wait_ge(m_ld[2 * h // H].sem, m_ld[2 * h // H].at(b, 2))
                if h >= 2:
                    pe.wait_ge(t_e.sem, t_e.at(b, 3 * (h // 2) + 2 * (h % 2) - 2))
                for kt in (0, 1, 3):
                    mm = turned_tile(b, h, kt, 3 * (h % 2) + P_AT[kt] // 512, P_AT[kt] % 512)
                mm.then_inc(t_mm.sem, 1)

            def turned_shared(b, h):
                if h >= 2:
                    pe.wait_ge(t_e.sem, t_e.at(b, 3 * (h // 2) - 1))
                turned_tile(b, h, 2, 2, 0)
                turned_tile(b, h + 1, 2, 2, 2 * P).then_inc(t_mm.sem, 1)

            def values(b, g):
                pe.wait_ge(t_e.sem, t_e.at(b, 6 * (g + 1)))
                if g == 0:
                    pe.wait_ge(m_h.sem, m_h.at(b, 2))
                    pe.wait_ge(v_c.sem, v_c.at(b, 1))
                else:
                    pe.wait_ge(o_v.sem, o_v.at(b, g))
                for kt in range(NT):
                    for j in range(4):
                        w = T - kt * P
                        at = P_AT[kt]
                        mm = pe.matmul(PS[32 * j:32 * j + 32, 5, kt * P:T], VA[:, kt, 4 * g + j],
                                       PR[:, g % 2, j, at:at + w],
                                       start=(kt == 0), stop=(kt == NT - 1))
                mm.then_inc(o_mm.sem, 1)

            def values_turn(b, g):
                pe.wait_ge(o_e.sem, o_e.at(b, g + 1))
                for j in range(NT):
                    mm = pe.transpose(PS[:, 5, j * P:(j + 1) * P], OS[:, j * P:(j + 1) * P], ident[:, :])
                mm.then_inc(o_t.sem, 1)

            def heads_turn(b):
                pe.wait_ge(o_v.sem, o_v.at(b, 4))
                pe.wait_ge(t_e.sem, t_e.at(b, TU))
                for k in range(KT):
                    for j in range(NT):
                        mm = pe.transpose(PS[:, k, j * P:(j + 1) * P], AT[:, j, k * P:(k + 1) * P], ident[:, :])
                    mm.then_inc(r_t.sem, 1)

            def project(b):
                pe.wait_ge(r_e.sem, r_e.at(b, KT))
                for j in range(NT):
                    for k in range(KT):
                        mm = pe.matmul(tokens(2, j), AO[:, k, j * P:(j + 1) * P], w_pr[:, k],
                                       start=(k == 0), stop=(k == KT - 1))
                    if j % 2:
                        mm.then_inc(z_mm.sem, 1)

            def run(steps, n):
                for step in steps.get(n, ()):
                    step()

            def batch(b, more):
                pe.wait_ge(q_ld.sem, q_ld.at(b, 2 * len(PAIRS)))
                side = {0: [lambda: low_rank(b, 3)], 2: [lambda: low_rank_turn(b, 3), lambda: weights_turn(b)],
                        19: [lambda: maxima_turn(b, 0)]}
                for n, u in enumerate((6, 7, 9, 10, 12, 13, 15, 16)):
                    side[u] = [lambda n=n: experts(b, n, more)]
                if more:
                    for m in range(KT):
                        side[3 + m] = [lambda m=m: mix(b + 1, m)]
                    for j, u in enumerate((20, 21, 24, 25)):
                        side[u] = [lambda j=j: leave(b + 1, j)]
                for u in range(NT * H // 2):
                    scores(b, u)
                    run(side, u)
                pe.wait_ge(m_r.sem, m_r.at(b, NT * H // 2 - 1))
                turned_own(b, 0)
                maxima_turn(b, 1)
                side = {4: [lambda: values(b, 0)], 5: [lambda: values_turn(b, 0)], 8: [lambda: values(b, 1)], 10: [lambda: values_turn(b, 1)], 12: [lambda: values(b, 2)], 14: [lambda: values_turn(b, 2)]}
                if more:
                    side.setdefault(4, []).extend([lambda: normal_turn(b + 1)])
                    side.setdefault(5, []).extend([lambda: query_key(b + 1, 0), lambda: query_key(b + 1, 1)])
                    side.setdefault(6, []).extend([lambda: query_key(b + 1, 2), lambda: query_key(b + 1, 3)])
                    side.setdefault(7, []).extend([lambda: value(b + 1, 0), lambda: value(b + 1, 1)])
                    side.setdefault(8, []).extend([lambda: distance(b + 1)])
                for h in range(H):
                    if h:
                        turned_own(b, h)
                    if h % 2 == 0:
                        turned_shared(b, h)
                    run(side, h)
                if more:
                    low_rank(b + 1, 0)
                values(b, 3)
                if more:
                    low_rank_turn(b + 1, 0)
                    low_rank(b + 1, 1)
                values_turn(b, 3)
                if more:
                    low_rank_turn(b + 1, 1)
                    low_rank(b + 1, 2)
                heads_turn(b)
                if more:
                    low_rank_turn(b + 1, 2)
                project(b)

            for m in range(KT):
                mix(0, m)
            for j in range(NT):
                leave(0, j)
            normal_turn(0)
            for n in range(4):
                query_key(0, n)
            value(0, 0)
            value(0, 1)
            distance(0)
            pe.wait_ge(f_e, 2)
            pe.wait_ge(f_p2, 1)
            pe.wait_ge(init, 7)
            pe.wait_ge(f_set, 2)
            for j in range(NT - 1):
                low_rank(0, j)
                low_rank_turn(0, j)
            with pe.Fori(0, B - 1) as b:
                batch(b, True)
            batch(B - 1, False)

        @block.scalar
        def _(act):
            s_ = nc.scalar
            for s in (a_xt, c_h, c_t, g_t, n_x2, n_xt, q_e, d_e, h_e, y_v, s_v, e_t, t_e, o_e, r_e, x_n, a_ue, g_h, m_a, n_xn,
                      w_e):
                act.sem_inc(s.sem, s.credit)
            act.wait_ge(ld_in, 16 * len(loads_in))
            with act.Fori(0, B // 2) as g:
                for s in range(2):
                    act.wait_ge(a_u.sem, a_u.at(g, 0))
                    act.wait_ge(a_sx[s].sem, a_sx[s].at(g, 0))
                    for k in range(KT):
                        act.wait_ge(a_tr.sem, a_tr.at(g, KT * s + k + 1))
                        s_.copy(xtp[s][:, k], PS[:, 2 * s + k, :]).then_inc(a_xt.sem, 1)
                for s in range(2):
                    act.wait_ge(a_u.sem, a_u.at(g, s + 1))
                    s_.activation(HU[ST:P, :].rearrange("p (t b) -> p b t", b=B)
                                  [:, bass.ds(g * 2 + s, 1)].rearrange("p o t -> p (o t)"),
                                  PS[ST:P, 4 + s, :], ACT.Identity, bias=b_in[ST:P, 0:1]).then_inc(a_ue.sem, 1)
            act.wait_ge(ld_w, 16 * len(loads))
            s_.mul(b_z[:, 0:2], b_z[:, 0:2], 0.5).then_inc(act_init, 1)
            s_.mul(b_z[:, 3], b_z[:, 3], 0.5).then_inc(act_init, 1)
            act.wait_ge(act_init, 2)

            tasks = {10: (0, 0), 12: (0, 1), 18: (1, 0), 20: (1, 1), 26: (2, 0), 28: (2, 1),
                     30: (3, 0), 31: (3, 1)}

            def half(b, n):
                for s in range(STEPS):
                    step = n * STEPS + s
                    act.wait_ge(c_mm.sem, c_mm.at(b, step + 1))
                    nxt = (step + 1) % (2 * STEPS)
                    if s == 0:
                        act.wait_ge(c_hs[n].sem, c_hs[n].at(b, 0))
                    s_.activation(HB[0:ST, nxt], PS[0:ST, 7, 0:B], ACT.Tanh).then_inc(c_h.sem, 1)
                    if s in tasks:
                        z, m = tasks[s]
                        if m == 0:
                            act.wait_ge(c_z.sem, c_z.at(b, 5 * n + z + 1))
                            if z < 3:
                                act.wait_ge(c_c.sem, c_c.at(b, 4 * n))
                            else:
                                act.wait_ge(c_gs.sem, c_gs.at(b, n))
                        dst = TG[:, z, m] if z < 3 else GS[:, m]
                        s_.activation(dst, PS[:, z, m * HALF:(m + 1) * HALF], ACT.Tanh,
                                      bias=b_z[:, z, m:m + 1], scale=(1.0 if z == 2 else 0.5)
                                      ).then_inc(c_t.sem, 1)

            with act.Fori(0, B) as b:
                half(b, 0)
                half(b, 1)
            act.wait_ge(c_h.sem, 2 * STEPS * B + 1)
            act.wait_ge(c_t.sem, 16 * B + c_t.credit)
            act.sem_inc(f_act, 1)

            def normal_again(b):
                act.wait_ge(l_st.sem, l_st.at(b, 1))
                act.wait_ge(l_x.sem, l_x.at(b, 1))
                act.wait_ge(s_v.sem, s_v.at(b, 0))
                for j in range(NT):
                    s_.activation(XNB[:, j], X1[:, j], ACT.Identity, scale=stb[:, 0, j:j + 1],
                                  bias=stb[:, 1, j:j + 1]).then_inc(x_n.sem, 1)

            def hidden(b):
                act.wait_ge(p_hq.sem, p_hq.at(b, 1))
                s_.activation(WX[:, :, :], WX[:, :, :], ACT.Tanh).then_inc(g_t.sem, 1)
                act.wait_ge(g_t.sem, g_t.at(b, 1))
                act.wait_ge(s_p.sem, s_p.at(b, 0))
                act.wait_ge(n_x2.sem, n_x2.at(b, 0))
                s_.activation(SG[:, :, :], WX[:, :, :], ACT.Tanh, scale=0.5).then_inc(g_t.sem, 1)
                act.wait_ge(g_t.sem, g_t.at(b, 2))
                s_.activation(SG[:, :, :], SG[:, :, :], ACT.Identity, scale=0.5, bias=half1[:, 0:1]
                              ).then_inc(g_t.sem, 1)

            def take_mixed(b):
                act.wait_ge(v_c.sem, v_c.at(b, 0))
                for m in range(KT):
                    act.wait_ge(y_mm.sem, y_mm.at(b, m + 1))
                    s_.copy(YS[:, m], PS[:, 6 + m, :]).then_inc(y_v.sem, 1)

            def take_left(b):
                for n in range(2):
                    act.wait_ge(s_mm.sem, s_mm.at(b, n + 1))
                    s_.copy(S1[:, 2 * n:2 * n + 2], PS[:, 6 + n, :].rearrange("p (j d) -> p j d", d=D)
                            ).then_inc(s_v.sem, 1)

            def open_gate(b):
                act.wait_ge(l_gt.sem, l_gt.at(b, 1))
                s_.activation(GT[:, :, :], GT[:, :, :], ACT.Identity, scale=0.5, bias=half1[:, 0:1]
                              ).then_inc(g_h.sem, 1)

            def normalise(b):
                act.wait_ge(n_mr.sem, n_mr.at(b, 2))
                for j in range(NT):
                    s_.activation(S1[:, j], X1[:, j], ACT.Identity, scale=rst[:, j:j + 1],
                                  bias=mrs[:, j:j + 1]).then_inc(n_xn.sem, 1)

            def take_weights(b):
                act.wait_ge(w_t.sem, w_t.at(b, 1))
                s_.copy(wmt[:, :], PS[0:NP, 6, :]).then_inc(w_e.sem, 1)

            def maxima_high(b, a):
                act.wait_ge(m_t.sem, m_t.at(b, a + 1))
                s_.copy(nmh[:, a], PS[0:H // 2, 7 - 2 * a, :]).then_inc(m_a.sem, 1)

            def take_normal(b):
                for k in range(KT):
                    act.wait_ge(n_tr.sem, n_tr.at(b, k + 1))
                    s_.copy(XT1[:, k], PS[:, 6 + k, :]).then_inc(n_xt.sem, 1)

            def square(b):
                act.wait_ge(n_xn.sem, n_xn.at(b, NT))
                for j in range(NT):
                    s_.activation(SG[:, j], S1[:, j], ACT.Square, accum_out=x2[:, j:j + 1]
                                  ).then_inc(n_x2.sem, 1)

            def take_query_key(b, n):
                if n == 0:
                    act.wait_ge(z_mm.sem, z_mm.at(b, -2))
                act.wait_ge(q_mm.sem, q_mm.at(b, n + 1))
                s_.copy(QF[:, n], PS[:, 6 + n % 2, :]).then_inc(q_e.sem, 1)

            def second_odds(b):
                act.wait_ge(d_v.sem, d_v.at(b, 8))
                s_.activation(odds[:, :], odds[:, :], ACT.Exp, scale=ntemp[:, 0:1]).then_inc(d_e.sem, 1)

            def take_low_rank(b, j):
                act.wait_ge(h_t.sem, h_t.at(b, j + 1))
                s_.copy(HMT[:, :, j * P:(j + 1) * P],
                        PS[:, 7, :].rearrange("p (n q) -> p n q", q=P)).then_inc(h_e.sem, 1)

            def expert_gate(b, p):
                if p == 0:
                    act.wait_ge(z_o.sem, z_o.at(b, 0))
                act.wait_ge(e_mm.sem, e_mm.at(b, p + 1))
                s_.activation(SG2[:, 2 * p:2 * p + 2], PS[:, 7 - p, :].rearrange("p (j d) -> p j d", d=D),
                              ACT.Tanh, scale=0.5).then_inc(e_t.sem, 1)

            def exp(b, h):
                if h % 4 == 0:
                    act.wait_ge(o_mm.sem, o_mm.at(b, h // 4 - 1 if h >= 8 else 0))
                unit = 3 * (h // 2) + h % 2
                act.wait_ge(t_mm.sem, t_mm.at(b, unit + 1))
                if h % 2:
                    s_.activation(PR[:, h // 4 % 2, h % 4 - 1:h % 4 + 1, PU:PW],
                                  PS[:, 2, :].rearrange("p (a b) -> p a b", a=2),
                                  ACT.Exp, scale=SCORE_SCALE).then_inc(t_e.sem, 1)
                    act.wait_ge(t_mm.sem, t_mm.at(b, unit + 2))
                base = 3 * (h % 2)
                s_.activation(PR[:, h // 4 % 2, h % 4, 0:PU],
                              PS[:, base:base + 2, :].rearrange("p a b -> p (a b)"),
                              ACT.Exp, scale=SCORE_SCALE).then_inc(t_e.sem, 1)

            def take_values(b, g):
                act.wait_ge(o_mm.sem, o_mm.at(b, g + 1))
                act.wait_ge(o_t.sem, o_t.at(b, g))
                s_.copy(OS[:, :], PS[:, 5, :]).then_inc(o_e.sem, 1)

            def take_heads(b):
                for k in range(KT):
                    act.wait_ge(r_t.sem, r_t.at(b, k + 1))
                    s_.copy(AO[:, k], PS[:, k, :]).then_inc(r_e.sem, 1)

            def run(steps, n):
                for step in steps.get(n, ()):
                    step()

            def batch(b, more):
                take_low_rank(b, 3)
                take_weights(b)
                if more:
                    take_mixed(b + 1)
                    open_gate(b + 1)
                    hidden(b + 1)
                    normal_again(b + 1)
                expert_gate(b, 0)
                expert_gate(b, 1)
                maxima_high(b, 0)
                if more:
                    take_left(b + 1)
                maxima_high(b, 1)
                side = {4: [lambda: take_values(b, 0)], 8: [lambda: take_values(b, 1)], 12: [lambda: take_values(b, 2)]}
                if more:
                    side.setdefault(3, []).extend([lambda: normalise(b + 1)])
                    side.setdefault(4, []).extend([lambda: take_normal(b + 1)])
                    side.setdefault(5, []).extend([lambda: take_query_key(b + 1, 0), lambda: take_query_key(b + 1, 1)])
                    side.setdefault(6, []).extend([lambda: take_query_key(b + 1, 2), lambda: take_query_key(b + 1, 3)])
                    side.setdefault(8, []).extend([lambda: square(b + 1)])
                    side.setdefault(12, []).extend([lambda: second_odds(b + 1)])
                for h in range(H):
                    exp(b, h)
                    run(side, h)
                take_values(b, 3)
                if more:
                    take_low_rank(b + 1, 0)
                    take_low_rank(b + 1, 1)
                take_heads(b)
                if more:
                    take_low_rank(b + 1, 2)
                act.wait_ge(z_v.sem, z_v.at(b, 4))
                act.dma_start(o_view[bass.ds(b, 1)].rearrange("o p j d -> p (o j) d"), SG2[:, :, :]
                              ).then_inc(z_o.sem, 16)

            act.wait_ge(init, 7)
            take_mixed(0)
            open_gate(0)
            normal_again(0)
            hidden(0)
            take_left(0)
            normalise(0)
            take_normal(0)
            square(0)
            for n in range(4):
                take_query_key(0, n)
            second_odds(0)
            for j in range(NT - 1):
                take_low_rank(0, j)
            with act.Fori(0, B - 1) as b:
                batch(b, True)
            batch(B - 1, False)

        @block.vector
        def _(dve):
            v_ = nc.vector
            for s in (a_st, a_xn, c_w, c_c, n_st, q_s, q_d, v_e, d_v, d_m, m_r, m_h, h_v,
                      e_v, o_r, o_v, z_v):
                dve.sem_inc(s.sem, s.credit)

            def hold():
                v_.memset(scratch[:, :], 0.0)

            v_.memset(HB[0:ST, 0], 0.0).then_inc(init, 1)

            def aggregate(st, b, base, parts, to):
                dve.wait_ge(st.sem, st.at(b, base + NT))
                hold()
                for j in range(NT):
                    v_.bn_aggr(to[:, j], parts[:, j]).then_inc(st.sem, 1)

            with dve.Fori(0, B // 2) as g:
                for s in range(2):
                    dve.wait_ge(a_x[s].sem, a_x[s].at(g, 1))
                    dve.wait_ge(a_mr.sem, a_mr.at(g, 0))
                    for j in range(NT):
                        v_.bn_stats(abn[:, s, j], xin[s][:, j]).then_inc(a_st.sem, 1)
                    aggregate(a_st, g, 2 * NT * s, abn[:, s], amv[:, s])
                for s in range(2):
                    dve.wait_ge(a_rs.sem, a_rs.at(g, 2 * (s + 1)))
                    dve.wait_ge(a_tr.sem, a_tr.at(g, 0))
                    for j in range(NT):
                        mm = v_.tensor_scalar(xnp[s][:, j], xin[s][:, j], amv[:, s, j, 0:1],
                                              sst[:, s, 0, j:j + 1], ALU.subtract, ALU.mult)
                    mm.then_inc(a_xn.sem, 1)

            dve.wait_ge(ld_w, 16 * len(loads))
            v_.tensor_copy(CT, c0.unsqueeze(2).to_broadcast([P, KT, T])).then_inc(init, 1)
            dve.wait_ge(a_tr.sem, 2 * KT * (B // 2) + 1)
            v_.tensor_tensor(ptsq, w_pt[:, :, :], w_pt[:, :, :], ALU.mult).then_inc(init, 1)
            v_.scalar_tensor_tensor(out=atemp[:, :], in0=ntemp[:, :], scalar=-1.0, in1=ntemp[:, :],
                                    op0=ALU.mult, op1=ALU.max).then_inc(temps, 1)
            dve.wait_ge(temps, 1)
            v_.tensor_scalar(ntemp[:, :], atemp[:, :], 0.1, None, ALU.max).then_inc(init, 1)
            dve.wait_ge(init, 4)
            v_.reciprocal(ntemp[:, :], ntemp[:, :]).then_inc(init, 1)
            dve.wait_ge(init, 5)
            v_.tensor_scalar(ntemp[:, :], ntemp[:, :], -1.0, None, ALU.mult).then_inc(init, 1)
            v_.memset(K6[KS:P, :, :], 1.0).then_inc(init, 1)

            def half(b, n):
                c = CT[:, :, n * HALF:(n + 1) * HALF]
                dve.wait_ge(c_t.sem, c_t.at(b, 8 * n + 6))
                v_.scalar_tensor_tensor(out=c, in0=TG[:, 0], scalar=1.0, in1=c, op0=ALU.add, op1=ALU.mult
                                        ).then_inc(c_c.sem, 1)
                v_.scalar_tensor_tensor(out=CA, in0=TG[:, 1], scalar=1.0, in1=TG[:, 2], op0=ALU.add,
                                        op1=ALU.mult).then_inc(c_c.sem, 1)
                dve.wait_ge(c_c.sem, c_c.at(b, 4 * n + 2))
                v_.tensor_tensor(c, c, CA, ALU.add).then_inc(c_c.sem, 1)
                dve.wait_ge(c_c.sem, c_c.at(b, 4 * n + 3))
                v_.tensor_scalar(c, c, 0.5, None, ALU.mult).then_inc(c_c.sem, 1)
                dve.wait_ge(c_z.sem, c_z.at(b, 5 * n + 5))
                dve.wait_ge(c_ws.sem, c_ws.at(b, n))
                v_.tensor_copy(WS, PS[:, 4, :].rearrange("p (j d) -> p j d", d=D)).then_inc(c_w.sem, 1)

            with dve.Fori(0, B) as b:
                half(b, 0)
                half(b, 1)

            dve.wait_ge(f_pe, 1)
            v_.tensor_copy(p2[:, :], PS[:, 5, 0:NP]).then_inc(f_p2, 1)
            for n in range(2):
                v_.tensor_tensor(UC[:, 2 * n:2 * n + 2], PS[:, n, :].rearrange("p (j d) -> p j d", d=D),
                                 bo[:, :].unsqueeze(1).to_broadcast([P, 2, D]), ALU.add).then_inc(f_e, 1)

            def gather_statistics(b):
                dve.wait_ge(s_p.sem, s_p.at(b, 3))
                hold()
                for j in range(NT):
                    v_.bn_stats(bnst[:, j], X1[:, j]).then_inc(n_st.sem, 1)
                aggregate(n_st, b, 0, bnst, mv)

            Q, K = slice(0, KT), slice(KT, 2 * KT)

            def split(b, n, c):
                if n == 0:
                    dve.wait_ge(q_e.sem, q_e.at(b, 2 if c == Q else 4))
                    dve.wait_ge(q_st.sem, q_st.at(b, 0))
                elif c == Q:
                    dve.wait_ge(q_d.sem, q_d.at(b, n))
                else:
                    dve.wait_ge(q_r.sem, q_r.at(b, n))
                v_.tensor_copy(QB[:, n, c], QF[:, c]).then_inc(q_s.sem, 1)

            def remainder(b, n):
                dve.wait_ge(q_s.sem, q_s.at(b, 1 if n == 0 else 3))
                v_.tensor_tensor(QF[:, Q], QF[:, Q], QB[:, n, Q], ALU.subtract).then_inc(q_d.sem, 1)

            def value(b, p):
                dve.wait_ge(v_mm.sem, v_mm.at(b, p + 1))
                v_.tensor_copy(V1[:, 2 * p:2 * p + 2], PS[:, 6 + p, :].rearrange("p (j d) -> p j d", d=D)
                               ).then_inc(v_e.sem, 1)

            def distance(b):
                dve.wait_ge(d_mm.sem, d_mm.at(b, 1))
                v_.scalar_tensor_tensor(out=dst[:, :, :],
                                        in0=PS[:, 6, 0:NT * NP].rearrange("p (j n) -> p j n", n=NP),
                                        scalar=2.0, in1=p2[:, :].unsqueeze(1).to_broadcast([P, NT, NP]),
                                        op0=ALU.mult, op1=ALU.subtract).then_inc(d_v.sem, 1)
                dve.wait_ge(d_v.sem, d_v.at(b, 1))
                dve.wait_ge(n_x2.sem, n_x2.at(b, NT))
                v_.tensor_tensor(dst[:, :, :], dst[:, :, :],
                                 x2[:, :].unsqueeze(2).to_broadcast([P, NT, NP]), ALU.subtract
                                 ).then_inc(d_v.sem, 1)
                dve.wait_ge(d_v.sem, d_v.at(b, 2))
                v_.tensor_scalar(dst[:, :, :], dst[:, :, :], 0.0, None, ALU.min).then_inc(d_v.sem, 1)
                dve.wait_ge(d_v.sem, d_v.at(b, 3))
                hold()
                for j in range(NT):
                    v_.max(top[:, j], dst[:, j]).then_inc(d_m.sem, 1)
                dve.wait_ge(d_m.sem, d_m.at(b, NT))
                hold()
                for j in range(NT):
                    v_.max_index(topi[:, j], top[:, j], dst[:, j]).then_inc(d_m.sem, 1)
                dve.wait_ge(d_m.sem, d_m.at(b, 2 * NT))
                v_.tensor_copy(topf[:, :, :], topi[:, :, 0:2]).then_inc(d_v.sem, 1)
                v_.tensor_scalar(near[:, :, :], top[:, :, 0:2], -1.0, None, ALU.mult).then_inc(d_v.sem, 1)
                dve.wait_ge(d_v.sem, d_v.at(b, 5))
                for n, chosen in enumerate((hit, wm)):
                    v_.tensor_tensor(chosen[:, :, :], iota[:, :].unsqueeze(1).to_broadcast([P, NT, NP]),
                                     topf[:, :, n:n + 1].to_broadcast([P, NT, NP]), ALU.is_equal
                                     ).then_inc(d_v.sem, 1)

            def odds_apart(b):
                dve.wait_ge(d_p.sem, d_p.at(b, 1))
                v_.tensor_tensor(odds[:, :], near[:, :, 1], near[:, :, 0], ALU.subtract).then_inc(d_v.sem, 1)

            def choose(b):
                dve.wait_ge(d_e.sem, d_e.at(b, 1))
                v_.tensor_scalar(rden[:, :], odds[:, :], 1.0, None, ALU.add).then_inc(d_v.sem, 1)
                dve.wait_ge(d_v.sem, d_v.at(b, 9))
                v_.reciprocal(rden[:, :], rden[:, :]).then_inc(d_v.sem, 1)
                dve.wait_ge(d_v.sem, d_v.at(b, 10))
                v_.tensor_tensor(odds[:, :], odds[:, :], rden[:, :], ALU.mult).then_inc(d_v.sem, 1)
                dve.wait_ge(d_v.sem, d_v.at(b, 11))
                for weight, chosen in ((rden, hit), (odds, wm)):
                    v_.tensor_tensor(chosen[:, :, :], chosen[:, :, :],
                                     weight[:, :].unsqueeze(2).to_broadcast([P, NT, NP]), ALU.mult
                                     ).then_inc(d_v.sem, 1)
                dve.wait_ge(d_v.sem, d_v.at(b, 13))
                v_.tensor_tensor(wm[:, :, :], wm[:, :, :], hit[:, :, :], ALU.add).then_inc(d_v.sem, 1)

            def weigh(b, j):
                dve.wait_ge(h_mm.sem, h_mm.at(b, j + 1))
                dve.wait_ge(d_v.sem, d_v.at(b, 14))
                dve.wait_ge(h_t.sem, h_t.at(b, j))
                v_.tensor_tensor(HM.rearrange("p (n r) -> p n r", r=RANK),
                                 PS[:, 6, :].rearrange("p (n r) -> p n r", r=RANK),
                                 wm[:, j].unsqueeze(2).to_broadcast([P, NP, RANK]), ALU.mult
                                 ).then_inc(h_v.sem, 1)

            def gate(b, p):
                dve.wait_ge(e_t.sem, e_t.at(b, p + 1))
                v_.scalar_tensor_tensor(out=SG2[:, 2 * p:2 * p + 2], in0=SG2[:, 2 * p:2 * p + 2],
                                        scalar=1.0, in1=PS[:, 7 - p, :].rearrange("p (j d) -> p j d", d=D),
                                        op0=ALU.add, op1=ALU.mult).then_inc(e_v.sem, 1)

            def maxima(b, u):
                hp, i = u // NT, u % NT
                dve.wait_ge(m_mm.sem, m_mm.at(b, u + 1))
                v_.tensor_reduce(nm[:, i, 2 * hp:2 * hp + 2],
                                 PS[:, 2 * (u % 3):2 * (u % 3) + 2, 0:(i + 1) * P], AX.X, ALU.max,
                                 negate=True).then_inc(m_r.sem, 1)

            def maxima_low(b, a):
                dve.wait_ge(m_a.sem, m_a.at(b, a + 1))
                v_.tensor_tensor(nml[:, a], PS[0:H // 2, 7 - 2 * a, :], nmh[:, a], ALU.subtract
                                 ).then_inc(m_h.sem, 1)

            def divide(b, g):
                dve.wait_ge(o_t.sem, o_t.at(b, g + 1))
                o = PS[:, 5, :].rearrange("p (j n d) -> p j n d", n=4, d=32)
                v_.reciprocal(rec[:, :, :], o[:, :, :, HD]).then_inc(o_r.sem, 1)
                dve.wait_ge(o_r.sem, o_r.at(b, g + 1))
                v_.tensor_tensor(AT[:, :, g * 64:(g + 1) * 64].rearrange("p j (n d) -> p j n d", d=HD),
                                 o[:, :, :, 0:HD], rec[:, :, :].unsqueeze(3).to_broadcast([P, NT, 4, HD]),
                                 ALU.mult).then_inc(o_v.sem, 1)

            def finish(b):
                for p in range(2):
                    dve.wait_ge(z_mm.sem, z_mm.at(b, p + 1))
                    v_.tensor_tensor(SG2[:, 2 * p:2 * p + 2], PS[:, 2 + p, :].rearrange("p (j d) -> p j d", d=D),
                                     SG2[:, 2 * p:2 * p + 2], ALU.mult).then_inc(z_v.sem, 1)
                dve.wait_ge(x_ld.sem, x_ld.at(b, 1))
                dve.wait_ge(z_v.sem, z_v.at(b, 2))
                for p in range(2):
                    v_.scalar_tensor_tensor(out=SG2[:, 2 * p:2 * p + 2], in0=SG2[:, 2 * p:2 * p + 2],
                                            scalar=0.5 * OUT_SCALE, in1=S1[:, 2 * p:2 * p + 2],
                                            op0=ALU.mult, op1=ALU.add).then_inc(z_v.sem, 1)

            def batch(b, more):
                side = {0: [lambda: weigh(b, 3)], 11: [lambda: gate(b, 0)], 17: [lambda: gate(b, 1)],
                        21: [lambda: maxima_low(b, 0)]}
                for u in range(NT * H // 2):
                    maxima(b, u)
                    for step in side.get(u, ()):
                        step()
                if more:
                    gather_statistics(b + 1)
                maxima_low(b, 1)
                if more:
                    split(b + 1, 0, Q)
                    remainder(b + 1, 0)
                    split(b + 1, 0, K)
                divide(b, 0)
                if more:
                    split(b + 1, 1, Q)
                    remainder(b + 1, 1)
                    value(b + 1, 0)
                    split(b + 1, 2, Q)
                    value(b + 1, 1)
                    split(b + 1, 1, K)
                    distance(b + 1)
                    split(b + 1, 2, K)
                divide(b, 1)
                if more:
                    odds_apart(b + 1)
                    choose(b + 1)
                divide(b, 2)
                if more:
                    weigh(b + 1, 0)
                    weigh(b + 1, 1)
                divide(b, 3)
                if more:
                    weigh(b + 1, 2)
                finish(b)

            dve.wait_ge(f_p2, 1)
            gather_statistics(0)
            split(0, 0, Q)
            remainder(0, 0)
            split(0, 0, K)
            split(0, 1, Q)
            remainder(0, 1)
            split(0, 2, Q)
            value(0, 0)
            value(0, 1)
            split(0, 1, K)
            distance(0)
            split(0, 2, K)
            odds_apart(0)
            choose(0)
            for j in range(NT - 1):
                weigh(0, j)
            with dve.Fori(0, B - 1) as b:
                batch(b, True)
            batch(B - 1, False)


_SHAPE = ((B, T, D), "float32")


def _layout(inputs):
    import numpy as np

    def c(x):
        return np.ascontiguousarray(x)

    i = {k: np.asarray(v) for k, v in inputs.items()}
    f, s = "L0_ffn_", "L0_attn_"
    w = {"L0_attn_x": c(i["L0_attn_x"]), "W_in": c(i[s + "W_in"]), "W_gate": c(i[s + "W_gate"]),
         "A": c(i[s + "A"]), "Bm": c(i[s + "Bm"]), "CT": c(i[s + "C"].T), "DT": c(i[s + "D"].T),
         "W_out": c(i[s + "W_out"]), "b_in": c(i[s + "b_in"]), "b_gate": c(i[s + "b_gate"]),
         "b_out": c(i[s + "b_out"])}
    for n in ("wf", "uf", "wi", "ui", "wc", "uc", "wo", "uo"):
        w[n + "T"] = c(i[f + n].T)
    w["bo"] = c(i[f + "bo"])
    w["b_gate"] = c(w["b_gate"].reshape(KT, P).T)
    for n in ("bf", "bi", "bc", "in_c"):
        w[n] = c(i[f + n].reshape(KT, P).T)
    for n, m in (("WqT", "W_query"), ("WkT", "W_key"), ("WvT", "W_value"), ("WpT", "W_proj")):
        w[n] = c(i["L1_attn_" + m].T)
    w["BT"] = c(i["L1_ffn_B"].reshape(NR, D).T)
    w["AT"] = c(i["L1_ffn_A"].transpose(0, 2, 1).reshape(NR, D))
    w["protoT"] = c(i["L1_ffn_prototypes"].T)
    w["bias"] = c(i["L1_ffn_bias"])
    w["temp"] = c(i["L1_ffn_temp"].reshape(1))
    return w


def kernel(**inputs):
    import concourse.bacc as bacc
    from concourse.bass_utils import run_bass_kernel_spmd

    nc = bacc.Bacc("TRN2", target_bir_lowering=False, num_devices=1)
    arrays = {}
    aps = {}
    for name, x in _layout(inputs).items():
        arrays[f"in_{name}"] = x
        aps[name] = nc.dram_tensor(f"in_{name}", x.shape, mybir.dt.from_np(x.dtype), kind="ExternalInput").ap()
    out = nc.dram_tensor("out_0", _SHAPE[0], F32, kind="ExternalOutput").ap()
    two_layers(nc, aps, out)
    r = run_bass_kernel_spmd(nc, [arrays], core_ids=[0])
    return r.results[0]["out_0"]
```
